# Optimizing a Trainium2 kernel written in Bass

```python
import numpy as np
import jax
import jax.numpy as jnp

def _softmax(x, axis=-1):
    return jax.nn.softmax(x, axis=axis)

def _gelu(x):
    return jax.nn.gelu(x, approximate=True)

def _silu(x):
    return jax.nn.silu(x)

def _sigmoid(x):
    return jax.nn.sigmoid(x)

def _layernorm(x, axis=-1, eps=1e-05):
    m = jnp.mean(x, axis=axis, keepdims=True)
    v = jnp.var(x, axis=axis, keepdims=True)
    return (x - m) / jnp.sqrt(v + eps)

def _scatter_add(tgt, idx, src, axis=0):
    return tgt.at[idx].add(src)

def _segment_sum(src, seg, n):
    return jax.ops.segment_sum(src, seg, n)
kernel_name = 'mk_adaln_d2_jaxref_r8_abd6d9'

def setup_inputs(seed: int=0):
    np.random.seed(seed)
    _w = jnp.asarray

    def _L0_attn_setup():
        import jax, jax.numpy as jnp
        import numpy as np
        B, T, D_MODEL = (2, 256, 256)
        N_HEADS, N_KV_HEADS, HEAD_DIM = (16, 4, 128)
        N_REP = N_HEADS // N_KV_HEADS
        EPS = 1e-06

        def _qknorm(t, scale):
            norm = jax.lax.rsqrt(jnp.mean(t * t, axis=-1, keepdims=True) + EPS)
            return t * norm * scale
        key = jax.random.key(seed)
        ks = jax.random.split(key, 5)
        return {'x': jax.random.normal(ks[0], (B, T, D_MODEL), dtype=jnp.float32), 'Wq': jax.random.normal(ks[1], (N_HEADS * HEAD_DIM, D_MODEL), dtype=jnp.float32) * 0.02, 'Wk': jax.random.normal(ks[2], (N_KV_HEADS * HEAD_DIM, D_MODEL), dtype=jnp.float32) * 0.02, 'Wv': jax.random.normal(ks[3], (N_KV_HEADS * HEAD_DIM, D_MODEL), dtype=jnp.float32) * 0.02, 'Wo': jax.random.normal(ks[4], (D_MODEL, N_HEADS * HEAD_DIM), dtype=jnp.float32) * 0.02, 'q_scale': jnp.ones((HEAD_DIM,), dtype=jnp.float32), 'k_scale': jnp.ones((HEAD_DIM,), dtype=jnp.float32)}
    _L0_attn_in = _L0_attn_setup()

    def _L0_ffn_setup():
        import jax, jax.numpy as jnp
        import numpy as np
        TOPK = 6
        CAP = 128
        ROUTE_SCALE = 1.0
        key = jax.random.key(seed)
        k = jax.random.split(key, 6)
        B, T, C = (2, 256, 256)
        E, H, HS = (64, 32, 64)
        std = 0.01
        return {'x': jax.random.normal(k[0], (B, T, C), jnp.float32), 'w_gate': jax.random.normal(k[1], (C, E), jnp.float32) * std, 'w_shared_up': jax.random.normal(k[2], (C, 2 * HS), jnp.float32) * std, 'w_shared_down': jax.random.normal(k[3], (HS, C), jnp.float32) * std, 'w_up': jax.random.normal(k[4], (E, C, 2 * H), jnp.float32) * std, 'w_down': jax.random.normal(k[5], (E, H, C), jnp.float32) * std}
    _L0_ffn_in = _L0_ffn_setup()
    _L0_c = _w((lambda *s: np.random.randn(*s).astype(np.float32) * 0.05)(1, 256))
    _L0_wmod = _w((lambda *s: np.random.randn(*s).astype(np.float32) * 0.05)(256, 6 * 256) * 256 ** (-0.5))

    def _L1_attn_setup():
        import jax, jax.numpy as jnp
        import numpy as np
        D_MODEL = 256
        D_STATE = 128
        LN_EPS = 1e-05

        def _layernorm(x, w, b):
            mu = jnp.mean(x, axis=-1, keepdims=True)
            var = jnp.mean(jnp.square(x - mu), axis=-1, keepdims=True)
            return (x - mu) * jax.lax.rsqrt(var + LN_EPS) * w + b
        key = jax.random.key(seed)
        k_x, k_a, k_b, k_c = jax.random.split(key, 4)
        x = jax.random.normal(k_x, (8, 256, D_MODEL), dtype=jnp.float32)
        log_A_diag = jax.random.normal(k_a, (D_STATE,), dtype=jnp.float32) * 0.5 - 1.0
        B_mat = jax.random.normal(k_b, (D_STATE, D_MODEL), dtype=jnp.float32) * 0.01
        C_mat = jax.random.normal(k_c, (D_MODEL, D_STATE), dtype=jnp.float32) * 0.01
        D_vec = jnp.ones((D_MODEL,), dtype=jnp.float32) * 0.1
        ln_w = jnp.ones((D_MODEL,), dtype=jnp.float32)
        ln_b = jnp.zeros((D_MODEL,), dtype=jnp.float32)
        return {'x': x, 'log_A_diag': log_A_diag, 'B_mat': B_mat, 'C_mat': C_mat, 'D_vec': D_vec, 'ln_w': ln_w, 'ln_b': ln_b}
    _L1_attn_in = _L1_attn_setup()

    def _L1_ffn_setup():
        import jax, jax.numpy as jnp
        import numpy as np
        B, S, H, I, E, K = (4, 256, 256, 512, 8, 2)
        key = jax.random.key(seed)
        k1, k2, k3, k4 = jax.random.split(key, 4)
        return {'hidden_states': jax.random.normal(k1, (B, S, H), dtype=jnp.float32), 'gate_weight': jax.random.normal(k2, (E, H), dtype=jnp.float32) * 0.02, 'gate_up_proj': jax.random.normal(k3, (E, 2 * I, H), dtype=jnp.float32) * 0.02, 'down_proj': jax.random.normal(k4, (E, H, I), dtype=jnp.float32) * 0.02}
    _L1_ffn_in = _L1_ffn_setup()
    _L1_c = _w((lambda *s: np.random.randn(*s).astype(np.float32) * 0.05)(1, 256))
    _L1_wmod = _w((lambda *s: np.random.randn(*s).astype(np.float32) * 0.05)(256, 6 * 256) * 256 ** (-0.5))
    _d = {'L0_attn_x': _L0_attn_in['x'], 'L0_attn_Wq': _L0_attn_in['Wq'], 'L0_attn_Wk': _L0_attn_in['Wk'], 'L0_attn_Wv': _L0_attn_in['Wv'], 'L0_attn_Wo': _L0_attn_in['Wo'], 'L0_attn_q_scale': _L0_attn_in['q_scale'], 'L0_attn_k_scale': _L0_attn_in['k_scale'], 'L0_ffn_w_gate': _L0_ffn_in['w_gate'], 'L0_ffn_w_shared_up': _L0_ffn_in['w_shared_up'], 'L0_ffn_w_shared_down': _L0_ffn_in['w_shared_down'], 'L0_ffn_w_up': _L0_ffn_in['w_up'], 'L0_ffn_w_down': _L0_ffn_in['w_down'], 'L0_c': _L0_c, 'L0_wmod': _L0_wmod, 'L1_attn_log_A_diag': _L1_attn_in['log_A_diag'], 'L1_attn_B_mat': _L1_attn_in['B_mat'], 'L1_attn_C_mat': _L1_attn_in['C_mat'], 'L1_attn_D_vec': _L1_attn_in['D_vec'], 'L1_attn_ln_w': _L1_attn_in['ln_w'], 'L1_attn_ln_b': _L1_attn_in['ln_b'], 'L1_ffn_gate_weight': _L1_ffn_in['gate_weight'], 'L1_ffn_gate_up_proj': _L1_ffn_in['gate_up_proj'], 'L1_ffn_down_proj': _L1_ffn_in['down_proj'], 'L1_c': _L1_c, 'L1_wmod': _L1_wmod}
    _x0 = _d['L0_attn_x']
    _d['L0_attn_x'] = jax.random.normal(jax.random.fold_in(jax.random.key(seed), 1), (1, 1024, 256), dtype=_x0.dtype)
    del _x0
    return _d

def reference(L0_attn_x, L0_attn_Wq, L0_attn_Wk, L0_attn_Wv, L0_attn_Wo, L0_attn_q_scale, L0_attn_k_scale, L0_ffn_w_gate, L0_ffn_w_shared_up, L0_ffn_w_shared_down, L0_ffn_w_up, L0_ffn_w_down, L0_c, L0_wmod, L1_attn_log_A_diag, L1_attn_B_mat, L1_attn_C_mat, L1_attn_D_vec, L1_attn_ln_w, L1_attn_ln_b, L1_ffn_gate_weight, L1_ffn_gate_up_proj, L1_ffn_down_proj, L1_c, L1_wmod):

    def _L0_attn_ref(x, Wq, Wk, Wv, Wo, q_scale, k_scale):
        import jax, jax.numpy as jnp
        import numpy as np
        B, T, D_MODEL = (2, 256, 256)
        N_HEADS, N_KV_HEADS, HEAD_DIM = (16, 4, 128)
        N_REP = N_HEADS // N_KV_HEADS
        EPS = 1e-06

        def _qknorm(t, scale):
            norm = jax.lax.rsqrt(jnp.mean(t * t, axis=-1, keepdims=True) + EPS)
            return t * norm * scale
        b, t, _ = x.shape
        q = (x @ Wq.T).reshape(b, t, N_HEADS, HEAD_DIM).transpose(0, 2, 1, 3)
        k = (x @ Wk.T).reshape(b, t, N_KV_HEADS, HEAD_DIM).transpose(0, 2, 1, 3)
        v = (x @ Wv.T).reshape(b, t, N_KV_HEADS, HEAD_DIM).transpose(0, 2, 1, 3)
        q = _qknorm(q, q_scale)
        k = _qknorm(k, k_scale)
        k = jnp.repeat(k, N_REP, axis=1)
        v = jnp.repeat(v, N_REP, axis=1)
        scale = 1.0 / np.sqrt(HEAD_DIM).astype(np.float32)
        scores = jnp.einsum('bhtd,bhsd->bhts', q, k) * scale
        causal = jnp.tril(jnp.ones((t, t), dtype=bool))
        scores = jnp.where(causal, scores, jnp.finfo(scores.dtype).min)
        attn = jax.nn.softmax(scores, axis=-1)
        out = jnp.einsum('bhts,bhsd->bhtd', attn, v)
        out = out.transpose(0, 2, 1, 3).reshape(b, t, N_HEADS * HEAD_DIM)
        return out @ Wo.T

    def _L0_ffn_ref(x, w_gate, w_shared_up, w_shared_down, w_up, w_down):
        import jax, jax.numpy as jnp
        import numpy as np
        TOPK = 6
        CAP = 128
        ROUTE_SCALE = 1.0
        B, T, C = x.shape
        E = w_gate.shape[1]
        x_flat = x.reshape(-1, C)
        N = x_flat.shape[0]
        su = x_flat @ w_shared_up
        y_s, g_s = jnp.split(su, 2, axis=-1)
        shared = jax.nn.silu(g_s) * y_s @ w_shared_down
        scores = jax.nn.sigmoid(x_flat @ w_gate)
        _, topk_idx = jax.lax.top_k(scores, TOPK)
        w = jnp.take_along_axis(scores, topk_idx, axis=-1)
        w = w / w.sum(-1, keepdims=True) * ROUTE_SCALE
        flat_e = topk_idx.reshape(-1)
        oh = jax.nn.one_hot(flat_e, E, dtype=jnp.int32)
        pos = jnp.take_along_axis(jnp.cumsum(oh, axis=0), flat_e[:, None], axis=1)[:, 0] - 1
        valid = pos < CAP
        pos_c = jnp.where(valid, pos, CAP - 1)
        token_ids = jnp.repeat(jnp.arange(N), TOPK)
        x_disp = jnp.zeros((E, CAP, C), x.dtype).at[flat_e, pos].set(x_flat[token_ids], mode='drop')
        up = jnp.einsum('ecd,edh->ech', x_disp, w_up)
        g_r, v_r = jnp.split(up, 2, axis=-1)
        h_r = jax.nn.silu(g_r) * v_r
        out_r = jnp.einsum('ech,ehd->ecd', h_r, w_down)
        y_ts = out_r[flat_e, pos_c]
        y_ts = jnp.where(valid[:, None], y_ts, 0.0)
        routed = (y_ts.reshape(N, TOPK, C) * w[:, :, None]).sum(axis=1)
        return (shared + routed).reshape(B, T, C)

    def _L1_attn_ref(x, log_A_diag, B_mat, C_mat, D_vec, ln_w, ln_b):
        import jax, jax.numpy as jnp
        import numpy as np
        D_MODEL = 256
        D_STATE = 128
        LN_EPS = 1e-05

        def _layernorm(x, w, b):
            mu = jnp.mean(x, axis=-1, keepdims=True)
            var = jnp.mean(jnp.square(x - mu), axis=-1, keepdims=True)
            return (x - mu) * jax.lax.rsqrt(var + LN_EPS) * w + b
        Bsz, T, D = x.shape
        A_disc = jnp.exp(-jnp.exp(log_A_diag))
        u = jnp.einsum('btd,nd->btn', x, B_mat)

        def step(h, u_t):
            h = h * A_disc + u_t
            return (h, h)
        h0 = jnp.zeros((Bsz, D_STATE), dtype=x.dtype)
        _, hs = jax.lax.scan(step, h0, jnp.transpose(u, (1, 0, 2)))
        hs = jnp.transpose(hs, (1, 0, 2))
        y = jnp.einsum('btn,dn->btd', hs, C_mat) + x * D_vec
        return _layernorm(x + y, ln_w, ln_b)

    def _L1_ffn_ref(hidden_states, gate_weight, gate_up_proj, down_proj):
        import jax, jax.numpy as jnp
        import numpy as np
        B, S, H, I, E, K = (4, 256, 256, 512, 8, 2)
        b, s, h = hidden_states.shape
        num_experts, top_k = (gate_weight.shape[0], K)
        x = hidden_states.reshape(-1, h)
        router_logits = x @ gate_weight.T
        probs = jax.nn.softmax(router_logits.astype(jnp.float32), axis=-1)
        top_v, top_i = jax.lax.top_k(probs, top_k)
        top_v = top_v / top_v.sum(axis=-1, keepdims=True)
        combine_w = jnp.einsum('tke,tk->te', jax.nn.one_hot(top_i, num_experts, dtype=top_v.dtype), top_v).astype(x.dtype)

        def expert_step(acc, inp):
            gu, dp, w = inp
            gate, up = jnp.split(x @ gu.T, 2, axis=-1)
            hidden = jax.nn.silu(gate) * up
            y = hidden @ dp.T
            return (acc + w[:, None] * y, None)
        out, _ = jax.lax.scan(expert_step, jnp.zeros_like(x), (gate_up_proj, down_proj, combine_w.T))
        return out.reshape(b, s, h)
    x = L0_attn_x
    mod = (_silu(L0_c) @ L0_wmod).reshape(L0_c.shape[0], 6, 1, -1)
    sa, ca, ga, sb, cb, gb = (mod[:, 0], mod[:, 1], mod[:, 2], mod[:, 3], mod[:, 4], mod[:, 5])
    ga = (2 * (ga >= 0) - 1) * jnp.maximum(jnp.abs(ga), 0.25)
    gb = (2 * (gb >= 0) - 1) * jnp.maximum(jnp.abs(gb), 0.25)
    h = _layernorm(x, axis=-1) * (1 + ca) + sa
    x = x + ga * _L0_attn_ref(h, L0_attn_Wq, L0_attn_Wk, L0_attn_Wv, L0_attn_Wo, L0_attn_q_scale, L0_attn_k_scale)
    h = _layernorm(x, axis=-1) * (1 + cb) + sb
    x = x + gb * _L0_ffn_ref(h, L0_ffn_w_gate, L0_ffn_w_shared_up, L0_ffn_w_shared_down, L0_ffn_w_up, L0_ffn_w_down)
    mod = (_silu(L1_c) @ L1_wmod).reshape(L1_c.shape[0], 6, 1, -1)
    sa, ca, ga, sb, cb, gb = (mod[:, 0], mod[:, 1], mod[:, 2], mod[:, 3], mod[:, 4], mod[:, 5])
    ga = (2 * (ga >= 0) - 1) * jnp.maximum(jnp.abs(ga), 0.25)
    gb = (2 * (gb >= 0) - 1) * jnp.maximum(jnp.abs(gb), 0.25)
    h = _layernorm(x, axis=-1) * (1 + ca) + sa
    x = x + ga * _L1_attn_ref(h, L1_attn_log_A_diag, L1_attn_B_mat, L1_attn_C_mat, L1_attn_D_vec, L1_attn_ln_w, L1_attn_ln_b)
    h = _layernorm(x, axis=-1) * (1 + cb) + sb
    x = x + gb * _L1_ffn_ref(h, L1_ffn_gate_weight, L1_ffn_gate_up_proj, L1_ffn_down_proj)
    return x

_drawn_inputs = setup_inputs


def setup_inputs(seed=0):
    import zlib

    import numpy as np

    out = dict(_drawn_inputs(seed))
    spreads = {'L0_attn_q_scale': (1.0, 0.6),
     'L0_attn_k_scale': (1.0, 0.6),
     'L1_attn_D_vec': (0.10000000149011612, 0.6),
     'L1_attn_ln_w': (1.0, 0.2),
     'L1_attn_ln_b': (0.0, 0.346)}
    factors = {'L0_attn_Wq': 6.739,
     'L0_attn_Wk': 6.808,
     'L0_attn_Wv': 5.469,
     'L0_attn_Wo': 5.444,
     'L0_ffn_w_gate': 8.0,
     'L0_ffn_w_shared_up': 8.0,
     'L0_ffn_w_shared_down': 8.0,
     'L0_ffn_w_up': 8.0,
     'L0_ffn_w_down': 8.0,
     'L0_c': 5.232,
     'L0_wmod': 5.32,
     'L1_attn_log_A_diag': 8.0,
     'L1_attn_B_mat': 8.0,
     'L1_attn_C_mat': 8.0,
     'L1_ffn_gate_weight': 8.0,
     'L1_ffn_gate_up_proj': 8.0,
     'L1_ffn_down_proj': 8.0}
    for name, (base, spread) in spreads.items():
        noise = np.random.default_rng([zlib.crc32(name.encode()), seed]).standard_normal(out[name].shape)
        drawn = base * np.exp(spread * noise) if base else spread * noise
        out[name] = jnp.asarray(drawn.astype(out[name].dtype))
    for name, factor in factors.items():
        out[name] = (out[name] * factor).astype(out[name].dtype)
    return out
```

```python
import concourse.bass as bass
from concourse import mybir
from contextlib import ExitStack

F32 = mybir.dt.float32
F32R = mybir.dt.float32r
BF16 = mybir.dt.bfloat16
I32 = mybir.dt.int32
U32 = mybir.dt.uint32
ALU = mybir.AluOpType
ACT = mybir.ActivationFunctionType
AX = mybir.AxisListType

P = 128
T, D = 1024, 256
NT = T // P
KC = D // P
NG, HPG, HD = 4, 4, 128
E0, H0, TOPK0, CAP = 64, 32, 6, 128
HS = 64
E1, H1, TOPK1 = 8, 512, 2
EPT0 = P // H0
IT0 = E0 // EPT0
IT1 = E1 * H1 // P
NSTATE = 128
QKV = HPG * HD + 2 * HD
MASKED = -1e30
EPS_Q = 1e-6
EPS_LN = 1e-5
RSQRT_SEED = float(0x5F3759DF)
NEWTON = 3

STEPS = 2 * HPG * 4
TLAG, PVLAG, WOLAG = 2, 3, 5


def step_of(n):
    m, qi = divmod(n, 4)
    return m, m // HPG, m % HPG, qi


def blocks(n):
    m, c, h, qi = step_of(n)
    return 4 * c + qi + 1


def transposed_groups(n):
    k = blocks(n)
    return [(u, 4 * u, min(4, k - 4 * u)) for u in range((k + 3) // 4)]


TG_BEFORE = [0]
for _n in range(STEPS):
    TG_BEFORE.append(TG_BEFORE[-1] + len(transposed_groups(_n)))
TGS = TG_BEFORE[-1]


def unit_base(m):
    return m if m < HPG else HPG + 2 * (m - HPG)


def unit_owner(u):
    return u if u < HPG else HPG + (u - HPG) // 2


NUNITS = 3


def program(nc, x_d, w_attn_d, w_out_d, qk_scale_d, gate0_d, ffn0_d, c_d, wmod_d, const_d,
            ssm_vec_d, bmat_d, cmat_d, lnwb_d, gate1_d, ffn1_d, out_d, wt0_d, wt1_d):
    ctx = ExitStack()

    def sem(name):
        return ctx.enter_context(nc.semaphore(name))

    def keep(name, shape, dt=F32):
        return ctx.enter_context(nc.sbuf_tensor(name, shape, dt))

    with ctx:
        x = keep("x", [P, NT, D])
        hT_hi = keep("hT_hi", [P, KC, T], F32R)
        hT_lo = keep("hT_lo", [P, KC, T], F32R)
        ident = keep("ident", [P, P])
        mask_b = keep("mask_b", [P, P], BF16)
        ident_b = keep("ident_b", [P, P], BF16)
        before_b = keep("before_b", [P, P], BF16)
        ones_b = keep("ones_b", [P, P], BF16)
        iota = keep("iota", [P, E0])
        modc = keep("modc", [P, 2, 12])
        opc = keep("opc", [P, 2, 12])
        gates = keep("gates", [P, 4, D])
        ccol = keep("ccol", [P, 4])
        cth = keep("cth", [P, 4])
        csil = keep("csil", [P, 4])
        qks = keep("qks", [P, 2])
        stat = keep("stat", [P, NT, 6])
        mv = keep("mv", [P, NT, 2])
        rs_in = keep("rs_in", [P, NT * 5])
        rs_y = keep("rs_y", [P, NT * 5])
        rs_t = keep("rs_t", [P, NT * 5])
        wqkv_raw = keep("wqkv_raw", [P, KC, QKV])
        wqkv_hi = keep("wqkv_hi", [P, KC, QKV], F32R)
        wqkv_lo = keep("wqkv_lo", [P, KC, QKV], F32R)
        wo_raw = keep("wo_raw", [P, HPG, D])
        wo_hi = keep("wo_hi", [P, HPG, D], F32R)
        wo_lo = keep("wo_lo", [P, HPG, D], F32R)

        def stage(*specs):
            with ExitStack() as s:
                return [s.enter_context(nc.sbuf_tensor(name, shape, dt)) for name, shape, dt in specs]

        hT_a, xn_a, wmod, csb, const, gmag, gsgn, grow = stage(
            ("hT_a", [P, KC, T], F32), ("xn_a", [P, NT, D], F32),
            ("wmod", [P, 2, KC, 6 * D], F32), ("csb", [P, 4, P], F32), ("const", [P, 3 * P + E0], F32),
            ("gmag", [P, 4, D], F32), ("gsgn", [P, 4, D], F32), ("grow", [P, 4, D], F32))
        (qT_hi, qT_lo, kT_hi, kT_lo, v_hi, v_lo, prob, pT_hi, pT_lo, oT_hi, oT_lo, q_f, k_f, sq, ytmp,
         mx, negb, rsum, rinv, rqs) = stage(
            ("qT_hi", [P, HPG, T], F32R), ("qT_lo", [P, HPG, T], F32R),
            ("kT_hi", [P, T], F32R), ("kT_lo", [P, T], F32R),
            ("v_hi", [P, NT, HD], F32R), ("v_lo", [P, NT, HD], F32R),
            ("prob", [P, 3, T], F32),
            ("pT_hi", [P, NUNITS, 4, 512], F32R), ("pT_lo", [P, NUNITS, 4, 512], F32R),
            ("oT_hi", [P, HPG, 512], F32R), ("oT_lo", [P, HPG, 512], F32R),
            ("q_f", [P, 2, HPG * HD], F32), ("k_f", [P, NT, HD], F32),
            ("sq", [P, 5 * HD], F32), ("ytmp", [P, 4, D], F32),
            ("mx", [P, 2], F32), ("negb", [P, 2], F32), ("rsum", [P, 4], F32), ("rinv", [P, 2], F32),
            ("rqs", [P, NT * 5], F32))
        (hT_b, xn_b, w_raw, w_hi, w_lo, wbc, th, fa, fb, fc, hid_hi, hid_lo, wgate, wgate1, key, sig, sel, eq,
         ws, wc, sel_b, top, topi, topf, wT, rsm, bT, cT, hs, zT, lnwb, svec, a_t, a_disc, opd, ffy) = stage(
            ("hT_b", [P, KC, T], F32), ("xn_b", [P, NT, D], F32),
            ("w_raw", [P, 2, 6 * P], F32), ("w_hi", [P, 2, 6 * P], F32R), ("w_lo", [P, 2, 6 * P], F32R),
            ("wbc", [P, 2, T], F32), ("th", [P, 2, 512], F32), ("fa", [P, 2, 512], F32),
            ("fb", [P, 2, 512], F32), ("fc", [P, 2, 512], F32),
            ("hid_hi", [P, 2, 512], F32R), ("hid_lo", [P, 2, 512], F32R),
            ("wgate", [P, KC, E0], F32), ("wgate1", [P, KC, E1], F32),
            ("key", [P, NT, E0], F32), ("sig", [P, NT, E0], F32), ("sel", [P, NT, E0], F32),
            ("eq", [P, NT, E0], F32), ("ws", [P, NT, E0], F32), ("wc", [P, NT, E0], F32),
            ("sel_b", [P, NT, E0], BF16), ("top", [P, NT, 8], F32), ("topi", [P, NT, 8], U32),
            ("topf", [P, NT, 8], F32), ("wT", [E0, T], F32), ("rsm", [P, 4, NT], F32),
            ("bT", [P, KC, NSTATE], F32), ("cT", [P, D], F32), ("hs", [P, T], F32),
            ("zT", [P, KC, T], F32), ("lnwb", [P, 2, D], F32), ("svec", [P, 1 + KC], F32),
            ("a_t", [P, 1], F32), ("a_disc", [P, 1], F32), ("opd", [P, KC], F32), ("ffy", [P, NT, D], F32))
        hT_of = [hT_a, hT_b, hT_b, hT_b]
        xn_of = [xn_a, xn_b, xn_b, xn_b]
        ps = ctx.enter_context(nc.psum_tensor("ps", [P, 8, 512], F32))

        (setup_loaded, x_loaded, consts_ready, c_tanh, c_ready, mod_done, mod_ready, vec_step, ln_normed,
         ln_transposed, h_full, h_hi, h_lo, wqkv_raw_in, wqkv_hi_in, wqkv_ready, wo_raw_in, wo_hi_in, wo_ready,
         projected, q_copied, kv_copied, squares, square_sums, v_split, q_transposed, qT_hi_done, qT_lo_done,
         qk_norm_step, k_normed, k_transposed, kT_hi_done, kT_lo_done, scored, row_max, bias_ready, exp_done,
         row_inv, prob_ready, p_transposed, pT_hi_done, pT_lo_done, pv_done, oT_hi_done, oT_lo_done, wo_done,
         y_scaled, y_added) = [sem(n) for n in (
            "setup_loaded x_loaded consts_ready c_tanh c_ready mod_done mod_ready vec_step ln_normed "
            "ln_transposed h_full h_hi h_lo wqkv_raw_in wqkv_hi_in wqkv_ready wo_raw_in wo_hi_in wo_ready "
            "projected q_copied kv_copied squares square_sums v_split q_transposed qT_hi_done qT_lo_done "
            "qk_norm_step k_normed k_transposed kT_hi_done kT_lo_done scored row_max bias_ready exp_done "
            "row_inv prob_ready p_transposed pT_hi_done pT_lo_done pv_done oT_hi_done oT_lo_done wo_done "
            "y_scaled y_added").split()]
        (gate_loaded, logits_done, logits_exp, shifted, sel_ready, counted, wc_ready,
         wc_transposed, wT_ready, wT_stored, y_cleared, w_ready, up_done, tanh_done, silu_done, gated, weighted,
         hid_hi_done, hid_lo_done, down_done, ssm_loaded, a_step, u_done, scanned, hc_done, z_ready,
         z_transposed, sublayer_added, stored) = [sem(n) for n in (
            "gate_loaded logits_done logits_exp shifted sel_ready counted wc_ready "
            "wc_transposed wT_ready wT_stored y_cleared w_ready up_done tanh_done silu_done gated weighted "
            "hid_hi_done hid_lo_done down_done ssm_loaded a_step u_done scanned hc_done z_ready "
            "z_transposed sublayer_added stored").split()]
        w_raw_in = [sem("w_raw_in0"), sem("w_raw_in1")]
        w_hi_in = [sem("w_hi_in0"), sem("w_hi_in1")]
        wbc_in = [sem("wbc_in0"), sem("wbc_in1")]

        FF = [dict(total=1 + IT0, peel=3, base=0, wused=(0, 0), cused=(-1, 0)),
              dict(total=IT1, peel=2, base=1 + IT0, wused=(1 + IT0 // 2, IT0 // 2), cused=(IT0 // 2, IT0 // 2))]

        def walk(eng, f, body, start=0):
            peel = FF[f]["peel"]
            for pos in range(start, peel):
                body(pos, pos // 2, pos)
            with eng.Fori(0, (FF[f]["total"] - peel) // 2) as j:
                for u in range(2):
                    body(j * 2 + (peel + u), j + (peel + u) // 2, peel + u)

        block = ctx.enter_context(nc.Block())

        @block.sync
        def _(sp):
            sp.dma_start(ccol[:], c_d).then_inc(setup_loaded, 16)
            sp.dma_start(wmod[:], wmod_d).then_inc(setup_loaded, 16)
            sp.dma_start(const[:], const_d).then_inc(setup_loaded, 16)
            sp.dma_start(qks[:], qk_scale_d).then_inc(setup_loaded, 16)
            sp.dma_start(wqkv_raw[:], w_attn_d[0]).then_inc(wqkv_raw_in, 16)
            sp.dma_start(wo_raw[:], w_out_d[0]).then_inc(wo_raw_in, 16)
            with sp.Fori(0, NG - 1) as g:
                sp.wait_ge(projected, g * NT + NT)
                sp.dma_start(wqkv_raw[:], w_attn_d[g + 1]).then_inc(wqkv_raw_in, 16)
                sp.wait_ge(wo_done, g * 2 + 2)
                sp.dma_start(wo_raw[:], w_out_d[g + 1]).then_inc(wo_raw_in, 16)

            def load_weights(f, src, pos, low):
                buf = low % 2
                if FF[f]["base"] + low >= 2:
                    sp.wait_ge(w_ready, pos + (FF[f]["base"] - 1))
                sp.dma_start(w_raw[:, buf, :], src[pos]).then_inc(w_raw_in[buf], 16)

            def load_combine(f, dst_view, row, pos, low):
                buf = low % 2
                if FF[f]["base"] + low >= 2:
                    sp.wait_ge(weighted, pos * 2 + (FF[f]["base"] * 2 - 2))
                sp.dma_start(dst_view(wbc[:, buf, :]), row).then_inc(wbc_in[buf], 16)

            sp.wait_ge(y_added, 2 * NG)
            sp.dma_start(wgate[:], gate0_d).then_inc(gate_loaded, 16)
            load_weights(0, ffn0_d, 0, 0)
            load_weights(0, ffn0_d, 1, 1)
            sp.wait_ge(wT_ready, 1)
            sp.dma_start(wt0_d, wT[0:E0, :]).then_inc(wT_stored, 16)
            sp.wait_ge(wT_stored, 16)
            rows0 = wt0_d.rearrange("(i e) t -> i e t", e=EPT0)

            def tile0(pos, half, low):
                if low >= 2:
                    load_weights(0, ffn0_d, pos, low)
                load_combine(0, lambda w: w.rearrange("(e r) t -> e r t", e=EPT0) if False else w,
                             rows0[pos - 1].unsqueeze(1).to_broadcast([EPT0, H0, T]), pos, low)
            walk(sp, 0, tile0, start=1)

            sp.wait_ge(sublayer_added, 1)
            sp.dma_start(svec[:], ssm_vec_d).then_inc(ssm_loaded, 16)
            sp.dma_start(bT[:], bmat_d).then_inc(ssm_loaded, 16)
            sp.dma_start(cT[:], cmat_d).then_inc(ssm_loaded, 16)
            sp.dma_start(lnwb[:], lnwb_d.unsqueeze(0).to_broadcast([P, 2, D])).then_inc(ssm_loaded, 16)
            sp.dma_start(wgate1[:], gate1_d).then_inc(gate_loaded, 16)

            load_weights(1, ffn1_d, 0, 0)
            load_weights(1, ffn1_d, 1, 1)
            sp.wait_ge(wT_ready, 2)
            for r in range(4):
                sp.dma_start(wt1_d[:, r, :], wT[0:E1, :]).then_inc(wT_stored, 16)
            sp.wait_ge(wT_stored, 16 * 5)
            rows1 = wt1_d.rearrange("e r t -> (e r) t")

            def tile1(pos, half, low):
                if low >= 2:
                    load_weights(1, ffn1_d, pos, low)
                load_combine(1, lambda w: w, rows1[pos].unsqueeze(0).to_broadcast([P, T]), pos, low)
            walk(sp, 1, tile1)

            sp.wait_ge(sublayer_added, 3)
            sp.dma_start(out_d.rearrange("(t p) d -> p t d", p=P), x[:]).then_inc(stored, 16)
            sp.wait_ge(stored, 16)

        @block.gpsimd
        def _(pool):
            def split(raw, hi, lo, raw_in, hi_in, value, ready):
                pool.wait_ge(raw_in, value)
                pool.wait_ge(hi_in, value)
                nc.gpsimd.tensor_tensor(lo, raw, hi, ALU.subtract).then_inc(ready, 1)

            pool.dma_start(wqkv_hi[:], w_attn_d[0]).then_inc(wqkv_hi_in, 16)
            pool.dma_start(wo_hi[:], w_out_d[0]).then_inc(wo_hi_in, 16)
            split(wqkv_raw[:], wqkv_hi[:], wqkv_lo[:], wqkv_raw_in, wqkv_hi_in, 16, wqkv_ready)
            split(wo_raw[:], wo_hi[:], wo_lo[:], wo_raw_in, wo_hi_in, 16, wo_ready)
            with pool.Fori(0, NG - 1) as g:
                pool.wait_ge(projected, g * NT + NT)
                pool.dma_start(wqkv_hi[:], w_attn_d[g + 1]).then_inc(wqkv_hi_in, 16)
                split(wqkv_raw[:], wqkv_hi[:], wqkv_lo[:], wqkv_raw_in, wqkv_hi_in, g * 16 + 32, wqkv_ready)
                pool.wait_ge(wo_done, g * 2 + 2)
                pool.dma_start(wo_hi[:], w_out_d[g + 1]).then_inc(wo_hi_in, 16)
                split(wo_raw[:], wo_hi[:], wo_lo[:], wo_raw_in, wo_hi_in, g * 16 + 32, wo_ready)

            def ffn_weights(f, src):
                base, wused = FF[f]["base"], FF[f]["wused"]

                def tile(pos, half, low):
                    buf = low % 2
                    if base + low >= 2:
                        pool.wait_ge(down_done, pos * 2 + (base * 2 - 2))
                    pool.dma_start(w_hi[:, buf, :], src[pos]).then_inc(w_hi_in[buf], 16)
                    split(w_raw[:, buf, :], w_hi[:, buf, :], w_lo[:, buf, :], w_raw_in[buf], w_hi_in[buf],
                          half * 16 + 16 * (wused[buf] + 1), w_ready)
                walk(pool, f, tile)

            pool.wait_ge(y_added, 2 * NG)
            ffn_weights(0, ffn0_d)
            pool.wait_ge(sublayer_added, 1)
            ffn_weights(1, ffn1_d)

        @block.scalar
        def _(act):
            act.dma_start(x[:], x_d.rearrange("(t p) d -> p t d", p=P)).then_inc(x_loaded, 16)
            act.wait_ge(setup_loaded, 64)
            nc.scalar.activation(cth[:], ccol[:], ACT.Tanh, scale=0.5).then_inc(c_tanh, 1)

            def modulate(n, layer, kind):
                hT = hT_of[n]
                if n == 0:
                    act.wait_ge(mod_ready, 1)
                for hf in range(2):
                    for kc in range(KC):
                        b = 2 * hf + kc
                        act.wait_ge(ln_transposed, 4 * n + b + 1)
                        cols = hT[:, kc, hf * 512:hf * 512 + 512]
                        nc.scalar.activation(cols, ps[:, 4 + b, :], ACT.Identity,
                                             bias=modc[:, layer, 2 * kind + kc:2 * kind + kc + 1],
                                             scale=opc[:, layer, 2 * kind + 2 + kc:2 * kind + 3 + kc]
                                             ).then_inc(h_full, 1)
                        act.wait_ge(h_full, 4 * n + b + 1)
                        nc.scalar.activation(hT_hi[:, kc, hf * 512:hf * 512 + 512], cols,
                                             ACT.Copy).then_inc(h_hi, 1)

            modulate(0, 0, 0)

            with act.Fori(0, NG) as g:
                def q_high(t):
                    act.wait_ge(q_transposed, g * NT + (t + 1))
                    nc.scalar.activation(qT_hi[:, :, t * P:(t + 1) * P],
                                         ps[:, 4 + t % 2, :].rearrange("p (h t) -> p h t", h=HPG),
                                         ACT.Copy, scale=qks[:, 0:1]).then_inc(qT_hi_done, 1)

                for t in range(NT):
                    act.wait_ge(projected, g * NT + (t + 1))
                    if t >= 1:
                        act.wait_ge(square_sums, g * NT + t)
                    nc.scalar.activation(sq[:, HPG * HD:], ps[:, 2 + t % 2, 0:HD], ACT.Square)
                    nc.scalar.activation(v_hi[:, t, :], ps[:, 2 + t % 2, HD:2 * HD], ACT.Copy).then_inc(v_split, 1)
                    nc.scalar.activation(sq[:, 0:HPG * HD], ps[:, t % 2, :], ACT.Square).then_inc(squares, 1)
                    if t >= 2:
                        act.wait_ge(q_transposed, g * NT + (t - 1))
                    nc.scalar.activation(q_f[:, t % 2, :], ps[:, t % 2, :], ACT.Copy).then_inc(q_copied, 1)
                    if t >= 1:
                        q_high(t - 1)
                q_high(NT - 1)
                for b in range(2):
                    act.wait_ge(k_transposed, g * 2 + (b + 1))
                    nc.scalar.activation(kT_hi[:, b * 512:(b + 1) * 512], ps[:, 2 + b, :], ACT.Copy,
                                         scale=qks[:, 1:2]).then_inc(kT_hi_done, 1)

                for n in range(STEPS + WOLAG + 1):
                    if n < STEPS:
                        m, c, h, qi = step_of(n)
                        w = blocks(n) * P
                        pair = 2 * (n % 2)
                        act.wait_ge(bias_ready, g * STEPS + (n + 1))
                        if n >= 3:
                            act.wait_ge(p_transposed, g * TGS + TG_BEFORE[n - 2])
                        if c == 0:
                            src, dst = ps[:, pair, 0:w], prob[:, n % 3, 0:w]
                        else:
                            src = ps[:, pair:pair + 2, 0:w // 2]
                            dst = prob[:, n % 3, 0:w].rearrange("p (a w) -> p a w", a=2)
                        nc.scalar.activation(dst, src, ACT.Exp, bias=negb[:, n % 2:n % 2 + 1],
                                             scale=rqs[:, (4 * c + qi) * 5 + h:(4 * c + qi) * 5 + h + 1],
                                             accum_out=rsum[:, n % 4:n % 4 + 1]).then_inc(exp_done, 1)
                    m = (n - 1 - (3 + PVLAG)) // 4
                    if n - 1 >= 3 + PVLAG and (n - 1 - (3 + PVLAG)) % 4 == 0 and m < 2 * HPG:
                        act.wait_ge(pv_done, g * 2 * HPG + (m + 1))
                        if m >= HPG:
                            act.wait_ge(wo_done, g * 2 + 1)
                        nc.scalar.activation(oT_hi[:, m % HPG, :], ps[:, 6 + m % 2, :],
                                             ACT.Copy).then_inc(oT_hi_done, 1)
                    if 0 <= n - TLAG < STEPS:
                        k = n - TLAG
                        m, c, h, qi = step_of(k)
                        for u, j0, nb in transposed_groups(k):
                            q = TG_BEFORE[k] + u
                            unit = unit_base(m) + u
                            act.wait_ge(p_transposed, g * TGS + (q + 1))
                            if unit >= NUNITS:
                                act.wait_ge(pv_done, g * 2 * HPG + (unit_owner(unit - NUNITS) + 1))
                            nc.scalar.activation(pT_hi[:, unit % NUNITS, 0:nb, qi * P:(qi + 1) * P],
                                                 ps[:, 4 + q % 2, 0:nb * P].rearrange("p (j t) -> p j t", j=nb),
                                                 ACT.Copy).then_inc(pT_hi_done, 1)

            def ffn(f, after_first=None):
                base, total = FF[f]["base"], FF[f]["total"]

                def high(pos, low, hf, back):
                    act.wait_ge(weighted, pos * 2 + (2 * (base - back) + hf + 1))
                    if 2 * (base + low - back) + hf - 1 > 0:
                        act.wait_ge(down_done, pos * 2 + (2 * (base - back) + hf - 1))
                    nc.scalar.activation(hid_hi[:, hf, :], fc[:, hf, :], ACT.Copy).then_inc(hid_hi_done, 1)

                def tile(pos, half, low):
                    for hf in range(2):
                        act.wait_ge(up_done, pos * 2 + (2 * base + hf + 1))
                        if 2 * (base + low) + hf - 1 > 0:
                            act.wait_ge(silu_done, pos * 2 + (2 * base + hf - 1))
                        nc.scalar.activation(th[:, hf, :], ps[:, 4 + 2 * hf, :], ACT.Tanh,
                                             scale=0.5).then_inc(tanh_done, 1)
                        if hf == 1:
                            high(pos, low, 0, 0)
                        elif low > 0:
                            high(pos, low, 1, 1)
                walk(act, f, tile)
                high(total - 1, total - 1, 1, 0)

            modulate(1, 0, 3)
            act.wait_ge(logits_done, 1)
            nc.scalar.activation(sig[:], ps[:, 0, :].rearrange("p (t e) -> p t e", t=NT), ACT.Exp,
                                 scale=-1.0).then_inc(logits_exp, 1)
            ffn(0)

            modulate(2, 1, 0)
            act.wait_ge(ssm_loaded, 64)
            nc.scalar.activation(a_t[:], svec[:, 0:1], ACT.Exp).then_inc(a_step, 1)
            act.wait_ge(a_step, 1)
            nc.scalar.activation(a_disc[:], a_t[:], ACT.Exp, scale=-1.0).then_inc(a_step, 1)

            modulate(3, 1, 3)
            act.wait_ge(shifted, 1)
            nc.scalar.activation(key[:, :, 0:E1], sig[:, :, 0:E1], ACT.Exp).then_inc(logits_exp, 1)
            ffn(1)

        @block.vector
        def _(dve):
            steps = [0]

            def link(ins):
                steps[0] += 1
                ins.then_inc(vec_step, 1)
                dve.wait_ge(vec_step, steps[0])

            def inverse_root(width, link_):
                v, y, t = rs_in[:, 0:width], rs_y[:, 0:width], rs_t[:, 0:width]
                link_(nc.vector.tensor_scalar(y.bitcast(I32), v.bitcast(I32), -0.5, RSQRT_SEED, ALU.mult, ALU.add))
                for _ in range(NEWTON):
                    link_(nc.vector.tensor_tensor(t, y, y, ALU.mult))
                    link_(nc.vector.scalar_tensor_tensor(t, t, -0.5, v, ALU.mult, ALU.mult))
                    link_(nc.vector.scalar_tensor_tensor(y, t, 1.5, y, ALU.add, ALU.mult))

            def normalise(src, dst, done):
                for t in range(NT):
                    ins = nc.vector.bn_stats(stat[:, t, :], src(t))
                link(ins)
                for t in range(NT):
                    ins = nc.vector.bn_aggr(mv[:, t, :], stat[:, t, :])
                link(ins)
                link(nc.vector.tensor_scalar(rs_in[:, 0:NT], mv[:, :, 1], EPS_LN, None, ALU.add))
                inverse_root(NT, link)
                for t in range(NT):
                    nc.vector.tensor_scalar(dst[:, t, :], src(t), mv[:, t, 0:1], rs_y[:, t:t + 1],
                                            ALU.subtract, ALU.mult).then_inc(done, 1)

            def split_input(n):
                hT = hT_of[n]
                for hf in range(2):
                    for kc in range(KC):
                        dve.wait_ge(h_hi, 4 * n + 2 * hf + kc + 1)
                        s = slice(hf * 512, hf * 512 + 512)
                        nc.vector.tensor_tensor(hT_lo[:, kc, s], hT[:, kc, s], hT_hi[:, kc, s],
                                                ALU.subtract).then_inc(h_lo, 1)

            dve.wait_ge(setup_loaded, 64)
            nc.vector.tensor_copy(ident[:], const[:, 0:P])
            nc.vector.tensor_copy(ident_b[:], const[:, 0:P])
            nc.vector.tensor_copy(mask_b[:], const[:, P:2 * P])
            nc.vector.tensor_copy(before_b[:], const[:, 2 * P:3 * P])
            nc.vector.memset(ones_b[:], 1.0)
            nc.vector.tensor_copy(iota[:], const[:, 3 * P:]).then_inc(consts_ready, 1)
            dve.wait_ge(c_tanh, 1)
            link(nc.vector.scalar_tensor_tensor(csil[:], cth[:], 1.0, ccol[:], ALU.add, ALU.mult))
            link(nc.vector.tensor_scalar(csil[:], csil[:], 0.5, None, ALU.mult))
            nc.vector.tensor_copy(csb[:], csil[:].unsqueeze(2).to_broadcast([P, 4, P])).then_inc(c_ready, 1)
            dve.wait_ge(x_loaded, 16)
            normalise(lambda t: x[:, t, :], xn_of[0], ln_normed)
            dve.wait_ge(mod_done, 1)
            nc.vector.tensor_copy(modc[:], ps[:, 0, 0:24].rearrange("p (l j) -> p l j", l=2))
            nc.vector.tensor_scalar(opc[:], ps[:, 0, 0:24].rearrange("p (l j) -> p l j", l=2), 1.0, None,
                                    ALU.add).then_inc(mod_ready, 1)
            dve.wait_ge(mod_done, 2)
            link(nc.vector.tensor_copy(grow[:], ps[:, 1:3, :].rearrange("p b (r d) -> p (b r) d", r=2)))
            link(nc.vector.tensor_scalar(gsgn[:], grow[:], 0.0, 2.0, ALU.is_ge, ALU.mult))
            link(nc.vector.tensor_scalar(gsgn[:], gsgn[:], -1.0, None, ALU.add))
            link(nc.vector.scalar_tensor_tensor(gmag[:], grow[:], -1.0, grow[:], ALU.mult, ALU.max))
            link(nc.vector.scalar_tensor_tensor(gates[:], gmag[:], 0.25, gsgn[:], ALU.max, ALU.mult))
            split_input(0)

            NORM_STEPS = 3 + 3 * NEWTON
            with dve.Fori(0, NG) as g:
                def q_low(t):
                    dve.wait_ge(qT_hi_done, g * NT + (t + 1))
                    nc.vector.scalar_tensor_tensor(
                        qT_lo[:, :, t * P:(t + 1) * P], ps[:, 4 + t % 2, :].rearrange("p (h t) -> p h t", h=HPG),
                        qks[:, 0:1], qT_hi[:, :, t * P:(t + 1) * P], ALU.mult, ALU.subtract).then_inc(qT_lo_done, 1)

                for t in range(NT):
                    dve.wait_ge(projected, g * NT + (t + 1))
                    dve.wait_ge(v_split, g * NT + (t + 1))
                    nc.vector.tensor_copy(k_f[:, t, :], ps[:, 2 + t % 2, 0:HD])
                    nc.vector.tensor_tensor(v_lo[:, t, :], ps[:, 2 + t % 2, HD:2 * HD], v_hi[:, t, :],
                                            ALU.subtract).then_inc(kv_copied, 1)
                    dve.wait_ge(squares, g * NT + (t + 1))
                    nc.vector.reduce_sum(rs_in[:, 5 * t:5 * t + 5], sq[:].rearrange("p (h d) -> p h d", d=HD),
                                         AX.X).then_inc(square_sums, 1)
                    if t >= 1:
                        q_low(t - 1)
                q_low(NT - 1)
                dve.wait_ge(square_sums, g * NT + NT)
                dve.wait_ge(kv_copied, g * NT + NT)
                norm_steps = [0]

                def norm_link(ins):
                    norm_steps[0] += 1
                    ins.then_inc(qk_norm_step, 1)
                    dve.wait_ge(qk_norm_step, g * NORM_STEPS + norm_steps[0])

                norm_link(nc.vector.tensor_scalar(rs_in[:], rs_in[:], 1.0 / HD, EPS_Q, ALU.mult, ALU.add))
                inverse_root(5 * NT, norm_link)
                for t in range(NT):
                    nc.vector.tensor_scalar(k_f[:, t, :], k_f[:, t, :], rs_y[:, 5 * t + 4:5 * t + 5], None,
                                            ALU.mult).then_inc(k_normed, 1)
                norm_link(nc.vector.tensor_scalar(rqs[:], rs_y[:], HD ** -0.5, None, ALU.mult))
                assert norm_steps[0] == NORM_STEPS
                for b in range(2):
                    dve.wait_ge(kT_hi_done, g * 2 + (b + 1))
                    s = slice(b * 512, (b + 1) * 512)
                    nc.vector.scalar_tensor_tensor(kT_lo[:, s], ps[:, 2 + b, :], qks[:, 1:2], kT_hi[:, s],
                                                   ALU.mult, ALU.subtract).then_inc(kT_lo_done, 1)

                for n in range(STEPS + WOLAG + 1):
                    if n < STEPS:
                        m, c, h, qi = step_of(n)
                        w = blocks(n) * P
                        pair = 2 * (n % 2)
                        i = n % 2
                        dve.wait_ge(scored, g * STEPS + (n + 1))
                        if c == 0:
                            nc.vector.reduce_max(mx[:, i:i + 1], ps[:, pair, 0:w], AX.X).then_inc(row_max, 1)
                        else:
                            nc.vector.reduce_max(mx[:, i:i + 1], ps[:, pair:pair + 2, 0:w // 2],
                                                 AX.XY).then_inc(row_max, 1)
                        dve.wait_ge(row_max, g * STEPS + (n + 1))
                        col = (4 * c + qi) * 5 + h
                        nc.vector.tensor_scalar(negb[:, i:i + 1], mx[:, i:i + 1], rqs[:, col:col + 1], -1.0,
                                                ALU.mult, ALU.mult).then_inc(bias_ready, 1)
                    if 1 <= n <= STEPS:
                        k = n - 1
                        w = blocks(k) * P
                        i = k % 2
                        dve.wait_ge(exp_done, g * STEPS + (k + 1))
                        nc.vector.reciprocal(rinv[:, i:i + 1], rsum[:, k % 4:k % 4 + 1]).then_inc(row_inv, 1)
                        dve.wait_ge(row_inv, g * STEPS + (k + 1))
                        nc.vector.tensor_scalar(prob[:, k % 3, 0:w], prob[:, k % 3, 0:w], rinv[:, i:i + 1], None,
                                                ALU.mult).then_inc(prob_ready, 1)
                    m = (n - 1 - (3 + PVLAG)) // 4
                    if n - 1 >= 3 + PVLAG and (n - 1 - (3 + PVLAG)) % 4 == 0 and m < 2 * HPG:
                        dve.wait_ge(oT_hi_done, g * 2 * HPG + (m + 1))
                        nc.vector.tensor_tensor(oT_lo[:, m % HPG, :], ps[:, 6 + m % 2, :], oT_hi[:, m % HPG, :],
                                                ALU.subtract).then_inc(oT_lo_done, 1)
                    for c in range(2):
                        if n - 1 == 16 * c + 15 + WOLAG:
                            dve.wait_ge(wo_done, g * 2 + (c + 1))
                            nc.vector.tensor_tensor(ytmp[:], ps[:, 6:8, :].rearrange("p b (r d) -> p (b r) d", r=2),
                                                    gates[:, 0:1, :].to_broadcast([P, 4, D]),
                                                    ALU.mult).then_inc(y_scaled, 1)
                            dve.wait_ge(y_scaled, g * 2 + (c + 1))
                            nc.vector.tensor_tensor(x[:, 4 * c:4 * c + 4, :], x[:, 4 * c:4 * c + 4, :], ytmp[:],
                                                    ALU.add).then_inc(y_added, 1)
                    if 0 <= n - TLAG < STEPS:
                        k = n - TLAG
                        m, c, h, qi = step_of(k)
                        for u, j0, nb in transposed_groups(k):
                            q = TG_BEFORE[k] + u
                            unit = unit_base(m) + u
                            dve.wait_ge(pT_hi_done, g * TGS + (q + 1))
                            dst = (slice(None), unit % NUNITS, slice(0, nb), slice(qi * P, (qi + 1) * P))
                            nc.vector.tensor_tensor(pT_lo[dst],
                                                    ps[:, 4 + q % 2, 0:nb * P].rearrange("p (j t) -> p j t", j=nb),
                                                    pT_hi[dst], ALU.subtract).then_inc(pT_lo_done, 1)

            def add_sublayer(f, gate):
                dve.wait_ge(down_done, 2 * (FF[f]["base"] + FF[f]["total"]))
                link(nc.vector.tensor_tensor(ffy[:], ps[:, 0:4, :].rearrange("p b (r d) -> p (b r) d", r=2),
                                             gates[:, gate:gate + 1, :].to_broadcast([P, NT, D]), ALU.mult))
                link(nc.vector.tensor_tensor(x[:], x[:], ffy[:], ALU.add))

            def pick(source, width, k):
                for t in range(NT):
                    ins = nc.vector.max(top[:, t, :], source[:, t, 0:width])
                link(ins)
                for t in range(NT):
                    ins = nc.vector.max_index(topi[:, t, :], top[:, t, :], source[:, t, 0:width])
                link(ins)
                link(nc.vector.tensor_copy(topf[:], topi[:]))
                place = iota[:, 0:width].unsqueeze(1).to_broadcast([P, NT, width])
                for i in range(k):
                    index = topf[:, :, i:i + 1].to_broadcast([P, NT, width])
                    got = sel if i == 0 else eq
                    link(nc.vector.tensor_tensor(got[:, :, 0:width], place, index, ALU.is_equal))
                    if i:
                        link(nc.vector.tensor_tensor(sel[:, :, 0:width], sel[:, :, 0:width], eq[:, :, 0:width],
                                                     ALU.add))

            def store_combine(f, width):
                dve.wait_ge(wc_transposed, f + 1)
                nc.vector.tensor_copy(wT[0:width, :], ps[0:width, 1:3, :].rearrange("p b t -> p (b t)")
                                      ).then_inc(wT_ready, 1)

            def ffn_tiles(f, start, stop_after=False, last_low=True):
                base, total, cused = FF[f]["base"], FF[f]["total"], FF[f]["cused"]

                def low_half(pos, hf, back):
                    dve.wait_ge(hid_hi_done, pos * 2 + (2 * (base - back) + hf + 1))
                    nc.vector.tensor_tensor(hid_lo[:, hf, :], fc[:, hf, :], hid_hi[:, hf, :],
                                            ALU.subtract).then_inc(hid_lo_done, 1)

                def tile(pos, half, low):
                    buf = low % 2
                    for hf in range(2):
                        k1 = 2 * base + hf + 1
                        dve.wait_ge(tanh_done, pos * 2 + k1)
                        nc.vector.scalar_tensor_tensor(fa[:, hf, :], th[:, hf, :], 1.0, ps[:, 4 + 2 * hf, :],
                                                       ALU.add, ALU.mult).then_inc(silu_done, 1)
                        dve.wait_ge(silu_done, pos * 2 + k1)
                        nc.vector.tensor_tensor(fb[:, hf, :], fa[:, hf, :], ps[:, 5 + 2 * hf, :],
                                                ALU.mult).then_inc(gated, 1)
                        dve.wait_ge(gated, pos * 2 + k1)
                        if 2 * (base + low) + hf - 1 > 0:
                            dve.wait_ge(hid_lo_done, pos * 2 + (k1 - 2))
                        if f == 0 and isinstance(pos, int) and pos == 0:
                            nc.vector.tensor_scalar(fc[:, hf, :], fb[:, hf, :], 0.5, None,
                                                    ALU.mult).then_inc(weighted, 1)
                        else:
                            dve.wait_ge(wbc_in[buf], half * 16 + 16 * (cused[buf] + 1))
                            nc.vector.tensor_tensor(fc[:, hf, :], fb[:, hf, :],
                                                    wbc[:, buf, hf * 512:hf * 512 + 512],
                                                    ALU.mult).then_inc(weighted, 1)
                        if hf == 1:
                            low_half(pos, 0, 0)
                        elif low > 0:
                            low_half(pos, 1, 1)
                return tile, lambda: low_half(total - 1, 1, 0)

            def clear_sum():
                nc.vector.memset(ps[:, 0:4, :], 0.0).then_inc(y_cleared, 1)

            dve.wait_ge(y_added, 2 * NG)
            normalise(lambda t: x[:, t, :], xn_of[1], ln_normed)
            split_input(1)
            dve.wait_ge(logits_exp, 1)
            link(nc.vector.tensor_copy(key[:], ps[:, 0, :].rearrange("p (t e) -> p t e", t=NT)))
            pick(key, E0, TOPK0)
            nc.vector.tensor_copy(sel_b[:], sel[:]).then_inc(sel_ready, 1)
            dve.wait_ge(logits_exp, 1)
            link(nc.vector.tensor_scalar(sig[:], sig[:], 1.0, None, ALU.add))
            link(nc.vector.reciprocal(sig[:], sig[:]))
            link(nc.vector.tensor_tensor(ws[:], sel[:], sig[:], ALU.mult))
            link(nc.vector.reduce_sum(rsm[:, 0, :], ws[:], AX.X))
            link(nc.vector.reciprocal(rsm[:, 1, :], rsm[:, 0, :]))
            link(nc.vector.tensor_scalar(rsm[:, 2, :], rsm[:, 1, :], 0.5, None, ALU.mult))
            link(nc.vector.tensor_tensor(ws[:], ws[:], rsm[:, 2, :].unsqueeze(2).to_broadcast([P, NT, E0]),
                                         ALU.mult))
            dve.wait_ge(counted, 1)
            nc.vector.scalar_tensor_tensor(wc[:], ps[:, 3, :].rearrange("p (t e) -> p t e", t=NT), float(CAP),
                                           ws[:], ALU.is_lt, ALU.mult).then_inc(wc_ready, 1)
            store_combine(0, E0)
            dve.wait_ge(wT_ready, 1)
            clear_sum()
            tile, finish = ffn_tiles(0, 0)
            walk(dve, 0, tile)
            finish()
            add_sublayer(0, 1)
            nc.vector.memset(mx[:, 0:1] if False else a_t[:], 0.0).then_inc(sublayer_added, 1)

            normalise(lambda t: x[:, t, :], xn_of[2], ln_normed)
            split_input(2)
            dve.wait_ge(ssm_loaded, 64)
            link(nc.vector.tensor_scalar(opd[:], svec[:, 1:1 + KC], 1.0, None, ALU.add))
            dve.wait_ge(a_step, 2)
            for hf in range(2):
                dve.wait_ge(u_done, hf + 1)
                nc.vector.tensor_tensor_scan(hs[:, hf * 512:hf * 512 + 512], a_disc[:].to_broadcast([P, 512]),
                                             ps[:, hf, :], 0.0 if hf == 0 else hs[:, 511:512], ALU.mult,
                                             ALU.add).then_inc(scanned, 1)
                dve.wait_ge(scanned, hf + 1)
            for hf in range(2):
                for mc in range(KC):
                    b = 2 * hf + mc
                    dve.wait_ge(hc_done, b + 1)
                    s = slice(hf * 512, hf * 512 + 512)
                    nc.vector.scalar_tensor_tensor(zT[:, mc, s], hT_b[:, mc, s], opd[:, mc:mc + 1], ps[:, 4 + b, :],
                                                   ALU.mult, ALU.add).then_inc(z_ready, 1)
            link(nc.vector.tensor_tensor(lnwb[:], lnwb[:], gates[:, 2:3, :].to_broadcast([P, 2, D]), ALU.mult))
            dve.wait_ge(z_transposed, NT)
            zrow = ps[:, 0:4, :].rearrange("p b (r d) -> p (b r) d", r=2)
            normalise(lambda t: zrow[:, t, :], xn_b, scanned)
            dve.wait_ge(scanned, 2 + NT)
            link(nc.vector.tensor_tensor(ffy[:], xn_b[:], lnwb[:, 0:1, :].to_broadcast([P, NT, D]), ALU.mult))
            link(nc.vector.tensor_tensor(ffy[:], ffy[:], lnwb[:, 1:2, :].to_broadcast([P, NT, D]), ALU.add))
            link(nc.vector.tensor_tensor(x[:], x[:], ffy[:], ALU.add))
            nc.vector.memset(opd[:], 0.0).then_inc(sublayer_added, 1)

            normalise(lambda t: x[:, t, :], xn_of[3], ln_normed)
            split_input(3)
            dve.wait_ge(logits_done, 2)
            lg = ps[:, 0, 0:NT * E1].rearrange("p (t e) -> p t e", t=NT)
            link(nc.vector.reduce_max(rsm[:, 0, :], lg, AX.X))
            nc.vector.tensor_tensor(sig[:, :, 0:E1], lg, rsm[:, 0, :].unsqueeze(2).to_broadcast([P, NT, E1]),
                                    ALU.subtract).then_inc(shifted, 1)
            dve.wait_ge(logits_exp, 2)
            link(nc.vector.reduce_sum(rsm[:, 1, :], key[:, :, 0:E1], AX.X))
            link(nc.vector.reciprocal(rsm[:, 1, :], rsm[:, 1, :]))
            link(nc.vector.tensor_tensor(key[:, :, 0:E1], key[:, :, 0:E1],
                                         rsm[:, 1, :].unsqueeze(2).to_broadcast([P, NT, E1]), ALU.mult))
            pick(key, E1, TOPK1)
            link(nc.vector.tensor_tensor(ws[:, :, 0:E1], sel[:, :, 0:E1], key[:, :, 0:E1], ALU.mult))
            link(nc.vector.reduce_sum(rsm[:, 2, :], ws[:, :, 0:E1], AX.X))
            link(nc.vector.reciprocal(rsm[:, 2, :], rsm[:, 2, :]))
            link(nc.vector.tensor_scalar(rsm[:, 3, :], rsm[:, 2, :], 0.5, None, ALU.mult))
            nc.vector.tensor_tensor(wc[:, :, 0:E1], ws[:, :, 0:E1],
                                    rsm[:, 3, :].unsqueeze(2).to_broadcast([P, NT, E1]),
                                    ALU.mult).then_inc(wc_ready, 1)
            store_combine(1, E1)
            dve.wait_ge(wT_ready, 2)
            clear_sum()
            tile, finish = ffn_tiles(1, 0)
            walk(dve, 1, tile)
            finish()
            add_sublayer(1, 3)
            nc.vector.memset(opd[:], 0.0).then_inc(sublayer_added, 1)

        @block.tensor
        def _(pe):
            def three(out, w_hi_, w_lo_, m_hi, m_lo, start, stop):
                nc.tensor.matmul(out, w_hi_, m_hi, start=start, stop=False, skip_group_check=True)
                nc.tensor.matmul(out, w_hi_, m_lo, start=False, stop=False, skip_group_check=True)
                return nc.tensor.matmul(out, w_lo_, m_hi, start=False, stop=stop, skip_group_check=True)

            def transpose_input(n):
                xn = xn_of[n]
                for hf in range(2):
                    pe.wait_ge(ln_normed, NT * n + 4 * hf + 4)
                    for kc in range(KC):
                        for t in range(4):
                            ins = nc.tensor.transpose(ps[:, 4 + 2 * hf + kc, t * P:(t + 1) * P],
                                                      xn[:, 4 * hf + t, kc * P:(kc + 1) * P], ident[:])
                        ins.then_inc(ln_transposed, 1)

            pe.wait_ge(setup_loaded, 64)
            pe.wait_ge(c_ready, 1)
            for layer in range(2):
                for j in range(12):
                    for kc in range(KC):
                        ins = nc.tensor.matmul(ps[:, 0, 12 * layer + j:12 * layer + j + 1],
                                               wmod[:, layer, kc, j * P:(j + 1) * P],
                                               csil[:, 2 * layer + kc:2 * layer + kc + 1],
                                               start=(kc == 0), stop=(kc == KC - 1), skip_group_check=True)
            ins.then_inc(mod_done, 1)
            pe.wait_ge(consts_ready, 1)
            transpose_input(0)
            for layer in range(2):
                for i, kind in enumerate((2, 5)):
                    for kc in range(KC):
                        ins = nc.tensor.matmul(ps[:, 1 + layer, i * D:(i + 1) * D], csb[:, 2 * layer + kc, :],
                                               wmod[:, layer, kc, kind * D:(kind + 1) * D],
                                               start=(kc == 0), stop=(kc == KC - 1), skip_group_check=True)
            ins.then_inc(mod_done, 1)
            pe.wait_ge(h_lo, 4)
            pe.wait_ge(vec_step, 1)

            with pe.Fori(0, NG) as g:
                def transpose_q(t):
                    pe.wait_ge(q_copied, g * NT + (t + 1))
                    if t >= 2:
                        pe.wait_ge(qT_lo_done, g * NT + (t - 1))
                    for h in range(HPG):
                        ins = nc.tensor.transpose(ps[:, 4 + t % 2, h * P:(h + 1) * P],
                                                  q_f[:, t % 2, h * HD:(h + 1) * HD], ident[:])
                    ins.then_inc(q_transposed, 1)

                pe.wait_ge(wqkv_ready, g + 1)
                for t in range(NT):
                    if t >= 2:
                        pe.wait_ge(q_copied, g * NT + (t - 1))
                        pe.wait_ge(kv_copied, g * NT + (t - 1))
                    tok = slice(t * P, (t + 1) * P)
                    for out, cols in ((ps[:, t % 2, :], slice(0, HPG * HD)),
                                      (ps[:, 2 + t % 2, 0:2 * HD], slice(HPG * HD, QKV))):
                        for kc in range(KC):
                            ins = three(out, hT_hi[:, kc, tok], hT_lo[:, kc, tok], wqkv_hi[:, kc, cols],
                                        wqkv_lo[:, kc, cols], kc == 0, kc == KC - 1)
                    ins.then_inc(projected, 1)
                    if t >= 1:
                        transpose_q(t - 1)
                transpose_q(NT - 1)
                for b in range(2):
                    pe.wait_ge(k_normed, g * NT + (4 * b + 4))
                    for t in range(4):
                        ins = nc.tensor.transpose(ps[:, 2 + b, t * P:(t + 1) * P], k_f[:, 4 * b + t, :], ident[:])
                    ins.then_inc(k_transposed, 1)
                pe.wait_ge(q_copied, g * NT + NT)
                pe.wait_ge(qT_lo_done, g * NT + NT)
                pe.wait_ge(kT_lo_done, g * 2 + 2)

                for n in range(STEPS + WOLAG):
                    if n < STEPS:
                        m, c, h, qi = step_of(n)
                        w = blocks(n) * P
                        pair = 2 * (n % 2)
                        pieces = [(pair, 0, w)] if c == 0 else [(pair, 0, w // 2), (pair + 1, w // 2, w // 2)]
                        q = slice((4 * c + qi) * P, (4 * c + qi + 1) * P)
                        if n >= 2:
                            pe.wait_ge(exp_done, g * STEPS + (n - 1))
                        for bank, k0, kw in pieces:
                            three(ps[:, bank, 0:kw], qT_hi[:, h, q], qT_lo[:, h, q], kT_hi[:, k0:k0 + kw],
                                  kT_lo[:, k0:k0 + kw], True, False)
                        bank, k0, kw = pieces[-1]
                        nc.tensor.matmul(ps[:, bank, kw - P:kw], ident_b[:], mask_b[:], start=False, stop=True,
                                         skip_group_check=True).then_inc(scored, 1)
                    if 0 <= n - TLAG < STEPS:
                        k = n - TLAG
                        pe.wait_ge(prob_ready, g * STEPS + (k + 1))
                        for u, j0, nb in transposed_groups(k):
                            q = TG_BEFORE[k] + u
                            if q >= 2:
                                pe.wait_ge(pT_lo_done, g * TGS + (q - 1))
                            for j in range(nb):
                                ins = nc.tensor.transpose(ps[:, 4 + q % 2, j * P:(j + 1) * P],
                                                          prob[:, k % 3, (j0 + j) * P:(j0 + j + 1) * P], ident[:])
                            ins.then_inc(p_transposed, 1)
                    m = (n - (3 + PVLAG)) // 4
                    if n >= 3 + PVLAG and (n - (3 + PVLAG)) % 4 == 0 and m < 2 * HPG:
                        c = m // HPG
                        pe.wait_ge(pT_lo_done, g * TGS + TG_BEFORE[4 * m + 4])
                        if m >= 2:
                            pe.wait_ge(oT_lo_done, g * 2 * HPG + (m - 1))
                        if m == HPG:
                            pe.wait_ge(y_scaled, g * 2 + 1)
                        last = 4 * c + 3
                        for j in range(last + 1):
                            q0 = max(0, j - 4 * c) * P
                            u = (unit_base(m) + j // 4) % NUNITS
                            ins = three(ps[:, 6 + m % 2, q0:512], v_hi[:, j, :], v_lo[:, j, :],
                                        pT_hi[:, u, j % 4, q0:512], pT_lo[:, u, j % 4, q0:512], j == 0, j == last)
                        ins.then_inc(pv_done, 1)
                    for c in range(2):
                        if n == 16 * c + 15 + WOLAG:
                            pe.wait_ge(wo_ready, g + 1)
                            pe.wait_ge(oT_lo_done, g * 2 * HPG + (HPG * c + HPG))
                            for t in range(4):
                                tok = slice(t * P, (t + 1) * P)
                                for h in range(HPG):
                                    ins = three(ps[:, 6 + t // 2, (t % 2) * D:(t % 2 + 1) * D], oT_hi[:, h, tok],
                                                oT_lo[:, h, tok], wo_hi[:, h, :], wo_lo[:, h, :], h == 0,
                                                h == HPG - 1)
                            ins.then_inc(wo_done, 1)

            def router(gate, width):
                for t in range(NT):
                    for kc in range(KC):
                        ins = nc.tensor.matmul(ps[:, 0, t * width:(t + 1) * width], hT_b[:, kc, t * P:(t + 1) * P],
                                               gate[:, kc, :], start=(kc == 0), stop=(kc == KC - 1),
                                               skip_group_check=True)
                ins.then_inc(logits_done, 1)

            def transpose_combine(f, width):
                pe.wait_ge(wc_ready, f + 1)
                for t in range(NT):
                    ins = nc.tensor.transpose(ps[0:width, 1 + t // 4, (t % 4) * P:(t % 4 + 1) * P],
                                              wc[:, t, 0:width], ident[:])
                ins.then_inc(wc_transposed, 1)

            def ffn(f):
                base, total = FF[f]["base"], FF[f]["total"]

                def up(pos, low, hf):
                    buf = low % 2
                    if 2 * (base + low) + hf - 1 > 0:
                        pe.wait_ge(gated, pos * 2 + (2 * base + hf - 1))
                    tok = slice(hf * 512, hf * 512 + 512)
                    for v in range(2):
                        for kc in range(KC):
                            s = slice((2 * kc + v) * P, (2 * kc + v + 1) * P)
                            ins = three(ps[:, 4 + 2 * hf + v, :], w_hi[:, buf, s], w_lo[:, buf, s],
                                        hT_hi[:, kc, tok], hT_lo[:, kc, tok], kc == 0, kc == KC - 1)
                    ins.then_inc(up_done, 1)

                def down(pos, buf, hf, back):
                    pe.wait_ge(hid_lo_done, pos * 2 + (2 * (base - back) + hf + 1))
                    for t in range(4):
                        tile = 4 * hf + t
                        tok = slice(t * P, (t + 1) * P)
                        ins = three(ps[:, tile // 2, (tile % 2) * D:(tile % 2 + 1) * D], hid_hi[:, hf, tok],
                                    hid_lo[:, hf, tok], w_hi[:, buf, 4 * P:], w_lo[:, buf, 4 * P:], False, False)
                    ins.then_inc(down_done, 1)

                def tile(pos, half, low):
                    pe.wait_ge(w_ready, pos + (base + 1))
                    for hf in range(2):
                        up(pos, low, hf)
                        if low > 0:
                            down(pos, 1 - low % 2, hf, 1)

                pe.wait_ge(y_cleared, f + 1)
                walk(pe, f, tile)
                for hf in range(2):
                    down(total - 1, (total - 1) % 2, hf, 0)

            transpose_input(1)
            pe.wait_ge(h_full, 8)
            pe.wait_ge(gate_loaded, 16)
            router(wgate, E0)
            pe.wait_ge(sel_ready, 1)
            for t in range(NT):
                for s in range(t + 1):
                    ins = nc.tensor.matmul(ps[:, 3, t * E0:(t + 1) * E0], (before_b if s == t else ones_b)[:],
                                           sel_b[:, s, :], start=(s == 0), stop=(s == t), skip_group_check=True)
            ins.then_inc(counted, 1)
            transpose_combine(0, E0)
            pe.wait_ge(h_lo, 8)
            ffn(0)

            transpose_input(2)
            pe.wait_ge(h_full, 12)
            pe.wait_ge(ssm_loaded, 64)
            pe.wait_ge(sublayer_added, 1)
            for hf in range(2):
                for kc in range(KC):
                    ins = nc.tensor.matmul(ps[:, hf, :], bT[:, kc, :], hT_b[:, kc, hf * 512:hf * 512 + 512],
                                           start=(kc == 0), stop=(kc == KC - 1))
                ins.then_inc(u_done, 1)
            pe.wait_ge(h_hi, 12)
            for hf in range(2):
                pe.wait_ge(scanned, hf + 1)
                for mc in range(KC):
                    nc.tensor.matmul(ps[:, 4 + 2 * hf + mc, :], cT[:, mc * P:(mc + 1) * P],
                                     hs[:, hf * 512:hf * 512 + 512], start=True, stop=True).then_inc(hc_done, 1)
            for t in range(NT):
                if t % 4 == 0:
                    pe.wait_ge(z_ready, 2 * (t // 4) + 2)
                for mc in range(KC):
                    ins = nc.tensor.transpose(ps[:, t // 2, (t % 2) * D + mc * P:(t % 2) * D + (mc + 1) * P],
                                              zT[:, mc, t * P:(t + 1) * P], ident[:])
                ins.then_inc(z_transposed, 1)

            transpose_input(3)
            pe.wait_ge(h_full, 16)
            pe.wait_ge(gate_loaded, 32)
            router(wgate1, E1)
            transpose_combine(1, E1)
            pe.wait_ge(h_lo, 16)
            ffn(1)


def kernel(L0_attn_x, L0_attn_Wq, L0_attn_Wk, L0_attn_Wv, L0_attn_Wo, L0_attn_q_scale, L0_attn_k_scale,
           L0_ffn_w_gate, L0_ffn_w_shared_up, L0_ffn_w_shared_down, L0_ffn_w_up, L0_ffn_w_down, L0_c, L0_wmod,
           L1_attn_log_A_diag, L1_attn_B_mat, L1_attn_C_mat, L1_attn_D_vec, L1_attn_ln_w, L1_attn_ln_b,
           L1_ffn_gate_weight, L1_ffn_gate_up_proj, L1_ffn_down_proj, L1_c, L1_wmod):
    import numpy as np
    import concourse.bacc as bacc
    from concourse.bass_utils import run_bass_kernel_spmd

    def a(v):
        return np.asarray(v)

    def k_on_partitions(w):
        return np.ascontiguousarray(w.reshape(KC, P, -1).transpose(1, 0, 2))

    w_attn, w_out = [], []
    for g in range(NG):
        rows = slice(g * HPG * HD, (g + 1) * HPG * HD)
        kv = slice(g * HD, (g + 1) * HD)
        cols = np.concatenate([a(L0_attn_Wq)[rows].T, a(L0_attn_Wk)[kv].T, a(L0_attn_Wv)[kv].T], axis=1)
        w_attn.append(k_on_partitions(cols))
        w_out.append(a(L0_attn_Wo)[:, rows].T.reshape(HPG, HD, D).transpose(1, 0, 2))

    def hidden_tile(gate, value, down):
        gv = np.stack([gate.reshape(KC, P, P), value.reshape(KC, P, P)], axis=1)
        return np.concatenate([gv.transpose(2, 0, 1, 3).reshape(P, 4 * P), down], axis=1)

    up = a(L0_ffn_w_shared_up)
    pad = np.zeros((D, P - HS), up.dtype)
    ffn0 = [hidden_tile(np.concatenate([up[:, HS:], pad], axis=1), np.concatenate([up[:, :HS], pad], axis=1),
                        np.concatenate([a(L0_ffn_w_shared_down), np.zeros((P - HS, D), up.dtype)], axis=0))]
    for i in range(IT0):
        e = a(L0_ffn_w_up)[EPT0 * i:EPT0 * (i + 1)].transpose(1, 0, 2)
        ffn0.append(hidden_tile(e[:, :, :H0].reshape(D, P), e[:, :, H0:].reshape(D, P),
                                a(L0_ffn_w_down)[EPT0 * i:EPT0 * (i + 1)].reshape(P, D)))
    ffn1 = []
    for e in range(E1):
        for q in range(H1 // P):
            rows = slice(q * P, (q + 1) * P)
            gate_up = a(L1_ffn_gate_up_proj)[e]
            ffn1.append(hidden_tile(gate_up[:H1][rows].T, gate_up[H1:][rows].T, a(L1_ffn_down_proj)[e][:, rows].T))

    n = np.arange(P)
    const = np.concatenate([np.eye(P), np.where(n[None, :] > n[:, None], MASKED, 0.0), n[:, None] < n[None, :],
                            np.broadcast_to(np.arange(E0), (P, E0))], axis=1).astype(np.float32)
    ins = {
        "x": a(L0_attn_x).reshape(T, D),
        "w_attn": np.stack(w_attn), "w_out": np.stack(w_out),
        "qk_scale": np.stack([a(L0_attn_q_scale), a(L0_attn_k_scale)], axis=1),
        "gate0": k_on_partitions(a(L0_ffn_w_gate)), "ffn0": np.stack(ffn0),
        "c": np.concatenate([a(L0_c).reshape(KC, P).T, a(L1_c).reshape(KC, P).T], axis=1),
        "wmod": np.stack([k_on_partitions(a(L0_wmod)), k_on_partitions(a(L1_wmod))], axis=1),
        "const": const,
        "ssm_vec": np.concatenate([a(L1_attn_log_A_diag)[:, None], a(L1_attn_D_vec).reshape(KC, P).T], axis=1),
        "bmat": k_on_partitions(a(L1_attn_B_mat).T), "cmat": a(L1_attn_C_mat).T,
        "lnwb": np.stack([a(L1_attn_ln_w), a(L1_attn_ln_b)]),
        "gate1": k_on_partitions(a(L1_ffn_gate_weight).T), "ffn1": np.stack(ffn1),
    }
    ins = {k: np.ascontiguousarray(v) for k, v in ins.items()}
    nc = bacc.Bacc("TRN2", target_bir_lowering=False, num_devices=1)
    aps = [nc.dram_tensor("in_" + k, v.shape, F32, kind="ExternalInput").ap() for k, v in ins.items()]
    out = nc.dram_tensor("out", (T, D), F32, kind="ExternalOutput").ap()
    wt0 = nc.dram_tensor("combine0", (E0, T), F32, kind="Internal").ap()
    wt1 = nc.dram_tensor("combine1", (E1, 4, T), F32, kind="Internal").ap()
    program(nc, *aps, out, wt0, wt1)
    r = run_bass_kernel_spmd(nc, [{"in_" + k: v for k, v in ins.items()}], core_ids=[0])
    return r.results[0]["out"].reshape(1, T, D)
```

```python
import concourse.bass as bass
from concourse import mybir
from contextlib import ExitStack

F32 = mybir.dt.float32
F32R = mybir.dt.float32r
BF16 = mybir.dt.bfloat16
I32 = mybir.dt.int32
U32 = mybir.dt.uint32
ALU = mybir.AluOpType
ACT = mybir.ActivationFunctionType
AX = mybir.AxisListType

P = 128
T, D = 1024, 256
NT = T // P
KC = D // P
NG, HPG, HD = 4, 4, 128
E0, H0, TOPK0, CAP = 64, 32, 6, 128
HS = 64
E1, H1, TOPK1 = 8, 512, 2
EPT0 = P // H0
IT0 = E0 // EPT0
IT1 = E1 * H1 // P
NSTATE = 128
QKV = HPG * HD + 2 * HD
MASKED = -1e30
EPS_Q = 1e-6
EPS_LN = 1e-5
RSQRT_SEED = float(0x5F3759DF)
NEWTON = 3

STEPS = 2 * HPG * 4
TLAG = 2
PVLAG = 6
RLAG = 7
OLAG = 9
WOLAG = 12
PIECES = [[[0], [1], [2, 3]], [[0, 1, 2, 3], [4, 5], [6, 7]]]
NP = 3
NB = 3


def step_of(n):
    m, qi = divmod(n, 4)
    return m, m // HPG, m % HPG, qi


def blocks(n):
    m, c, h, qi = step_of(n)
    return 4 * c + qi + 1


def transposed_groups(n):
    k = blocks(n)
    return [(u, 4 * u, min(4, k - 4 * u)) for u in range((k + 3) // 4)]


TG_BEFORE = [0]
for _n in range(STEPS):
    TG_BEFORE.append(TG_BEFORE[-1] + len(transposed_groups(_n)))
TGS = TG_BEFORE[-1]


def unit_base(m):
    return m if m < HPG else HPG + 2 * (m - HPG)


def pieces_until_free(unit):
    if unit < HPG:
        return NP * unit + NP
    m, second = divmod(unit - HPG, 2)
    return NP * (m + HPG) + (NP if second else 1)


def head_at(n, lag):
    m, r = divmod(n - lag, 4)
    return m if r == 0 and 0 <= m < 2 * HPG else None


def banks_of_transposes():
    order, at = [], {}
    for n in range(STEPS + WOLAG - 3):
        if 0 <= n - TLAG < STEPS:
            for u, j0, nb in transposed_groups(n - TLAG):
                at.setdefault(n, []).append((("p", TG_BEFORE[n - TLAG] + u, u, j0, nb), len(order)))
                order.append(("p", TG_BEFORE[n - TLAG] + u))
        m = head_at(n, RLAG)
        if m is not None:
            at.setdefault(n, []).append((("r", m), len(order)))
            order.append(("r", m))
        c, r = divmod(n - 12 - WOLAG, 16)
        if r == 0 and c >= 0:
            for half in range(2):
                at.setdefault(n, []).append((("y", 2 * c + half), len(order)))
                order.append(("y", 2 * c + half))
    return order, at


BANK_ORDER, BANK_AT = banks_of_transposes()
NUNITS = 3


def program(nc, x_d, w_attn_d, w_out_d, qk_scale_d, gate0_d, ffn0_d, c_d, wmod_d, const_d,
            ssm_vec_d, bmat_d, cmat_d, lnwb_d, gate1_d, ffn1_d, out_d, wt0_d, wt1_d):
    ctx = ExitStack()

    def sem(name):
        return ctx.enter_context(nc.semaphore(name))

    def keep(name, shape, dt=F32):
        return ctx.enter_context(nc.sbuf_tensor(name, shape, dt))

    with ctx:
        x = keep("x", [P, NT, D])
        hT_hi = keep("hT_hi", [P, KC, T], F32R)
        hT_lo = keep("hT_lo", [P, KC, T], F32R)
        ident = keep("ident", [P, P])
        mask_b = keep("mask_b", [P, P], BF16)
        ident_b = keep("ident_b", [P, P], BF16)
        before_b = keep("before_b", [P, P], BF16)
        ones_b = keep("ones_b", [P, P], BF16)
        iota = keep("iota", [P, E0])
        modc = keep("modc", [P, 2, 12])
        opc = keep("opc", [P, 2, 12])
        gates = keep("gates", [P, 4, D])
        one = keep("one", [P, 1])
        ccol = keep("ccol", [P, 4])
        cth = keep("cth", [P, 4])
        csil = keep("csil", [P, 4])
        qks = keep("qks", [P, 2])
        stat = keep("stat", [P, NT, 6])
        mv = keep("mv", [P, NT, 2])
        rs_in = keep("rs_in", [P, NT * 5])
        rs_y = keep("rs_y", [P, NT * 5])
        rs_t = keep("rs_t", [P, NT * 5])
        wqkv_raw = keep("wqkv_raw", [P, KC, QKV])
        wqkv_hi = keep("wqkv_hi", [P, KC, QKV], F32R)
        wqkv_lo = keep("wqkv_lo", [P, KC, QKV], F32R)
        wo_raw = keep("wo_raw", [P, HPG, D])
        wo_hi = keep("wo_hi", [P, HPG, D], F32R)
        wo_lo = keep("wo_lo", [P, HPG, D], F32R)

        def stage(*specs):
            with ExitStack() as s:
                return [s.enter_context(nc.sbuf_tensor(name, shape, dt)) for name, shape, dt in specs]

        hT_a, xn_a, wmod, csb, const, gmag, gsgn, grow = stage(
            ("hT_a", [P, KC, T], F32), ("xn_a", [P, NT, D], F32),
            ("wmod", [P, 2, KC, 6 * D], F32), ("csb", [P, 4, P], F32), ("const", [P, 3 * P + E0], F32),
            ("gmag", [P, 4, D], F32), ("gsgn", [P, 4, D], F32), ("grow", [P, 4, D], F32))
        (qT_hi, qT_lo, kT_hi, kT_lo, v_hi, v_lo, prob, pT_hi, pT_lo, oT_hi, oT_lo, q_f, k_f, sq, sqk,
         r_sb, o_f, mx, negb, rsum, rinv, rqs, rk_in) = stage(
            ("qT_hi", [P, HPG, T], F32R), ("qT_lo", [P, HPG, T], F32R),
            ("kT_hi", [P, T], F32R), ("kT_lo", [P, T], F32R),
            ("v_hi", [P, NT, HD], F32R), ("v_lo", [P, NT, HD], F32R),
            ("prob", [P, 3, T], F32),
            ("pT_hi", [P, NUNITS, 4, 512], F32R), ("pT_lo", [P, NUNITS, 4, 512], F32R),
            ("oT_hi", [P, HPG, 512], F32R), ("oT_lo", [P, HPG, 512], F32R),
            ("q_f", [P, 2, HPG * HD], F32), ("k_f", [P, NT, HD], F32),
            ("sq", [P, HPG * HD], F32), ("sqk", [P, HD], F32), ("r_sb", [P, 2, 512], F32), ("o_f", [P, 512], F32),
            ("mx", [P, 2], F32), ("negb", [P, 2], F32), ("rsum", [P, 2, 4], F32), ("rinv", [P, 2, 4], F32),
            ("rqs", [P, NT, HPG], F32), ("rk_in", [P, NT], F32))
        ytmp = k_f[:].rearrange("p (r a) d -> p r (a d)", a=2)
        (hT_b, xn_b, w_raw, w_hi, w_lo, wbc, th, fa, fb, fc, hid_hi, hid_lo, wgate, wgate1, key, sig, sel, eq,
         ws, wc, sel_b, top, topi, topf, wT, rsm, bT, cT, hs, zT, lnwb, svec, a_t, a_disc, opd, ffy) = stage(
            ("hT_b", [P, KC, T], F32), ("xn_b", [P, NT, D], F32),
            ("w_raw", [P, NB, 6 * P], F32), ("w_hi", [P, NB, 6 * P], F32R), ("w_lo", [P, NB, 6 * P], F32R),
            ("wbc", [P, NB, T], F32), ("th", [P, 2, 512], F32), ("fa", [P, 2, 512], F32),
            ("fb", [P, 2, 512], F32), ("fc", [P, 2, 512], F32),
            ("hid_hi", [P, 2, 512], F32R), ("hid_lo", [P, 2, 512], F32R),
            ("wgate", [P, KC, E0], F32), ("wgate1", [P, KC, E1], F32),
            ("key", [P, NT, E0], F32), ("sig", [P, NT, E0], F32), ("sel", [P, NT, E0], F32),
            ("eq", [P, NT, E0], F32), ("ws", [P, NT, E0], F32), ("wc", [P, NT, E0], F32),
            ("sel_b", [P, NT, E0], BF16), ("top", [P, NT, 8], F32), ("topi", [P, NT, 8], U32),
            ("topf", [P, NT, 8], F32), ("wT", [E0, T], F32), ("rsm", [P, 4, NT], F32),
            ("bT", [P, KC, NSTATE], F32), ("cT", [P, D], F32), ("hs", [P, T], F32),
            ("zT", [P, KC, T], F32), ("lnwb", [P, 2, D], F32), ("svec", [P, 1 + KC], F32),
            ("a_t", [P, 1], F32), ("a_disc", [P, 1], F32), ("opd", [P, KC], F32), ("ffy", [P, NT, D], F32))
        hT_of = [hT_a, hT_b, hT_b, hT_b]
        xn_of = [xn_a, xn_b, xn_b, xn_b]
        ps = ctx.enter_context(nc.psum_tensor("ps", [P, 8, 512], F32))

        (setup_loaded, x_loaded, consts_ready, c_tanh, c_ready, mod_done, mod_ready, vec_step, ln_normed,
         ln_transposed, h_full, h_hi, h_lo, wqkv_raw_in, wqkv_high, wqkv_ready, wo_raw_in, wo_high, wo_ready,
         projected, q_copied, kv_copied, squares, square_sums, v_split, q_transposed, qT_hi_done, qT_lo_done,
         qk_norm_step, k_normed, k_transposed, kT_hi_done, kT_lo_done, scored, row_max, bias_ready, exp_done,
         row_inv, prob_ready, p_transposed, pT_hi_done, pT_lo_done, pv_done, oT_hi_done, oT_lo_done, wo_done,
         y_scaled, y_added, kv_projected, key_sums, keys_copied, q_sums, r_spread, r_copied, o_normed) = [sem(n) for n in (
            "setup_loaded x_loaded consts_ready c_tanh c_ready mod_done mod_ready vec_step ln_normed "
            "ln_transposed h_full h_hi h_lo wqkv_raw_in wqkv_high wqkv_ready wo_raw_in wo_high wo_ready "
            "projected q_copied kv_copied squares square_sums v_split q_transposed qT_hi_done qT_lo_done "
            "qk_norm_step k_normed k_transposed kT_hi_done kT_lo_done scored row_max bias_ready exp_done "
            "row_inv prob_ready p_transposed pT_hi_done pT_lo_done pv_done oT_hi_done oT_lo_done wo_done "
            "y_scaled y_added kv_projected key_sums keys_copied q_sums r_spread r_copied o_normed").split()]
        (gate_loaded, logits_done, logits_exp, shifted, sel_ready, counted, wc_ready,
         wc_transposed, wT_ready, wT_stored, y_cleared, w_ready, up_done, tanh_done, silu_done, gated, weighted,
         hid_hi_done, hid_lo_done, down_done, ssm_loaded, a_step, u_done, scanned, hc_done, z_ready,
         z_transposed, sublayer_added, stored) = [sem(n) for n in (
            "gate_loaded logits_done logits_exp shifted sel_ready counted wc_ready "
            "wc_transposed wT_ready wT_stored y_cleared w_ready up_done tanh_done silu_done gated weighted "
            "hid_hi_done hid_lo_done down_done ssm_loaded a_step u_done scanned hc_done z_ready "
            "z_transposed sublayer_added stored").split()]
        w_raw_in = [sem(f"w_raw_in{b}") for b in range(NB)]
        wbc_in = [sem(f"wbc_in{b}") for b in range(NB)]
        w_high = sem("w_high")
        one_ready = sem("one_ready")

        def loads_before(first, total):
            return tuple(len(range(b, total, NB)) - (1 if b < first else 0) for b in range(NB))

        FF = [dict(total=1 + IT0, peel=1 + NB + (IT0 - NB) % NB, base=0, wused=(0,) * NB, cused=(-1,) + (0,) * (NB - 1)),
              dict(total=IT1, peel=IT1 % NB, base=1 + IT0, wused=loads_before(0, 1 + IT0),
                   cused=loads_before(1, 1 + IT0))]

        def walk(eng, f, body, start=0):
            peel = FF[f]["peel"]
            for pos in range(start, peel):
                body(pos, pos // NB, pos)
            with eng.Fori(0, (FF[f]["total"] - peel) // NB) as j:
                for u in range(NB):
                    body(j * NB + (peel + u), j + (peel + u) // NB, peel + u)

        block = ctx.enter_context(nc.Block())

        @block.sync
        def _(sp):
            sp.dma_start(ccol[:], c_d).then_inc(setup_loaded, 16)
            sp.dma_start(wmod[:], wmod_d).then_inc(setup_loaded, 16)
            sp.dma_start(const[:], const_d).then_inc(setup_loaded, 16)
            sp.dma_start(qks[:], qk_scale_d).then_inc(setup_loaded, 16)
            sp.dma_start(wqkv_raw[:], w_attn_d[0]).then_inc(wqkv_raw_in, 16)
            sp.dma_start(wo_raw[:], w_out_d[0]).then_inc(wo_raw_in, 16)
            with sp.Fori(0, NG - 1) as g:
                sp.wait_ge(projected, g * NT + NT)
                sp.dma_start(wqkv_raw[:], w_attn_d[g + 1]).then_inc(wqkv_raw_in, 16)
                sp.wait_ge(wo_done, g * 4 + 4)
                sp.dma_start(wo_raw[:], w_out_d[g + 1]).then_inc(wo_raw_in, 16)

            def load_weights(f, src, pos, low):
                if FF[f]["base"] + low >= NB:
                    sp.wait_ge(w_ready, pos + (FF[f]["base"] - NB + 1))
                sp.dma_start(w_raw[:, low % NB, :], src[pos]).then_inc(w_raw_in[low % NB], 16)

            def load_combine(f, row, pos, low):
                if FF[f]["base"] + low >= NB:
                    sp.wait_ge(weighted, pos * 2 + 2 * (FF[f]["base"] - NB + 1))
                sp.dma_start(wbc[:, low % NB, :], row).then_inc(wbc_in[low % NB], 16)

            sp.wait_ge(y_added, 4 * NG)
            sp.dma_start(wgate[:], gate0_d).then_inc(gate_loaded, 16)
            for pos in range(NB):
                load_weights(0, ffn0_d, pos, pos)
            sp.wait_ge(wT_ready, 1)
            sp.dma_start(wt0_d, wT[0:E0, :]).then_inc(wT_stored, 16)
            sp.wait_ge(wT_stored, 16)
            rows0 = wt0_d.rearrange("(i e) t -> i e t", e=EPT0)

            def tile0(pos, turn, low):
                if low >= NB:
                    load_weights(0, ffn0_d, pos, low)
                load_combine(0, rows0[pos - 1].unsqueeze(1).to_broadcast([EPT0, H0, T]), pos, low)
            walk(sp, 0, tile0, start=1)

            sp.wait_ge(sublayer_added, 1)
            sp.dma_start(svec[:], ssm_vec_d).then_inc(ssm_loaded, 16)
            sp.dma_start(bT[:], bmat_d).then_inc(ssm_loaded, 16)
            sp.dma_start(cT[:], cmat_d).then_inc(ssm_loaded, 16)
            sp.dma_start(lnwb[:], lnwb_d.unsqueeze(0).to_broadcast([P, 2, D])).then_inc(ssm_loaded, 16)
            sp.dma_start(wgate1[:], gate1_d).then_inc(gate_loaded, 16)

            for pos in range(FF[1]["peel"]):
                load_weights(1, ffn1_d, pos, pos)
            sp.wait_ge(wT_ready, 2)
            for r in range(4):
                sp.dma_start(wt1_d[:, r, :], wT[0:E1, :]).then_inc(wT_stored, 16)
            sp.wait_ge(wT_stored, 16 * 5)
            rows1 = wt1_d.rearrange("e r t -> (e r) t")

            def tile1(pos, turn, low):
                if low >= FF[1]["peel"]:
                    load_weights(1, ffn1_d, pos, low)
                load_combine(1, rows1[pos].unsqueeze(0).to_broadcast([P, T]), pos, low)
            walk(sp, 1, tile1)

            sp.wait_ge(sublayer_added, 3)
            sp.dma_start(out_d.rearrange("(t p) d -> p t d", p=P), x[:]).then_inc(stored, 16)
            sp.wait_ge(stored, 16)

        @block.gpsimd
        def _(pool):
            nc.gpsimd.memset(one[:], 1.0).then_inc(one_ready, 1)
            pool.wait_ge(one_ready, 1)

            def split(raw, hi, lo, raw_in, value, high, high_value, ready):
                pool.wait_ge(raw_in, value)
                nc.gpsimd.tensor_tensor(hi, raw, one[:].to_broadcast(list(raw.shape)) if len(raw.shape) == 2 else
                                        one[:].unsqueeze(2).to_broadcast(list(raw.shape)),
                                        ALU.mult).then_inc(high, 1)
                pool.wait_ge(high, high_value)
                nc.gpsimd.tensor_tensor(lo, raw, hi, ALU.subtract).then_inc(ready, 1)

            pool.wait_ge(wqkv_high, 1)
            nc.gpsimd.tensor_tensor(wqkv_lo[:], wqkv_raw[:], wqkv_hi[:], ALU.subtract).then_inc(wqkv_ready, 1)
            split(wo_raw[:], wo_hi[:], wo_lo[:], wo_raw_in, 16, wo_high, 1, wo_ready)

            def outputs_low(g):
                for m in range(2 * HPG):
                    pool.wait_ge(oT_hi_done, g * 2 * HPG + (m + 1))
                    nc.gpsimd.tensor_tensor(oT_lo[:, m % HPG, :], o_f[:], oT_hi[:, m % HPG, :],
                                            ALU.subtract).then_inc(oT_lo_done, 1)

            with pool.Fori(0, NG - 1) as g:
                pool.wait_ge(projected, g * NT + NT)
                split(wqkv_raw[:], wqkv_hi[:], wqkv_lo[:], wqkv_raw_in, g * 16 + 32, wqkv_high, g + 2, wqkv_ready)
                outputs_low(g)
                pool.wait_ge(wo_done, g * 4 + 4)
                split(wo_raw[:], wo_hi[:], wo_lo[:], wo_raw_in, g * 16 + 32, wo_high, g + 2, wo_ready)

            def ffn_weights(f):
                base, wused = FF[f]["base"], FF[f]["wused"]

                def tile(pos, turn, low):
                    b = low % NB
                    if base + low >= NB:
                        pool.wait_ge(down_done, pos * 2 + 2 * (base - NB + 1))
                    split(w_raw[:, b, :], w_hi[:, b, :], w_lo[:, b, :], w_raw_in[b],
                          turn * 16 + 16 * (wused[b] + 1), w_high, pos + (base + 1), w_ready)
                walk(pool, f, tile)

            outputs_low(NG - 1)
            pool.wait_ge(y_added, 4 * NG)
            ffn_weights(0)
            pool.wait_ge(sublayer_added, 1)
            ffn_weights(1)

        @block.scalar
        def _(act):
            act.dma_start(x[:], x_d.rearrange("(t p) d -> p t d", p=P)).then_inc(x_loaded, 16)
            act.wait_ge(setup_loaded, 64)
            nc.scalar.activation(cth[:], ccol[:], ACT.Tanh, scale=0.5).then_inc(c_tanh, 1)

            def modulate(n, layer, kind):
                hT = hT_of[n]
                if n == 0:
                    act.wait_ge(mod_ready, 1)
                for hf in range(2):
                    for kc in range(KC):
                        b = 2 * hf + kc
                        act.wait_ge(ln_transposed, 4 * n + b + 1)
                        cols = hT[:, kc, hf * 512:hf * 512 + 512]
                        nc.scalar.activation(cols, ps[:, 4 + b, :], ACT.Identity,
                                             bias=modc[:, layer, 2 * kind + kc:2 * kind + kc + 1],
                                             scale=opc[:, layer, 2 * kind + 2 + kc:2 * kind + 3 + kc]
                                             ).then_inc(h_full, 1)
                        act.wait_ge(h_full, 4 * n + b + 1)
                        nc.scalar.activation(hT_hi[:, kc, hf * 512:hf * 512 + 512], cols,
                                             ACT.Copy).then_inc(h_hi, 1)

            act.wait_ge(wqkv_raw_in, 16)
            nc.scalar.activation(wqkv_hi[:], wqkv_raw[:], ACT.Copy).then_inc(wqkv_high, 1)
            modulate(0, 0, 0)

            with act.Fori(0, NG) as g:
                for t in range(NT):
                    act.wait_ge(kv_projected, g * NT + (t + 1))
                    nc.scalar.activation(sqk[:], ps[:, t % 4, 0:HD], ACT.Square,
                                         accum_out=rk_in[:, t:t + 1]).then_inc(key_sums, 1)
                    nc.scalar.activation(v_hi[:, t, :], ps[:, t % 4, HD:2 * HD], ACT.Copy).then_inc(v_split, 1)
                    act.wait_ge(key_sums, g * NT + (t + 1))

                def q_high(t):
                    act.wait_ge(q_transposed, g * NT + (t + 1))
                    nc.scalar.activation(qT_hi[:, :, t * P:(t + 1) * P],
                                         ps[:, 4 + t % 2, :].rearrange("p (h t) -> p h t", h=HPG),
                                         ACT.Copy, scale=qks[:, 0:1]).then_inc(qT_hi_done, 1)

                for t in range(NT):
                    act.wait_ge(projected, g * NT + (t + 1))
                    if t >= 1:
                        act.wait_ge(square_sums, g * NT + t)
                    nc.scalar.activation(sq[:], ps[:, t % 2, :], ACT.Square).then_inc(squares, 1)
                    if t >= 2:
                        act.wait_ge(q_transposed, g * NT + (t - 1))
                    nc.scalar.activation(q_f[:, t % 2, :], ps[:, t % 2, :], ACT.Copy).then_inc(q_copied, 1)
                    if t >= 1:
                        q_high(t - 1)
                    if t >= NT - 2:
                        b = t - (NT - 2)
                        act.wait_ge(k_transposed, g * 2 + (b + 1))
                        nc.scalar.activation(kT_hi[:, b * 512:(b + 1) * 512], ps[:, 2 + b, :], ACT.Copy,
                                             scale=qks[:, 1:2]).then_inc(kT_hi_done, 1)
                q_high(NT - 1)

                for n in range(STEPS + WOLAG - 3):
                    for what, place in BANK_AT.get(n, []):
                        if what[0] == "p":
                            _, q, u, j0, nb = what
                            m, c, h, qi = step_of(n - TLAG)
                            unit = unit_base(m) + u
                            act.wait_ge(p_transposed, g * TGS + (q + 1))
                            if unit >= NUNITS:
                                act.wait_ge(pv_done, g * 2 * HPG * NP + pieces_until_free(unit - NUNITS))
                            nc.scalar.activation(pT_hi[:, unit % NUNITS, 0:nb, qi * P:(qi + 1) * P],
                                                 ps[:, 4 + place % 2, 0:nb * P].rearrange("p (j t) -> p j t", j=nb),
                                                 ACT.Copy).then_inc(pT_hi_done, 1)
                        elif what[0] == "r":
                            m = what[1]
                            act.wait_ge(r_spread, g * 2 * HPG + (m + 1))
                            if m >= 2:
                                act.wait_ge(o_normed, g * 2 * HPG + (m - 1))
                            nc.scalar.activation(r_sb[:, m % 2, :], ps[:, 4 + place % 2, :],
                                                 ACT.Copy).then_inc(r_copied, 1)
                    m = head_at(n, OLAG)
                    if m is not None:
                        act.wait_ge(o_normed, g * 2 * HPG + (m + 1))
                        if m >= HPG:
                            act.wait_ge(wo_done, g * 4 + 2)
                        nc.scalar.activation(oT_hi[:, m % HPG, :], o_f[:], ACT.Copy).then_inc(oT_hi_done, 1)
                    if n < STEPS:
                        m, c, h, qi = step_of(n)
                        w = blocks(n) * P
                        pair = 2 * (n % 2)
                        act.wait_ge(bias_ready, g * STEPS + (n + 1))
                        if n >= 3:
                            act.wait_ge(p_transposed, g * TGS + TG_BEFORE[n - 2])
                        if c == 0:
                            src, dst = ps[:, pair, 0:w], prob[:, n % 3, 0:w]
                        else:
                            src = ps[:, pair:pair + 2, 0:w // 2]
                            dst = prob[:, n % 3, 0:w].rearrange("p (a w) -> p a w", a=2)
                        nc.scalar.activation(dst, src, ACT.Exp, bias=negb[:, n % 2:n % 2 + 1],
                                             scale=rqs[:, 4 * c + qi, h:h + 1],
                                             accum_out=rsum[:, m % 2, qi:qi + 1]).then_inc(exp_done, 1)

            def ffn(f, after_first=None):
                base, total = FF[f]["base"], FF[f]["total"]

                def high(pos, low, hf, back):
                    act.wait_ge(weighted, pos * 2 + (2 * (base - back) + hf + 1))
                    if 2 * (base + low - back) + hf - 1 > 0:
                        act.wait_ge(down_done, pos * 2 + (2 * (base - back) + hf - 1))
                    nc.scalar.activation(hid_hi[:, hf, :], fc[:, hf, :], ACT.Copy).then_inc(hid_hi_done, 1)

                def tile(pos, turn, low):
                    for hf in range(2):
                        act.wait_ge(up_done, pos * 2 + (2 * base + hf + 1))
                        if 2 * (base + low) + hf - 1 > 0:
                            act.wait_ge(silu_done, pos * 2 + (2 * base + hf - 1))
                        nc.scalar.activation(th[:, hf, :], ps[:, 4 + 2 * hf, :], ACT.Tanh,
                                             scale=0.5).then_inc(tanh_done, 1)
                        if hf == 1:
                            high(pos, low, 0, 0)
                        elif low > 0:
                            high(pos, low, 1, 1)
                walk(act, f, tile)
                high(total - 1, total - 1, 1, 0)

            modulate(1, 0, 3)
            act.wait_ge(logits_done, 1)
            nc.scalar.activation(sig[:], ps[:, 0, :].rearrange("p (t e) -> p t e", t=NT), ACT.Exp,
                                 scale=-1.0).then_inc(logits_exp, 1)
            ffn(0)

            modulate(2, 1, 0)
            act.wait_ge(ssm_loaded, 64)
            nc.scalar.activation(a_t[:], svec[:, 0:1], ACT.Exp).then_inc(a_step, 1)
            act.wait_ge(a_step, 1)
            nc.scalar.activation(a_disc[:], a_t[:], ACT.Exp, scale=-1.0).then_inc(a_step, 1)

            modulate(3, 1, 3)
            act.wait_ge(shifted, 1)
            nc.scalar.activation(key[:, :, 0:E1], sig[:, :, 0:E1], ACT.Exp).then_inc(logits_exp, 1)
            ffn(1)

        @block.vector
        def _(dve):
            steps = [0]

            def link(ins):
                steps[0] += 1
                ins.then_inc(vec_step, 1)
                dve.wait_ge(vec_step, steps[0])

            def inverse_root(width, link_):
                v, y, t = rs_in[:, 0:width], rs_y[:, 0:width], rs_t[:, 0:width]
                link_(nc.vector.tensor_scalar(y.bitcast(I32), v.bitcast(I32), -0.5, RSQRT_SEED, ALU.mult, ALU.add))
                for _ in range(NEWTON):
                    link_(nc.vector.tensor_tensor(t, y, y, ALU.mult))
                    link_(nc.vector.scalar_tensor_tensor(t, t, -0.5, v, ALU.mult, ALU.mult))
                    link_(nc.vector.scalar_tensor_tensor(y, t, 1.5, y, ALU.add, ALU.mult))

            def normalise(src, dst, done):
                for t in range(NT):
                    ins = nc.vector.bn_stats(stat[:, t, :], src(t))
                link(ins)
                for t in range(NT):
                    ins = nc.vector.bn_aggr(mv[:, t, :], stat[:, t, :])
                link(ins)
                link(nc.vector.tensor_scalar(rs_in[:, 0:NT], mv[:, :, 1], EPS_LN, None, ALU.add))
                inverse_root(NT, link)
                for t in range(NT):
                    nc.vector.tensor_scalar(dst[:, t, :], src(t), mv[:, t, 0:1], rs_y[:, t:t + 1],
                                            ALU.subtract, ALU.mult).then_inc(done, 1)

            def split_input(n):
                hT = hT_of[n]
                for hf in range(2):
                    for kc in range(KC):
                        dve.wait_ge(h_hi, 4 * n + 2 * hf + kc + 1)
                        s = slice(hf * 512, hf * 512 + 512)
                        nc.vector.tensor_tensor(hT_lo[:, kc, s], hT[:, kc, s], hT_hi[:, kc, s],
                                                ALU.subtract).then_inc(h_lo, 1)

            dve.wait_ge(setup_loaded, 64)
            nc.vector.tensor_copy(ident[:], const[:, 0:P])
            nc.vector.tensor_copy(ident_b[:], const[:, 0:P])
            nc.vector.tensor_copy(mask_b[:], const[:, P:2 * P])
            nc.vector.tensor_copy(before_b[:], const[:, 2 * P:3 * P])
            nc.vector.memset(ones_b[:], 1.0)
            nc.vector.tensor_copy(iota[:], const[:, 3 * P:]).then_inc(consts_ready, 1)
            dve.wait_ge(c_tanh, 1)
            link(nc.vector.scalar_tensor_tensor(csil[:], cth[:], 1.0, ccol[:], ALU.add, ALU.mult))
            link(nc.vector.tensor_scalar(csil[:], csil[:], 0.5, None, ALU.mult))
            nc.vector.tensor_copy(csb[:], csil[:].unsqueeze(2).to_broadcast([P, 4, P])).then_inc(c_ready, 1)
            dve.wait_ge(x_loaded, 16)
            normalise(lambda t: x[:, t, :], xn_of[0], ln_normed)
            dve.wait_ge(mod_done, 1)
            nc.vector.tensor_copy(modc[:], ps[:, 0, 0:24].rearrange("p (l j) -> p l j", l=2))
            nc.vector.tensor_scalar(opc[:], ps[:, 0, 0:24].rearrange("p (l j) -> p l j", l=2), 1.0, None,
                                    ALU.add).then_inc(mod_ready, 1)
            dve.wait_ge(mod_done, 2)
            link(nc.vector.tensor_copy(grow[:], ps[:, 1:3, :].rearrange("p b (r d) -> p (b r) d", r=2)))
            link(nc.vector.tensor_scalar(gsgn[:], grow[:], 0.0, 2.0, ALU.is_ge, ALU.mult))
            link(nc.vector.tensor_scalar(gsgn[:], gsgn[:], -1.0, None, ALU.add))
            link(nc.vector.scalar_tensor_tensor(gmag[:], grow[:], -1.0, grow[:], ALU.mult, ALU.max))
            link(nc.vector.scalar_tensor_tensor(gates[:], gmag[:], 0.25, gsgn[:], ALU.max, ALU.mult))
            split_input(0)

            NORM_STEPS = 2 * (2 + 3 * NEWTON) + 1
            with dve.Fori(0, NG) as g:
                norm_steps = [0]

                def norm_link(ins):
                    norm_steps[0] += 1
                    ins.then_inc(qk_norm_step, 1)
                    dve.wait_ge(qk_norm_step, g * NORM_STEPS + norm_steps[0])

                for t in range(NT):
                    dve.wait_ge(v_split, g * NT + (t + 1))
                    nc.vector.tensor_copy(k_f[:, t, :], ps[:, t % 4, 0:HD]).then_inc(keys_copied, 1)
                    nc.vector.tensor_tensor(v_lo[:, t, :], ps[:, t % 4, HD:2 * HD], v_hi[:, t, :],
                                            ALU.subtract).then_inc(kv_copied, 1)
                dve.wait_ge(key_sums, g * NT + NT)
                norm_link(nc.vector.tensor_scalar(rs_in[:, 0:NT], rk_in[:], 1.0 / HD, EPS_Q, ALU.mult, ALU.add))
                inverse_root(NT, norm_link)
                dve.wait_ge(keys_copied, g * NT + NT)
                for t in range(NT):
                    nc.vector.tensor_scalar(k_f[:, t, :], k_f[:, t, :], rs_y[:, t:t + 1], None,
                                            ALU.mult).then_inc(k_normed, 1)

                def q_low(t):
                    dve.wait_ge(qT_hi_done, g * NT + (t + 1))
                    nc.vector.scalar_tensor_tensor(
                        qT_lo[:, :, t * P:(t + 1) * P], ps[:, 4 + t % 2, :].rearrange("p (h t) -> p h t", h=HPG),
                        qks[:, 0:1], qT_hi[:, :, t * P:(t + 1) * P], ALU.mult, ALU.subtract).then_inc(qT_lo_done, 1)

                dve.wait_ge(k_normed, g * NT + NT)
                for t in range(NT):
                    dve.wait_ge(squares, g * NT + (t + 1))
                    nc.vector.reduce_sum(rs_in[:, HPG * t:HPG * t + HPG], sq[:].rearrange("p (h d) -> p h d", d=HD),
                                         AX.X).then_inc(square_sums, 1)
                    if t >= 1:
                        q_low(t - 1)
                    if t >= NT - 2:
                        b = t - (NT - 2)
                        dve.wait_ge(kT_hi_done, g * 2 + (b + 1))
                        s = slice(b * 512, (b + 1) * 512)
                        nc.vector.scalar_tensor_tensor(kT_lo[:, s], ps[:, 2 + b, :], qks[:, 1:2], kT_hi[:, s],
                                                       ALU.mult, ALU.subtract).then_inc(kT_lo_done, 1)
                q_low(NT - 1)
                dve.wait_ge(square_sums, g * NT + NT)
                w = HPG * NT
                norm_link(nc.vector.tensor_scalar(rs_in[:, 0:w], rs_in[:, 0:w], 1.0 / HD, EPS_Q,
                                                  ALU.mult, ALU.add))
                inverse_root(w, norm_link)
                norm_link(nc.vector.tensor_scalar(rqs[:].rearrange("p t h -> p (t h)"), rs_y[:, 0:w], HD ** -0.5,
                                                  None, ALU.mult))
                assert norm_steps[0] == NORM_STEPS

                for n in range(STEPS + WOLAG - 3):
                    if n < STEPS:
                        m, c, h, qi = step_of(n)
                        w = blocks(n) * P
                        pair = 2 * (n % 2)
                        i = n % 2
                        dve.wait_ge(scored, g * STEPS + (n + 1))
                        if c == 0:
                            nc.vector.reduce_max(mx[:, i:i + 1], ps[:, pair, 0:w], AX.X).then_inc(row_max, 1)
                        else:
                            nc.vector.reduce_max(mx[:, i:i + 1], ps[:, pair:pair + 2, 0:w // 2],
                                                 AX.XY).then_inc(row_max, 1)
                        dve.wait_ge(row_max, g * STEPS + (n + 1))
                        if n >= 2:
                            dve.wait_ge(exp_done, g * STEPS + (n - 1))
                        nc.vector.tensor_scalar(negb[:, i:i + 1], mx[:, i:i + 1], rqs[:, 4 * c + qi, h:h + 1], -1.0,
                                                ALU.mult, ALU.mult).then_inc(bias_ready, 1)
                    m = head_at(n, RLAG - 2)
                    if m is not None:
                        dve.wait_ge(exp_done, g * STEPS + (4 * m + 4))
                        if m >= 2:
                            dve.wait_ge(r_spread, g * 2 * HPG + (m - 1))
                        nc.vector.reciprocal(rinv[:, m % 2, :], rsum[:, m % 2, :]).then_inc(row_inv, 1)
                    m = head_at(n, OLAG)
                    if m is not None:
                        dve.wait_ge(pv_done, g * 2 * HPG * NP + NP * (m + 1))
                        dve.wait_ge(r_copied, g * 2 * HPG + (m + 1))
                        if m >= 1:
                            dve.wait_ge(oT_lo_done, g * 2 * HPG + m)
                        nc.vector.tensor_tensor(o_f[:], ps[:, 6 + m % 2, :], r_sb[:, m % 2, :],
                                                ALU.mult).then_inc(o_normed, 1)
                    for what, place in BANK_AT.get(n, []):
                        if what[0] == "p":
                            _, q, u, j0, nb = what
                            m, c, h, qi = step_of(n - TLAG)
                            unit = unit_base(m) + u
                            dve.wait_ge(pT_hi_done, g * TGS + (q + 1))
                            dst = (slice(None), unit % NUNITS, slice(0, nb), slice(qi * P, (qi + 1) * P))
                            nc.vector.tensor_tensor(pT_lo[dst],
                                                    ps[:, 4 + place % 2, 0:nb * P].rearrange("p (j t) -> p j t",
                                                                                             j=nb),
                                                    pT_hi[dst], ALU.subtract).then_inc(pT_lo_done, 1)
                        elif what[0] == "y":
                            y = what[1]
                            dve.wait_ge(wo_done, g * 4 + (y + 1))
                            nc.vector.tensor_tensor(ytmp[:, 2 * (y % 2):2 * (y % 2) + 2, :],
                                                    ps[:, 4 + place % 2, :].rearrange("p (r d) -> p r d", r=2),
                                                    gates[:, 0:1, :].to_broadcast([P, 2, D]),
                                                    ALU.mult).then_inc(y_scaled, 1)
                            dve.wait_ge(y_scaled, g * 4 + (y + 1))
                            nc.vector.tensor_tensor(x[:, 2 * y:2 * y + 2, :], x[:, 2 * y:2 * y + 2, :],
                                                    ytmp[:, 2 * (y % 2):2 * (y % 2) + 2, :],
                                                    ALU.add).then_inc(y_added, 1)
                dve.wait_ge(y_added, g * 4 + 4)

            def add_sublayer(f, gate):
                dve.wait_ge(down_done, 2 * (FF[f]["base"] + FF[f]["total"]))
                link(nc.vector.tensor_tensor(ffy[:], ps[:, 0:4, :].rearrange("p b (r d) -> p (b r) d", r=2),
                                             gates[:, gate:gate + 1, :].to_broadcast([P, NT, D]), ALU.mult))
                link(nc.vector.tensor_tensor(x[:], x[:], ffy[:], ALU.add))

            def pick(source, width, k):
                for t in range(NT):
                    ins = nc.vector.max(top[:, t, :], source[:, t, 0:width])
                link(ins)
                for t in range(NT):
                    ins = nc.vector.max_index(topi[:, t, :], top[:, t, :], source[:, t, 0:width])
                link(ins)
                link(nc.vector.tensor_copy(topf[:], topi[:]))
                place = iota[:, 0:width].unsqueeze(1).to_broadcast([P, NT, width])
                for i in range(k):
                    index = topf[:, :, i:i + 1].to_broadcast([P, NT, width])
                    got = sel if i == 0 else eq
                    link(nc.vector.tensor_tensor(got[:, :, 0:width], place, index, ALU.is_equal))
                    if i:
                        link(nc.vector.tensor_tensor(sel[:, :, 0:width], sel[:, :, 0:width], eq[:, :, 0:width],
                                                     ALU.add))

            def store_combine(f, width):
                dve.wait_ge(wc_transposed, f + 1)
                nc.vector.tensor_copy(wT[0:width, :], ps[0:width, 1:3, :].rearrange("p b t -> p (b t)")
                                      ).then_inc(wT_ready, 1)

            def ffn_tiles(f, start, stop_after=False, last_low=True):
                base, total, cused = FF[f]["base"], FF[f]["total"], FF[f]["cused"]

                def low_half(pos, hf, back):
                    dve.wait_ge(hid_hi_done, pos * 2 + (2 * (base - back) + hf + 1))
                    nc.vector.tensor_tensor(hid_lo[:, hf, :], fc[:, hf, :], hid_hi[:, hf, :],
                                            ALU.subtract).then_inc(hid_lo_done, 1)

                def tile(pos, turn, low):
                    buf = low % NB
                    for hf in range(2):
                        k1 = 2 * base + hf + 1
                        dve.wait_ge(tanh_done, pos * 2 + k1)
                        nc.vector.scalar_tensor_tensor(fa[:, hf, :], th[:, hf, :], 1.0, ps[:, 4 + 2 * hf, :],
                                                       ALU.add, ALU.mult).then_inc(silu_done, 1)
                        dve.wait_ge(silu_done, pos * 2 + k1)
                        nc.vector.tensor_tensor(fb[:, hf, :], fa[:, hf, :], ps[:, 5 + 2 * hf, :],
                                                ALU.mult).then_inc(gated, 1)
                        dve.wait_ge(gated, pos * 2 + k1)
                        if 2 * (base + low) + hf - 1 > 0:
                            dve.wait_ge(hid_lo_done, pos * 2 + (k1 - 2))
                        if f == 0 and isinstance(pos, int) and pos == 0:
                            nc.vector.tensor_scalar(fc[:, hf, :], fb[:, hf, :], 0.5, None,
                                                    ALU.mult).then_inc(weighted, 1)
                        else:
                            dve.wait_ge(wbc_in[buf], turn * 16 + 16 * (cused[buf] + 1))
                            nc.vector.tensor_tensor(fc[:, hf, :], fb[:, hf, :],
                                                    wbc[:, buf, hf * 512:hf * 512 + 512],
                                                    ALU.mult).then_inc(weighted, 1)
                        if hf == 1:
                            low_half(pos, 0, 0)
                        elif low > 0:
                            low_half(pos, 1, 1)
                return tile, lambda: low_half(total - 1, 1, 0)

            def clear_sum():
                nc.vector.memset(ps[:, 0:4, :], 0.0).then_inc(y_cleared, 1)

            dve.wait_ge(y_added, 4 * NG)
            normalise(lambda t: x[:, t, :], xn_of[1], ln_normed)
            split_input(1)
            dve.wait_ge(logits_exp, 1)
            link(nc.vector.tensor_copy(key[:], ps[:, 0, :].rearrange("p (t e) -> p t e", t=NT)))
            pick(key, E0, TOPK0)
            nc.vector.tensor_copy(sel_b[:], sel[:]).then_inc(sel_ready, 1)
            dve.wait_ge(logits_exp, 1)
            link(nc.vector.tensor_scalar(sig[:], sig[:], 1.0, None, ALU.add))
            link(nc.vector.reciprocal(sig[:], sig[:]))
            link(nc.vector.tensor_tensor(ws[:], sel[:], sig[:], ALU.mult))
            link(nc.vector.reduce_sum(rsm[:, 0, :], ws[:], AX.X))
            link(nc.vector.reciprocal(rsm[:, 1, :], rsm[:, 0, :]))
            link(nc.vector.tensor_scalar(rsm[:, 2, :], rsm[:, 1, :], 0.5, None, ALU.mult))
            link(nc.vector.tensor_tensor(ws[:], ws[:], rsm[:, 2, :].unsqueeze(2).to_broadcast([P, NT, E0]),
                                         ALU.mult))
            dve.wait_ge(counted, 1)
            nc.vector.scalar_tensor_tensor(wc[:], ps[:, 3, :].rearrange("p (t e) -> p t e", t=NT), float(CAP),
                                           ws[:], ALU.is_lt, ALU.mult).then_inc(wc_ready, 1)
            store_combine(0, E0)
            dve.wait_ge(wT_ready, 1)
            clear_sum()
            tile, finish = ffn_tiles(0, 0)
            walk(dve, 0, tile)
            finish()
            add_sublayer(0, 1)
            nc.vector.memset(mx[:, 0:1] if False else a_t[:], 0.0).then_inc(sublayer_added, 1)

            normalise(lambda t: x[:, t, :], xn_of[2], ln_normed)
            split_input(2)
            dve.wait_ge(ssm_loaded, 64)
            link(nc.vector.tensor_scalar(opd[:], svec[:, 1:1 + KC], 1.0, None, ALU.add))
            dve.wait_ge(a_step, 2)
            for hf in range(2):
                dve.wait_ge(u_done, hf + 1)
                nc.vector.tensor_tensor_scan(hs[:, hf * 512:hf * 512 + 512], a_disc[:].to_broadcast([P, 512]),
                                             ps[:, hf, :], 0.0 if hf == 0 else hs[:, 511:512], ALU.mult,
                                             ALU.add).then_inc(scanned, 1)
                dve.wait_ge(scanned, hf + 1)
            for hf in range(2):
                for mc in range(KC):
                    b = 2 * hf + mc
                    dve.wait_ge(hc_done, b + 1)
                    s = slice(hf * 512, hf * 512 + 512)
                    nc.vector.scalar_tensor_tensor(zT[:, mc, s], hT_b[:, mc, s], opd[:, mc:mc + 1], ps[:, 4 + b, :],
                                                   ALU.mult, ALU.add).then_inc(z_ready, 1)
            link(nc.vector.tensor_tensor(lnwb[:], lnwb[:], gates[:, 2:3, :].to_broadcast([P, 2, D]), ALU.mult))
            dve.wait_ge(z_transposed, NT)
            zrow = ps[:, 0:4, :].rearrange("p b (r d) -> p (b r) d", r=2)
            normalise(lambda t: zrow[:, t, :], xn_b, scanned)
            dve.wait_ge(scanned, 2 + NT)
            link(nc.vector.tensor_tensor(ffy[:], xn_b[:], lnwb[:, 0:1, :].to_broadcast([P, NT, D]), ALU.mult))
            link(nc.vector.tensor_tensor(ffy[:], ffy[:], lnwb[:, 1:2, :].to_broadcast([P, NT, D]), ALU.add))
            link(nc.vector.tensor_tensor(x[:], x[:], ffy[:], ALU.add))
            nc.vector.memset(opd[:], 0.0).then_inc(sublayer_added, 1)

            normalise(lambda t: x[:, t, :], xn_of[3], ln_normed)
            split_input(3)
            dve.wait_ge(logits_done, 2)
            lg = ps[:, 0, 0:NT * E1].rearrange("p (t e) -> p t e", t=NT)
            link(nc.vector.reduce_max(rsm[:, 0, :], lg, AX.X))
            nc.vector.tensor_tensor(sig[:, :, 0:E1], lg, rsm[:, 0, :].unsqueeze(2).to_broadcast([P, NT, E1]),
                                    ALU.subtract).then_inc(shifted, 1)
            dve.wait_ge(logits_exp, 2)
            link(nc.vector.reduce_sum(rsm[:, 1, :], key[:, :, 0:E1], AX.X))
            link(nc.vector.reciprocal(rsm[:, 1, :], rsm[:, 1, :]))
            link(nc.vector.tensor_tensor(key[:, :, 0:E1], key[:, :, 0:E1],
                                         rsm[:, 1, :].unsqueeze(2).to_broadcast([P, NT, E1]), ALU.mult))
            pick(key, E1, TOPK1)
            link(nc.vector.tensor_tensor(ws[:, :, 0:E1], sel[:, :, 0:E1], key[:, :, 0:E1], ALU.mult))
            link(nc.vector.reduce_sum(rsm[:, 2, :], ws[:, :, 0:E1], AX.X))
            link(nc.vector.reciprocal(rsm[:, 2, :], rsm[:, 2, :]))
            link(nc.vector.tensor_scalar(rsm[:, 3, :], rsm[:, 2, :], 0.5, None, ALU.mult))
            nc.vector.tensor_tensor(wc[:, :, 0:E1], ws[:, :, 0:E1],
                                    rsm[:, 3, :].unsqueeze(2).to_broadcast([P, NT, E1]),
                                    ALU.mult).then_inc(wc_ready, 1)
            store_combine(1, E1)
            dve.wait_ge(wT_ready, 2)
            clear_sum()
            tile, finish = ffn_tiles(1, 0)
            walk(dve, 1, tile)
            finish()
            add_sublayer(1, 3)
            nc.vector.memset(opd[:], 0.0).then_inc(sublayer_added, 1)

        @block.tensor
        def _(pe):
            def three(out, w_hi_, w_lo_, m_hi, m_lo, start, stop):
                nc.tensor.matmul(out, w_hi_, m_hi, start=start, stop=False, skip_group_check=True)
                nc.tensor.matmul(out, w_hi_, m_lo, start=False, stop=False, skip_group_check=True)
                return nc.tensor.matmul(out, w_lo_, m_hi, start=False, stop=stop, skip_group_check=True)

            def transpose_input(n):
                xn = xn_of[n]
                for hf in range(2):
                    pe.wait_ge(ln_normed, NT * n + 4 * hf + 4)
                    for kc in range(KC):
                        for t in range(4):
                            ins = nc.tensor.transpose(ps[:, 4 + 2 * hf + kc, t * P:(t + 1) * P],
                                                      xn[:, 4 * hf + t, kc * P:(kc + 1) * P], ident[:])
                        ins.then_inc(ln_transposed, 1)

            pe.wait_ge(setup_loaded, 64)
            pe.wait_ge(c_ready, 1)
            for layer in range(2):
                for j in range(12):
                    for kc in range(KC):
                        ins = nc.tensor.matmul(ps[:, 0, 12 * layer + j:12 * layer + j + 1],
                                               wmod[:, layer, kc, j * P:(j + 1) * P],
                                               csil[:, 2 * layer + kc:2 * layer + kc + 1],
                                               start=(kc == 0), stop=(kc == KC - 1), skip_group_check=True)
            ins.then_inc(mod_done, 1)
            pe.wait_ge(consts_ready, 1)
            transpose_input(0)
            for layer in range(2):
                for i, kind in enumerate((2, 5)):
                    for kc in range(KC):
                        ins = nc.tensor.matmul(ps[:, 1 + layer, i * D:(i + 1) * D], csb[:, 2 * layer + kc, :],
                                               wmod[:, layer, kc, kind * D:(kind + 1) * D],
                                               start=(kc == 0), stop=(kc == KC - 1), skip_group_check=True)
            ins.then_inc(mod_done, 1)
            pe.wait_ge(h_lo, 4)
            pe.wait_ge(vec_step, 1)

            with pe.Fori(0, NG) as g:
                def transpose_q(t):
                    pe.wait_ge(q_copied, g * NT + (t + 1))
                    if t >= 2:
                        pe.wait_ge(qT_lo_done, g * NT + (t - 1))
                    for h in range(HPG):
                        ins = nc.tensor.transpose(ps[:, 4 + t % 2, h * P:(h + 1) * P],
                                                  q_f[:, t % 2, h * HD:(h + 1) * HD], ident[:])
                    ins.then_inc(q_transposed, 1)

                def project(out, t, cols):
                    tok = slice(t * P, (t + 1) * P)
                    for kc in range(KC):
                        ins = three(out, hT_hi[:, kc, tok], hT_lo[:, kc, tok], wqkv_hi[:, kc, cols],
                                    wqkv_lo[:, kc, cols], kc == 0, kc == KC - 1)
                    return ins

                pe.wait_ge(wqkv_ready, g + 1)
                for t in range(NT):
                    if t >= 4:
                        pe.wait_ge(kv_copied, g * NT + (t - 3))
                    project(ps[:, t % 4, 0:2 * HD], t, slice(HPG * HD, QKV)).then_inc(kv_projected, 1)
                for t in range(NT):
                    if t < 2:
                        pe.wait_ge(kv_copied, g * NT + (t + 5))
                    else:
                        pe.wait_ge(q_copied, g * NT + (t - 1))
                    project(ps[:, t % 2, :], t, slice(0, HPG * HD)).then_inc(projected, 1)
                    if t >= 1:
                        transpose_q(t - 1)
                    if t >= NT - 2:
                        b = t - (NT - 2)
                        pe.wait_ge(kv_copied, g * NT + NT)
                        pe.wait_ge(k_normed, g * NT + (4 * b + 4))
                        for i in range(4):
                            ins = nc.tensor.transpose(ps[:, 2 + b, i * P:(i + 1) * P], k_f[:, 4 * b + i, :],
                                                      ident[:])
                        ins.then_inc(k_transposed, 1)
                transpose_q(NT - 1)
                pe.wait_ge(q_copied, g * NT + NT)
                pe.wait_ge(qT_lo_done, g * NT + NT)
                pe.wait_ge(kT_lo_done, g * 2 + 2)

                for n in range(STEPS + WOLAG - 3):
                    if n < STEPS:
                        m, c, h, qi = step_of(n)
                        w = blocks(n) * P
                        pair = 2 * (n % 2)
                        pieces = [(pair, 0, w)] if c == 0 else [(pair, 0, w // 2), (pair + 1, w // 2, w // 2)]
                        q = slice((4 * c + qi) * P, (4 * c + qi + 1) * P)
                        if n >= 2:
                            pe.wait_ge(exp_done, g * STEPS + (n - 1))
                        for bank, k0, kw in pieces:
                            three(ps[:, bank, 0:kw], qT_hi[:, h, q], qT_lo[:, h, q], kT_hi[:, k0:k0 + kw],
                                  kT_lo[:, k0:k0 + kw], True, False)
                        bank, k0, kw = pieces[-1]
                        nc.tensor.matmul(ps[:, bank, kw - P:kw], ident_b[:], mask_b[:], start=False, stop=True,
                                         skip_group_check=True).then_inc(scored, 1)
                    def bank_free(place):
                        if place >= 2:
                            kind, index = BANK_ORDER[place - 2][:2]
                            if kind == "p":
                                pe.wait_ge(pT_lo_done, g * TGS + (index + 1))
                            elif kind == "r":
                                pe.wait_ge(r_copied, g * 2 * HPG + (index + 1))
                            else:
                                pe.wait_ge(y_scaled, g * 4 + (index + 1))

                    for what, place in BANK_AT.get(n, []):
                        if what[0] == "p":
                            _, q, u, j0, nb = what
                            k = n - TLAG
                            bank_free(place)
                            pe.wait_ge(exp_done, g * STEPS + (k + 1))
                            for j in range(nb):
                                ins = nc.tensor.transpose(ps[:, 4 + place % 2, j * P:(j + 1) * P],
                                                          prob[:, k % 3, (j0 + j) * P:(j0 + j + 1) * P], ident[:])
                            ins.then_inc(p_transposed, 1)
                    for r in range(NP):
                        m = head_at(n, PVLAG + r)
                        if m is None:
                            continue
                        c = m // HPG
                        if r == 0:
                            pe.wait_ge(pT_lo_done, g * TGS + TG_BEFORE[4 * m + 4])
                            if m >= 2:
                                pe.wait_ge(o_normed, g * 2 * HPG + (m - 1))
                        for j in PIECES[c][r]:
                            q0 = max(0, j - 4 * c) * P
                            u = (unit_base(m) + j // 4) % NUNITS
                            ins = three(ps[:, 6 + m % 2, q0:512], v_hi[:, j, :], v_lo[:, j, :],
                                        pT_hi[:, u, j % 4, q0:512], pT_lo[:, u, j % 4, q0:512], j == 0,
                                        j == 4 * c + 3)
                        ins.then_inc(pv_done, 1)
                    for what, place in BANK_AT.get(n, []):
                        if what[0] == "r":
                            m = what[1]
                            bank_free(place)
                            pe.wait_ge(row_inv, g * 2 * HPG + (m + 1))
                            for qi in range(4):
                                ins = nc.tensor.transpose(ps[:, 4 + place % 2, qi * P:(qi + 1) * P],
                                                          rinv[:, m % 2, qi:qi + 1].to_broadcast([P, P]), ident[:])
                            ins.then_inc(r_spread, 1)
                        elif what[0] == "y":
                            y = what[1]
                            bank_free(place)
                            pe.wait_ge(wo_ready, g + 1)
                            pe.wait_ge(oT_lo_done, g * 2 * HPG + (HPG * (y // 2) + HPG))
                            for t in range(2):
                                tok = slice((2 * (y % 2) + t) * P, (2 * (y % 2) + t + 1) * P)
                                for h in range(HPG):
                                    ins = three(ps[:, 4 + place % 2, t * D:(t + 1) * D], oT_hi[:, h, tok],
                                                oT_lo[:, h, tok], wo_hi[:, h, :], wo_lo[:, h, :], h == 0,
                                                h == HPG - 1)
                            ins.then_inc(wo_done, 1)

            def router(gate, width):
                for t in range(NT):
                    for kc in range(KC):
                        ins = nc.tensor.matmul(ps[:, 0, t * width:(t + 1) * width], hT_b[:, kc, t * P:(t + 1) * P],
                                               gate[:, kc, :], start=(kc == 0), stop=(kc == KC - 1),
                                               skip_group_check=True)
                ins.then_inc(logits_done, 1)

            def transpose_combine(f, width):
                pe.wait_ge(wc_ready, f + 1)
                for t in range(NT):
                    ins = nc.tensor.transpose(ps[0:width, 1 + t // 4, (t % 4) * P:(t % 4 + 1) * P],
                                              wc[:, t, 0:width], ident[:])
                ins.then_inc(wc_transposed, 1)

            def ffn(f):
                base, total = FF[f]["base"], FF[f]["total"]

                def up(pos, low, hf):
                    buf = low % NB
                    if 2 * (base + low) + hf - 1 > 0:
                        pe.wait_ge(gated, pos * 2 + (2 * base + hf - 1))
                    tok = slice(hf * 512, hf * 512 + 512)
                    for v in range(2):
                        for kc in range(KC):
                            s = slice((2 * kc + v) * P, (2 * kc + v + 1) * P)
                            ins = three(ps[:, 4 + 2 * hf + v, :], w_hi[:, buf, s], w_lo[:, buf, s],
                                        hT_hi[:, kc, tok], hT_lo[:, kc, tok], kc == 0, kc == KC - 1)
                    ins.then_inc(up_done, 1)

                def down(pos, buf, hf, back):
                    pe.wait_ge(hid_lo_done, pos * 2 + (2 * (base - back) + hf + 1))
                    for t in range(4):
                        tile = 4 * hf + t
                        tok = slice(t * P, (t + 1) * P)
                        ins = three(ps[:, tile // 2, (tile % 2) * D:(tile % 2 + 1) * D], hid_hi[:, hf, tok],
                                    hid_lo[:, hf, tok], w_hi[:, buf, 4 * P:], w_lo[:, buf, 4 * P:], False, False)
                    ins.then_inc(down_done, 1)

                def tile(pos, turn, low):
                    pe.wait_ge(w_ready, pos + (base + 1))
                    for hf in range(2):
                        up(pos, low, hf)
                        if low > 0:
                            down(pos, (low - 1) % NB, hf, 1)

                pe.wait_ge(y_cleared, f + 1)
                walk(pe, f, tile)
                for hf in range(2):
                    down(total - 1, (total - 1) % NB, hf, 0)

            transpose_input(1)
            pe.wait_ge(h_full, 8)
            pe.wait_ge(gate_loaded, 16)
            router(wgate, E0)
            pe.wait_ge(sel_ready, 1)
            for t in range(NT):
                for s in range(t + 1):
                    ins = nc.tensor.matmul(ps[:, 3, t * E0:(t + 1) * E0], (before_b if s == t else ones_b)[:],
                                           sel_b[:, s, :], start=(s == 0), stop=(s == t), skip_group_check=True)
            ins.then_inc(counted, 1)
            transpose_combine(0, E0)
            pe.wait_ge(h_lo, 8)
            ffn(0)

            transpose_input(2)
            pe.wait_ge(h_full, 12)
            pe.wait_ge(ssm_loaded, 64)
            pe.wait_ge(sublayer_added, 1)
            for hf in range(2):
                for kc in range(KC):
                    ins = nc.tensor.matmul(ps[:, hf, :], bT[:, kc, :], hT_b[:, kc, hf * 512:hf * 512 + 512],
                                           start=(kc == 0), stop=(kc == KC - 1))
                ins.then_inc(u_done, 1)
            pe.wait_ge(h_hi, 12)
            for hf in range(2):
                pe.wait_ge(scanned, hf + 1)
                for mc in range(KC):
                    nc.tensor.matmul(ps[:, 4 + 2 * hf + mc, :], cT[:, mc * P:(mc + 1) * P],
                                     hs[:, hf * 512:hf * 512 + 512], start=True, stop=True).then_inc(hc_done, 1)
            for t in range(NT):
                if t % 4 == 0:
                    pe.wait_ge(z_ready, 2 * (t // 4) + 2)
                for mc in range(KC):
                    ins = nc.tensor.transpose(ps[:, t // 2, (t % 2) * D + mc * P:(t % 2) * D + (mc + 1) * P],
                                              zT[:, mc, t * P:(t + 1) * P], ident[:])
                ins.then_inc(z_transposed, 1)

            transpose_input(3)
            pe.wait_ge(h_full, 16)
            pe.wait_ge(gate_loaded, 32)
            router(wgate1, E1)
            transpose_combine(1, E1)
            pe.wait_ge(h_lo, 16)
            ffn(1)


def kernel(L0_attn_x, L0_attn_Wq, L0_attn_Wk, L0_attn_Wv, L0_attn_Wo, L0_attn_q_scale, L0_attn_k_scale,
           L0_ffn_w_gate, L0_ffn_w_shared_up, L0_ffn_w_shared_down, L0_ffn_w_up, L0_ffn_w_down, L0_c, L0_wmod,
           L1_attn_log_A_diag, L1_attn_B_mat, L1_attn_C_mat, L1_attn_D_vec, L1_attn_ln_w, L1_attn_ln_b,
           L1_ffn_gate_weight, L1_ffn_gate_up_proj, L1_ffn_down_proj, L1_c, L1_wmod):
    import numpy as np
    import concourse.bacc as bacc
    from concourse.bass_utils import run_bass_kernel_spmd

    def a(v):
        return np.asarray(v)

    def k_on_partitions(w):
        return np.ascontiguousarray(w.reshape(KC, P, -1).transpose(1, 0, 2))

    w_attn, w_out = [], []
    for g in range(NG):
        rows = slice(g * HPG * HD, (g + 1) * HPG * HD)
        kv = slice(g * HD, (g + 1) * HD)
        cols = np.concatenate([a(L0_attn_Wq)[rows].T, a(L0_attn_Wk)[kv].T, a(L0_attn_Wv)[kv].T], axis=1)
        w_attn.append(k_on_partitions(cols))
        w_out.append(a(L0_attn_Wo)[:, rows].T.reshape(HPG, HD, D).transpose(1, 0, 2))

    def hidden_tile(gate, value, down):
        gv = np.stack([gate.reshape(KC, P, P), value.reshape(KC, P, P)], axis=1)
        return np.concatenate([gv.transpose(2, 0, 1, 3).reshape(P, 4 * P), down], axis=1)

    up = a(L0_ffn_w_shared_up)
    pad = np.zeros((D, P - HS), up.dtype)
    ffn0 = [hidden_tile(np.concatenate([up[:, HS:], pad], axis=1), np.concatenate([up[:, :HS], pad], axis=1),
                        np.concatenate([a(L0_ffn_w_shared_down), np.zeros((P - HS, D), up.dtype)], axis=0))]
    for i in range(IT0):
        e = a(L0_ffn_w_up)[EPT0 * i:EPT0 * (i + 1)].transpose(1, 0, 2)
        ffn0.append(hidden_tile(e[:, :, :H0].reshape(D, P), e[:, :, H0:].reshape(D, P),
                                a(L0_ffn_w_down)[EPT0 * i:EPT0 * (i + 1)].reshape(P, D)))
    ffn1 = []
    for e in range(E1):
        for q in range(H1 // P):
            rows = slice(q * P, (q + 1) * P)
            gate_up = a(L1_ffn_gate_up_proj)[e]
            ffn1.append(hidden_tile(gate_up[:H1][rows].T, gate_up[H1:][rows].T, a(L1_ffn_down_proj)[e][:, rows].T))

    n = np.arange(P)
    const = np.concatenate([np.eye(P), np.where(n[None, :] > n[:, None], MASKED, 0.0), n[:, None] < n[None, :],
                            np.broadcast_to(np.arange(E0), (P, E0))], axis=1).astype(np.float32)
    ins = {
        "x": a(L0_attn_x).reshape(T, D),
        "w_attn": np.stack(w_attn), "w_out": np.stack(w_out),
        "qk_scale": np.stack([a(L0_attn_q_scale), a(L0_attn_k_scale)], axis=1),
        "gate0": k_on_partitions(a(L0_ffn_w_gate)), "ffn0": np.stack(ffn0),
        "c": np.concatenate([a(L0_c).reshape(KC, P).T, a(L1_c).reshape(KC, P).T], axis=1),
        "wmod": np.stack([k_on_partitions(a(L0_wmod)), k_on_partitions(a(L1_wmod))], axis=1),
        "const": const,
        "ssm_vec": np.concatenate([a(L1_attn_log_A_diag)[:, None], a(L1_attn_D_vec).reshape(KC, P).T], axis=1),
        "bmat": k_on_partitions(a(L1_attn_B_mat).T), "cmat": a(L1_attn_C_mat).T,
        "lnwb": np.stack([a(L1_attn_ln_w), a(L1_attn_ln_b)]),
        "gate1": k_on_partitions(a(L1_ffn_gate_weight).T), "ffn1": np.stack(ffn1),
    }
    ins = {k: np.ascontiguousarray(v) for k, v in ins.items()}
    nc = bacc.Bacc("TRN2", target_bir_lowering=False, num_devices=1)
    aps = [nc.dram_tensor("in_" + k, v.shape, F32, kind="ExternalInput").ap() for k, v in ins.items()]
    out = nc.dram_tensor("out", (T, D), F32, kind="ExternalOutput").ap()
    wt0 = nc.dram_tensor("combine0", (E0, T), F32, kind="Internal").ap()
    wt1 = nc.dram_tensor("combine1", (E1, 4, T), F32, kind="Internal").ap()
    program(nc, *aps, out, wt0, wt1)
    r = run_bass_kernel_spmd(nc, [{"in_" + k: v for k, v in ins.items()}], core_ids=[0])
    return r.results[0]["out"].reshape(1, T, D)
```

```python
import concourse.bass as bass
from concourse import mybir
from contextlib import ExitStack

F32 = mybir.dt.float32
F32R = mybir.dt.float32r
BF16 = mybir.dt.bfloat16
I32 = mybir.dt.int32
U32 = mybir.dt.uint32
ALU = mybir.AluOpType
ACT = mybir.ActivationFunctionType
AX = mybir.AxisListType

P = 128
T, D = 1024, 256
NT = T // P
KC = D // P
NG, HPG, HD = 4, 4, 128
E0, H0, TOPK0, CAP = 64, 32, 6, 128
HS = 64
E1, H1, TOPK1 = 8, 512, 2
EPT0 = P // H0
IT0 = E0 // EPT0
IT1 = E1 * H1 // P
NSTATE = 128
QKV = HPG * HD + 2 * HD
MASKED = -1e30
EPS_Q = 1e-6
EPS_LN = 1e-5
RSQRT_SEED = float(0x5F3759DF)
NEWTON = 3

STEPS = 2 * HPG * 4
TLAG = 2
PVLAG = 6
RLAG = 8
OLAG = 10
WOLAG = 12
PIECES = [[[0], [1], [2, 3]], [[0, 1, 2, 3], [4, 5], [6, 7]]]
NP = 3
NB = 3


def step_of(n):
    m, qi = divmod(n, 4)
    return m, m // HPG, m % HPG, qi


def blocks(n):
    m, c, h, qi = step_of(n)
    return 4 * c + qi + 1


def transposed_groups(n):
    k = blocks(n)
    return [(u, 4 * u, min(4, k - 4 * u)) for u in range((k + 3) // 4)]


TG_BEFORE = [0]
for _n in range(STEPS):
    TG_BEFORE.append(TG_BEFORE[-1] + len(transposed_groups(_n)))
TGS = TG_BEFORE[-1]


def unit_base(m):
    return m if m < HPG else HPG + 2 * (m - HPG)


def pieces_until_free(unit):
    if unit < HPG:
        return NP * unit + NP
    m, second = divmod(unit - HPG, 2)
    return NP * (m + HPG) + (NP if second else 1)


def head_at(n, lag):
    m, r = divmod(n - lag, 4)
    return m if r == 0 and 0 <= m < 2 * HPG else None


def banks_of_transposes():
    order, at = [], {}
    for n in range(STEPS + WOLAG - 3):
        if 0 <= n - TLAG < STEPS:
            for u, j0, nb in transposed_groups(n - TLAG):
                at.setdefault(n, []).append((("p", TG_BEFORE[n - TLAG] + u, u, j0, nb), len(order)))
                order.append(("p", TG_BEFORE[n - TLAG] + u))
        m = head_at(n, RLAG)
        if m is not None:
            at.setdefault(n, []).append((("r", m), len(order)))
            order.append(("r", m))
        c, r = divmod(n - 12 - WOLAG, 16)
        if r == 0 and c >= 0:
            for half in range(2):
                at.setdefault(n, []).append((("y", 2 * c + half), len(order)))
                order.append(("y", 2 * c + half))
    return order, at


BANK_ORDER, BANK_AT = banks_of_transposes()
NUNITS = 3


def program(nc, x_d, w_attn_d, w_out_d, qk_scale_d, gate0_d, ffn0_d, c_d, wmod_d, const_d,
            ssm_vec_d, bmat_d, cmat_d, lnwb_d, gate1_d, ffn1_d, out_d, wt0_d, wt1_d):
    ctx = ExitStack()

    def sem(name):
        return ctx.enter_context(nc.semaphore(name))

    def keep(name, shape, dt=F32):
        return ctx.enter_context(nc.sbuf_tensor(name, shape, dt))

    with ctx:
        x = keep("x", [P, NT, D])
        hT_hi = keep("hT_hi", [P, KC, T], F32R)
        hT_lo = keep("hT_lo", [P, KC, T], F32R)
        ident = keep("ident", [P, P])
        mask_b = keep("mask_b", [P, P], BF16)
        ident_b = keep("ident_b", [P, P], BF16)
        before_b = keep("before_b", [P, P], BF16)
        ones_b = keep("ones_b", [P, P], BF16)
        iota = keep("iota", [P, E0])
        modc = keep("modc", [P, 2, 8])
        opc = keep("opc", [P, 2, 8])
        csb = keep("csb", [P, 4, P])
        gates = keep("gates", [P, 4, D])
        one = keep("one", [P, 1])
        ccol = keep("ccol", [P, 4])
        cth = keep("cth", [P, 4])
        csil = keep("csil", [P, 4])
        qks = keep("qks", [P, 2])
        stat = keep("stat", [P, NT, 6])
        mv = keep("mv", [P, NT, 2])
        idle = keep("idle", [P, 1])
        rs_in = keep("rs_in", [P, NT * 5])
        rs_y = keep("rs_y", [P, NT * 5])
        rs_t = keep("rs_t", [P, NT * 5])
        wqkv_raw = keep("wqkv_raw", [P, KC, QKV])
        wqkv_hi = keep("wqkv_hi", [P, KC, QKV], F32R)
        wqkv_lo = keep("wqkv_lo", [P, KC, QKV], F32R)
        wo_raw = keep("wo_raw", [P, HPG, D])
        wo_hi = keep("wo_hi", [P, HPG, D], F32R)
        wo_lo = keep("wo_lo", [P, HPG, D], F32R)

        def stage(*specs):
            with ExitStack() as s:
                return [s.enter_context(nc.sbuf_tensor(name, shape, dt)) for name, shape, dt in specs]

        hT_a, xn_a, wmod, const, gmag, gsgn, grow = stage(
            ("hT_a", [P, KC, T], F32), ("xn_a", [P, NT, D], F32),
            ("wmod", [P, KC, 6 * D], F32), ("const", [P, 3 * P + E0], F32),
            ("gmag", [P, 2, D], F32), ("gsgn", [P, 2, D], F32), ("grow", [P, 2, D], F32))
        (qT_hi, qT_lo, kT_hi, kT_lo, v_hi, v_lo, prob, pT_hi, pT_lo, oT_hi, oT_lo, q_f, k_f, sq, sqk,
         r_sb, o_f, mx, negb, rsum, rinv, rqs, rk_in) = stage(
            ("qT_hi", [P, HPG, T], F32R), ("qT_lo", [P, HPG, T], F32R),
            ("kT_hi", [P, T], F32R), ("kT_lo", [P, T], F32R),
            ("v_hi", [P, NT, HD], F32R), ("v_lo", [P, NT, HD], F32R),
            ("prob", [P, 3, T], F32),
            ("pT_hi", [P, NUNITS, 4, 512], F32R), ("pT_lo", [P, NUNITS, 4, 512], F32R),
            ("oT_hi", [P, HPG, 512], F32R), ("oT_lo", [P, HPG, 512], F32R),
            ("q_f", [P, 2, HPG * HD], F32), ("k_f", [P, NT, HD], F32),
            ("sq", [P, HPG * HD], F32), ("sqk", [P, HD], F32), ("r_sb", [P, 2, 512], F32), ("o_f", [P, 512], F32),
            ("mx", [P, 2], F32), ("negb", [P, 2], F32), ("rsum", [P, 2, 4], F32), ("rinv", [P, 2, 4], F32),
            ("rqs", [P, NT, HPG], F32), ("rk_in", [P, NT], F32))
        ytmp = k_f[:].rearrange("p (r a) d -> p r (a d)", a=2)
        (hT_b, xn_b, w_raw, w_hi, w_lo, wbc, th, fa, fb, fc, hid_hi, hid_lo, wgate, wgate1, key, sig, sel, eq,
         ws, wc, sel_b, top, topi, topf, wT, rsm, bT, cT, hs, zT, lnwb, svec, a_t, a_disc, opd, x_b) = stage(
            ("hT_b", [P, KC, T], F32), ("xn_b", [P, NT, D], F32),
            ("w_raw", [P, NB, 6 * P], F32), ("w_hi", [P, NB, 6 * P], F32R), ("w_lo", [P, NB, 6 * P], F32R),
            ("wbc", [P, NB, T], F32), ("th", [P, 2, 512], F32), ("fa", [P, 2, 512], F32),
            ("fb", [P, 2, 512], F32), ("fc", [P, 2, 512], F32),
            ("hid_hi", [P, 2, 512], F32R), ("hid_lo", [P, 2, 512], F32R),
            ("wgate", [P, KC, E0], F32), ("wgate1", [P, KC, E1], F32),
            ("key", [P, NT, E0], F32), ("sig", [P, NT, E0], F32), ("sel", [P, NT, E0], F32),
            ("eq", [P, NT, E0], F32), ("ws", [P, NT, E0], F32), ("wc", [P, NT, E0], F32),
            ("sel_b", [P, NT, E0], BF16), ("top", [P, NT, 8], F32), ("topi", [P, NT, 8], U32),
            ("topf", [P, NT, 8], F32), ("wT", [E0, T], F32), ("rsm", [P, 4, NT], F32),
            ("bT", [P, KC, NSTATE], F32), ("cT", [P, D], F32), ("hs", [P, T], F32),
            ("zT", [P, KC, T], F32), ("lnwb", [P, 2, D], F32), ("svec", [P, 1 + KC], F32),
            ("a_t", [P, 1], F32), ("a_disc", [P, 1], F32), ("opd", [P, KC], F32), ("x_b", [P, NT, D], F32))
        wmod1 = [zT[:].rearrange("p k t -> p (k t)")[:, 0:6 * D], x_b[:].rearrange("p t d -> p (t d)")[:, 0:6 * D]]
        hT_of = [hT_a, hT_b, hT_b, hT_b]
        xn_of = [xn_a, xn_b, xn_b, xn_b]
        ps = ctx.enter_context(nc.psum_tensor("ps", [P, 8, 512], F32))

        (setup_loaded, x_loaded, consts_ready, c_tanh, c_ready, mod_done, mod_ready, vec_step, ln_normed,
         ln_transposed, h_full, h_hi, h_lo, wqkv_raw_in, wqkv_high, wqkv_ready, wo_raw_in, wo_high, wo_ready,
         projected, q_copied, kv_copied, squares, square_sums, v_split, q_transposed, qT_hi_done, qT_lo_done,
         qk_norm_step, k_normed, k_transposed, kT_hi_done, kT_lo_done, scored, row_max, bias_ready, exp_done,
         row_inv, prob_ready, p_transposed, pT_hi_done, pT_lo_done, pv_done, oT_hi_done, oT_lo_done, wo_done,
         y_scaled, y_added, kv_projected, key_sums, keys_copied, q_sums, r_spread, r_copied, o_normed) = [sem(n) for n in (
            "setup_loaded x_loaded consts_ready c_tanh c_ready mod_done mod_ready vec_step ln_normed "
            "ln_transposed h_full h_hi h_lo wqkv_raw_in wqkv_high wqkv_ready wo_raw_in wo_high wo_ready "
            "projected q_copied kv_copied squares square_sums v_split q_transposed qT_hi_done qT_lo_done "
            "qk_norm_step k_normed k_transposed kT_hi_done kT_lo_done scored row_max bias_ready exp_done "
            "row_inv prob_ready p_transposed pT_hi_done pT_lo_done pv_done oT_hi_done oT_lo_done wo_done "
            "y_scaled y_added kv_projected key_sums keys_copied q_sums r_spread r_copied o_normed").split()]
        (gate_loaded, logits_done, logits_exp, shifted, sel_ready, counted, wc_ready,
         wc_transposed, wT_ready, wT_stored, w_ready, up_done, tanh_done, silu_done, gated, weighted,
         hid_hi_done, hid_lo_done, down_done, ssm_loaded, a_step, u_done, scanned, hc_done, z_ready,
         z_transposed, stored) = [sem(n) for n in (
            "gate_loaded logits_done logits_exp shifted sel_ready counted wc_ready "
            "wc_transposed wT_ready wT_stored w_ready up_done tanh_done silu_done gated weighted "
            "hid_hi_done hid_lo_done down_done ssm_loaded a_step u_done scanned hc_done z_ready "
            "z_transposed stored").split()]
        w_raw_in = [sem(f"w_raw_in{b}") for b in range(NB)]
        wbc_in = [sem(f"wbc_in{b}") for b in range(NB)]
        w_high = sem("w_high")
        w_scaled = sem("w_scaled")
        one_ready = sem("one_ready")
        first_mod_loaded = sem("first_mod_loaded")
        rest_mod_loaded = sem("rest_mod_loaded")
        mod1_loaded = sem("mod1_loaded")
        mod_copied = sem("mod_copied")
        banks_marked = sem("banks_marked")
        x_in_sum = sem("x_in_sum")
        x_kept = sem("x_kept")
        gates1_ready = sem("gates1_ready")
        x_shifted = sem("x_shifted")
        x_out = sem("x_out")

        def loads_before(first, total):
            return tuple(len(range(b, total, NB)) - (1 if b < first else 0) for b in range(NB))

        FF = [dict(total=1 + IT0, peel=1 + NB + (IT0 - NB) % NB, base=0, wused=(0,) * NB, cused=(-1,) + (0,) * (NB - 1), reuse=NB),
              dict(total=IT1, peel=IT1 % NB, base=1 + IT0, wused=loads_before(0, 1 + IT0),
                   cused=loads_before(1, 1 + IT0), reuse=IT1 % NB)]

        def walk(eng, f, body, start=0):
            peel = FF[f]["peel"]
            for pos in range(start, peel):
                body(pos, pos // NB, pos)
            with eng.Fori(0, (FF[f]["total"] - peel) // NB) as j:
                for u in range(NB):
                    body(j * NB + (peel + u), j + (peel + u) // NB, peel + u)

        block = ctx.enter_context(nc.Block())

        @block.sync
        def _(sp):
            sp.dma_start(ccol[:], c_d).then_inc(setup_loaded, 16)
            sp.dma_start(const[:], const_d).then_inc(setup_loaded, 16)
            sp.dma_start(wmod[:, :, 0:2 * D], wmod_d[:, 0, :, 0:2 * D]).then_inc(first_mod_loaded, 16)
            sp.dma_start(qks[:], qk_scale_d).then_inc(setup_loaded, 16)
            sp.dma_start(wqkv_raw[:], w_attn_d[0]).then_inc(wqkv_raw_in, 16)
            sp.dma_start(wmod[:, :, 2 * D:], wmod_d[:, 0, :, 2 * D:]).then_inc(rest_mod_loaded, 16)
            sp.dma_start(wo_raw[:], w_out_d[0]).then_inc(wo_raw_in, 16)
            with sp.Fori(0, NG - 1) as g:
                sp.wait_ge(projected, g * NT + NT)
                sp.dma_start(wqkv_raw[:], w_attn_d[g + 1]).then_inc(wqkv_raw_in, 16)
                sp.wait_ge(wo_done, g * 4 + 4)
                sp.dma_start(wo_raw[:], w_out_d[g + 1]).then_inc(wo_raw_in, 16)

            def load_weights(f, src, pos, low):
                if low >= FF[f]["reuse"]:
                    sp.wait_ge(w_ready, pos + (FF[f]["base"] - NB + 1))
                elif f == 1:
                    sp.wait_ge(w_ready, FF[1]["base"])
                sp.dma_start(w_raw[:, low % NB, :], src[pos]).then_inc(w_raw_in[low % NB], 16)

            def load_combine(f, row, pos, low):
                if low >= FF[f]["reuse"]:
                    sp.wait_ge(weighted, pos * 2 + 2 * (FF[f]["base"] - NB + 1))
                elif f == 1:
                    sp.wait_ge(weighted, 2 * FF[1]["base"])
                sp.dma_start(wbc[:, low % NB, :], row).then_inc(wbc_in[low % NB], 16)

            sp.wait_ge(y_added, 4 * NG)
            sp.dma_start(wgate[:], gate0_d).then_inc(gate_loaded, 16)
            for pos in range(NB):
                load_weights(0, ffn0_d, pos, pos)
            for kc in range(KC):
                sp.dma_start(wmod1[kc], wmod_d[:, 1, kc, :]).then_inc(mod1_loaded, 16)
            sp.dma_start(svec[:], ssm_vec_d).then_inc(ssm_loaded, 16)
            sp.dma_start(bT[:], bmat_d).then_inc(ssm_loaded, 16)
            sp.dma_start(cT[:], cmat_d).then_inc(ssm_loaded, 16)
            sp.dma_start(lnwb[:], lnwb_d.unsqueeze(0).to_broadcast([P, 2, D])).then_inc(ssm_loaded, 16)
            sp.dma_start(wgate1[:], gate1_d).then_inc(ssm_loaded, 16)
            sp.wait_ge(wT_ready, 1)
            sp.dma_start(wt0_d, wT[0:E0, :]).then_inc(wT_stored, 16)
            sp.wait_ge(wT_stored, 16)
            rows0 = wt0_d.rearrange("(i e) t -> i e t", e=EPT0)

            def tile0(pos, turn, low):
                if low >= NB:
                    load_weights(0, ffn0_d, pos, low)
                load_combine(0, rows0[pos - 1].unsqueeze(1).to_broadcast([EPT0, H0, T]), pos, low)
            walk(sp, 0, tile0, start=1)

            for pos in range(FF[1]["peel"]):
                load_weights(1, ffn1_d, pos, pos)
            sp.wait_ge(wT_ready, 2)
            for r in range(4):
                sp.dma_start(wt1_d[:, r, :], wT[0:E1, :]).then_inc(wT_stored, 16)
            sp.wait_ge(wT_stored, 16 * 5)
            rows1 = wt1_d.rearrange("e r t -> (e r) t")

            def tile1(pos, turn, low):
                if low >= FF[1]["peel"]:
                    load_weights(1, ffn1_d, pos, low)
                load_combine(1, rows1[pos].unsqueeze(0).to_broadcast([P, T]), pos, low)
            walk(sp, 1, tile1)

            out_rows = out_d.rearrange("(t p) d -> p t d", p=P)
            for hf in range(2):
                sp.wait_ge(x_out, hf + 1)
                sp.dma_start(out_rows[:, 4 * hf:4 * hf + 4, :], x[:, 4 * hf:4 * hf + 4, :]).then_inc(stored, 16)
            sp.wait_ge(stored, 32)

        NORM_STEPS = 2 * (2 + 3 * NEWTON) + 1 + (4 + 3 * NEWTON)

        @block.gpsimd
        def _(pool):
            nc.gpsimd.memset(one[:], 1.0).then_inc(one_ready, 1)
            pool.wait_ge(one_ready, 1)

            def split(raw, hi, lo, raw_in, value, high, high_value, ready):
                pool.wait_ge(raw_in, value)
                nc.gpsimd.tensor_tensor(hi, raw, one[:].to_broadcast(list(raw.shape)) if len(raw.shape) == 2 else
                                        one[:].unsqueeze(2).to_broadcast(list(raw.shape)),
                                        ALU.mult).then_inc(high, 1)
                pool.wait_ge(high, high_value)
                nc.gpsimd.tensor_tensor(lo, raw, hi, ALU.subtract).then_inc(ready, 1)

            pool.wait_ge(wqkv_high, 1)
            nc.gpsimd.tensor_tensor(wqkv_lo[:], wqkv_raw[:], wqkv_hi[:], ALU.subtract).then_inc(wqkv_ready, 1)
            split(wo_raw[:], wo_hi[:], wo_lo[:], wo_raw_in, 16, wo_high, 1, wo_ready)

            def outputs_low(g):
                for m in range(2 * HPG):
                    pool.wait_ge(oT_hi_done, g * 2 * HPG + (m + 1))
                    nc.gpsimd.tensor_tensor(oT_lo[:, m % HPG, :], o_f[:], oT_hi[:, m % HPG, :],
                                            ALU.subtract).then_inc(oT_lo_done, 1)

            def normalise_keys(g):
                pool.wait_ge(keys_copied, g * NT + NT)
                pool.wait_ge(qk_norm_step, g * NORM_STEPS + (2 + 3 * NEWTON))
                for b in range(2):
                    half = k_f[:, 4 * b:4 * b + 4, :]
                    nc.gpsimd.tensor_tensor(half, half, rs_y[:, 4 * b:4 * b + 4].unsqueeze(2).to_broadcast(
                        [P, 4, HD]), ALU.mult).then_inc(k_normed, 1)

            with pool.Fori(0, NG - 1) as g:
                normalise_keys(g)
                pool.wait_ge(projected, g * NT + NT)
                split(wqkv_raw[:], wqkv_hi[:], wqkv_lo[:], wqkv_raw_in, g * 16 + 32, wqkv_high, g + 2, wqkv_ready)
                outputs_low(g)
                pool.wait_ge(wo_done, g * 4 + 4)
                split(wo_raw[:], wo_hi[:], wo_lo[:], wo_raw_in, g * 16 + 32, wo_high, g + 2, wo_ready)

            def ffn_weights(f):
                base, wused = FF[f]["base"], FF[f]["wused"]

                def tile(pos, turn, low):
                    b = low % NB
                    if low >= FF[f]["reuse"]:
                        pool.wait_ge(down_done, pos * 2 + 2 * (base - NB + 1))
                    elif f == 1:
                        pool.wait_ge(down_done, 2 * base)
                    pool.wait_ge(w_raw_in[b], turn * 16 + 16 * (wused[b] + 1))
                    down_rows = w_raw[:, b, 4 * P:]
                    nc.gpsimd.tensor_tensor(down_rows, down_rows, gates[:, 2 * f + 1, :],
                                            ALU.mult).then_inc(w_scaled, 1)
                    pool.wait_ge(w_scaled, pos + (base + 1))
                    split(w_raw[:, b, :], w_hi[:, b, :], w_lo[:, b, :], w_raw_in[b],
                          turn * 16 + 16 * (wused[b] + 1), w_high, pos + (base + 1), w_ready)
                walk(pool, f, tile)

            normalise_keys(NG - 1)
            outputs_low(NG - 1)
            pool.wait_ge(y_added, 4 * NG)
            ffn_weights(0)
            pool.wait_ge(gates1_ready, 2)
            pool.wait_ge(x_kept, 2)
            nc.gpsimd.tensor_tensor(x_b[:], x[:], lnwb[:, 1:2, :].to_broadcast([P, NT, D]),
                                    ALU.add).then_inc(x_shifted, 1)
            ffn_weights(1)

        @block.scalar
        def _(act):
            act.dma_start(x[:], x_d.rearrange("(t p) d -> p t d", p=P)).then_inc(x_loaded, 16)
            act.wait_ge(setup_loaded, 48)
            nc.scalar.activation(cth[:], ccol[:], ACT.Tanh, scale=0.5).then_inc(c_tanh, 1)
            nc.scalar.activation(ident[:], const[:, 0:P], ACT.Copy)
            nc.scalar.activation(ident_b[:], const[:, 0:P], ACT.Copy)
            nc.scalar.activation(mask_b[:], const[:, P:2 * P], ACT.Copy)
            nc.scalar.activation(before_b[:], const[:, 2 * P:3 * P], ACT.Copy)
            nc.scalar.activation(iota[:], const[:, 3 * P:], ACT.Copy).then_inc(consts_ready, 1)

            def modulate(n, layer, col):
                hT = hT_of[n]
                if n == 0:
                    act.wait_ge(mod_ready, 1)
                for hf in range(2):
                    for kc in range(KC):
                        b = 2 * hf + kc
                        act.wait_ge(ln_transposed, 4 * n + b + 1)
                        cols = hT[:, kc, hf * 512:hf * 512 + 512]
                        nc.scalar.activation(cols, ps[:, 4 + b, :], ACT.Identity,
                                             bias=modc[:, layer, col + kc:col + kc + 1],
                                             scale=opc[:, layer, col + 2 + kc:col + 3 + kc]
                                             ).then_inc(h_full, 1)
                        if n == 2:
                            continue
                        act.wait_ge(h_full, 4 * n + b + 1)
                        nc.scalar.activation(hT_hi[:, kc, hf * 512:hf * 512 + 512], cols,
                                             ACT.Copy).then_inc(h_hi, 1)

            act.wait_ge(wqkv_raw_in, 16)
            nc.scalar.activation(wqkv_hi[:], wqkv_raw[:], ACT.Copy).then_inc(wqkv_high, 1)
            modulate(0, 0, 0)

            with act.Fori(0, NG) as g:
                for t in range(NT):
                    act.wait_ge(kv_projected, g * NT + (t + 1))
                    nc.scalar.activation(sqk[:], ps[:, t % 4, 0:HD], ACT.Square,
                                         accum_out=rk_in[:, t:t + 1]).then_inc(key_sums, 1)
                    nc.scalar.activation(v_hi[:, t, :], ps[:, t % 4, HD:2 * HD], ACT.Copy).then_inc(v_split, 1)
                    act.wait_ge(key_sums, g * NT + (t + 1))

                def q_high(t):
                    act.wait_ge(q_transposed, g * NT + (t + 1))
                    nc.scalar.activation(qT_hi[:, :, t * P:(t + 1) * P],
                                         ps[:, 4 + t % 2, :].rearrange("p (h t) -> p h t", h=HPG),
                                         ACT.Copy, scale=qks[:, 0:1]).then_inc(qT_hi_done, 1)

                for t in range(NT):
                    act.wait_ge(projected, g * NT + (t + 1))
                    if t >= 1:
                        act.wait_ge(square_sums, g * NT + t)
                    nc.scalar.activation(sq[:], ps[:, t % 2, :], ACT.Square).then_inc(squares, 1)
                    if t >= 2:
                        act.wait_ge(q_transposed, g * NT + (t - 1))
                    nc.scalar.activation(q_f[:, t % 2, :], ps[:, t % 2, :], ACT.Copy).then_inc(q_copied, 1)
                    if t >= 1:
                        q_high(t - 1)
                    if t >= NT - 2:
                        b = t - (NT - 2)
                        act.wait_ge(k_transposed, g * 2 + (b + 1))
                        nc.scalar.activation(kT_hi[:, b * 512:(b + 1) * 512], ps[:, 2 + b, :], ACT.Copy,
                                             scale=qks[:, 1:2]).then_inc(kT_hi_done, 1)
                q_high(NT - 1)

                for n in range(STEPS + WOLAG - 3):
                    for what, place in BANK_AT.get(n, []):
                        if what[0] == "p":
                            _, q, u, j0, nb = what
                            m, c, h, qi = step_of(n - TLAG)
                            unit = unit_base(m) + u
                            act.wait_ge(p_transposed, g * TGS + (q + 1))
                            if unit >= NUNITS:
                                act.wait_ge(pv_done, g * 2 * HPG * NP + pieces_until_free(unit - NUNITS))
                            nc.scalar.activation(pT_hi[:, unit % NUNITS, 0:nb, qi * P:(qi + 1) * P],
                                                 ps[:, 4 + place % 2, 0:nb * P].rearrange("p (j t) -> p j t", j=nb),
                                                 ACT.Copy).then_inc(pT_hi_done, 1)
                        elif what[0] == "r":
                            m = what[1]
                            act.wait_ge(r_spread, g * 2 * HPG + (m + 1))
                            if m >= 2:
                                act.wait_ge(o_normed, g * 2 * HPG + (m - 1))
                            nc.scalar.activation(r_sb[:, m % 2, :], ps[:, 4 + place % 2, :],
                                                 ACT.Copy).then_inc(r_copied, 1)
                    m = head_at(n, OLAG)
                    if m is not None:
                        act.wait_ge(o_normed, g * 2 * HPG + (m + 1))
                        if m >= HPG:
                            act.wait_ge(wo_done, g * 4 + 2)
                        nc.scalar.activation(oT_hi[:, m % HPG, :], o_f[:], ACT.Copy).then_inc(oT_hi_done, 1)
                    if n < STEPS:
                        m, c, h, qi = step_of(n)
                        w = blocks(n) * P
                        pair = 2 * (n % 2)
                        act.wait_ge(bias_ready, g * STEPS + (n + 1))
                        if n >= 3:
                            act.wait_ge(p_transposed, g * TGS + TG_BEFORE[n - 2])
                        if c == 0:
                            src, dst = ps[:, pair, 0:w], prob[:, n % 3, 0:w]
                        else:
                            src = ps[:, pair:pair + 2, 0:w // 2]
                            dst = prob[:, n % 3, 0:w].rearrange("p (a w) -> p a w", a=2)
                        nc.scalar.activation(dst, src, ACT.Exp, bias=negb[:, n % 2:n % 2 + 1],
                                             scale=rqs[:, 4 * c + qi, h:h + 1],
                                             accum_out=rsum[:, m % 2, qi:qi + 1]).then_inc(exp_done, 1)

            def ffn(f):
                base, total = FF[f]["base"], FF[f]["total"]

                def high(pos, low, hf, back):
                    act.wait_ge(weighted, pos * 2 + (2 * (base - back) + hf + 1))
                    if 2 * (base + low - back) + hf - 1 > 0:
                        act.wait_ge(down_done, pos * 2 + (2 * (base - back) + hf - 1))
                    nc.scalar.activation(hid_hi[:, hf, :], fc[:, hf, :], ACT.Copy).then_inc(hid_hi_done, 1)

                def half_tanh(pos, low, hf):
                    act.wait_ge(up_done, pos * 2 + (2 * base + hf + 1))
                    if 2 * (base + low) + hf - 1 > 0:
                        act.wait_ge(silu_done, pos * 2 + (2 * base + hf - 1))
                    nc.scalar.activation(th[:, hf, :], ps[:, 4 + 2 * hf, :], ACT.Tanh,
                                         scale=0.5).then_inc(tanh_done, 1)

                half_tanh(0, 0, 0)
                half_tanh(0, 0, 1)
                act.wait_ge(banks_marked, 2 * f + 1)
                for b in (0, 3):
                    nc.scalar.activation(ps[:, b, :], x[:, 2 * b:2 * b + 2, :].rearrange("p r d -> p (r d)"),
                                         ACT.Copy).then_inc(x_in_sum, 1)
                high(0, 0, 0, 0)

                def tile(pos, turn, low):
                    for hf in range(2):
                        half_tanh(pos, low, hf)
                        if hf == 1:
                            high(pos, low, 0, 0)
                        elif low > 0:
                            high(pos, low, 1, 1)
                walk(act, f, tile, start=1)
                high(total - 1, total - 1, 1, 0)

            modulate(1, 0, 4)
            act.wait_ge(logits_done, 1)
            nc.scalar.activation(sig[:], ps[:, 0, :].rearrange("p (t e) -> p t e", t=NT), ACT.Exp,
                                 scale=-1.0).then_inc(logits_exp, 1)
            ffn(0)

            modulate(2, 1, 0)
            act.wait_ge(ssm_loaded, 80)
            nc.scalar.activation(a_t[:], svec[:, 0:1], ACT.Exp).then_inc(a_step, 1)
            act.wait_ge(a_step, 1)
            nc.scalar.activation(a_disc[:], a_t[:], ACT.Exp, scale=-1.0).then_inc(a_step, 1)

            modulate(3, 1, 4)
            act.wait_ge(shifted, 1)
            nc.scalar.activation(key[:, :, 0:E1], sig[:, :, 0:E1], ACT.Exp).then_inc(logits_exp, 1)
            ffn(1)
            act.wait_ge(down_done, 2 * (FF[1]["base"] + IT1))
            act.wait_ge(x_out, 1)
            nc.scalar.activation(x[:, 4:8, :].rearrange("p (b r) d -> p b (r d)", b=2), ps[:, 2:4, :],
                                 ACT.Copy).then_inc(x_out, 1)

        @block.vector
        def _(dve):
            steps = [0]

            def link(ins):
                steps[0] += 1
                ins.then_inc(vec_step, 1)
                dve.wait_ge(vec_step, steps[0])

            def inverse_root(width, link_, first=0):
                s = slice(first, first + width)
                v, y, t = rs_in[:, s], rs_y[:, s], rs_t[:, s]
                link_(nc.vector.tensor_scalar(y.bitcast(I32), v.bitcast(I32), -0.5, RSQRT_SEED, ALU.mult, ALU.add))
                for _ in range(NEWTON):
                    link_(nc.vector.tensor_tensor(t, y, y, ALU.mult))
                    link_(nc.vector.scalar_tensor_tensor(t, t, -0.5, v, ALU.mult, ALU.mult))
                    link_(nc.vector.scalar_tensor_tensor(y, t, 1.5, y, ALU.add, ALU.mult))

            def idle_step():
                nc.vector.memset(idle[:], 0.0)

            def row_stats(src, tiles, link_, ready=lambda t: None, before=lambda: None):
                for t in tiles:
                    ready(t)
                    ins = nc.vector.bn_stats(stat[:, t, :], src(t))
                link_(ins)
                before()
                for t in tiles:
                    ins = nc.vector.bn_aggr(mv[:, t, :], stat[:, t, :])
                link_(ins)
                s = slice(tiles[0], tiles[-1] + 1)
                link_(nc.vector.tensor_scalar(rs_in[:, s], mv[:, s, 1], EPS_LN, None, ALU.add))
                inverse_root(len(tiles), link_, tiles[0])

            def normalise(src, dst, tiles):
                for t in tiles:
                    nc.vector.tensor_scalar(dst[:, t, :], src(t), mv[:, t, 0:1], rs_y[:, t:t + 1],
                                            ALU.subtract, ALU.mult).then_inc(ln_normed, 1)

            def signed_gates(rows, sign, size, layer):
                link(nc.vector.tensor_scalar(sign, rows, 0.0, 2.0, ALU.is_ge, ALU.mult))
                link(nc.vector.tensor_scalar(sign, sign, -1.0, None, ALU.add))
                link(nc.vector.scalar_tensor_tensor(size, rows, -1.0, rows, ALU.mult, ALU.max))
                link(nc.vector.scalar_tensor_tensor(gates[:, 2 * layer:2 * layer + 2, :], size, 0.25, sign,
                                                    ALU.max, ALU.mult))

            def split_input(n):
                hT = hT_of[n]
                for hf in range(2):
                    for kc in range(KC):
                        dve.wait_ge(h_hi, 4 * min(n, 2) + 2 * hf + kc + 1)
                        s = slice(hf * 512, hf * 512 + 512)
                        nc.vector.tensor_tensor(hT_lo[:, kc, s], hT[:, kc, s], hT_hi[:, kc, s],
                                                ALU.subtract).then_inc(h_lo, 1)

            dve.wait_ge(setup_loaded, 48)
            nc.vector.memset(ones_b[:], 1.0)
            dve.wait_ge(c_tanh, 1)
            link(nc.vector.scalar_tensor_tensor(csil[:], cth[:], 1.0, ccol[:], ALU.add, ALU.mult))
            link(nc.vector.tensor_scalar(csil[:], csil[:], 0.5, None, ALU.mult))
            nc.vector.tensor_copy(csb[:], csil[:].unsqueeze(2).to_broadcast([P, 4, P])).then_inc(c_ready, 1)
            dve.wait_ge(x_loaded, 16)
            row_stats(lambda t: x[:, t, :], range(NT), link)
            normalise(lambda t: x[:, t, :], xn_of[0], range(NT))
            dve.wait_ge(mod_done, 1)
            nc.vector.tensor_copy(modc[:, 0, 0:4], ps[:, 0, 0:4])
            nc.vector.tensor_scalar(opc[:, 0, 0:4], ps[:, 0, 0:4], 1.0, None, ALU.add).then_inc(mod_ready, 1)
            split_input(0)
            dve.wait_ge(mod_done, 2)
            nc.vector.tensor_copy(modc[:, 0, 4:8], ps[:, 2, 0:4])
            nc.vector.tensor_scalar(opc[:, 0, 4:8], ps[:, 2, 0:4], 1.0, None, ALU.add)
            nc.vector.tensor_copy(grow[:], ps[:, 1, :].rearrange("p (r d) -> p r d", r=2)).then_inc(mod_copied, 1)
            dve.wait_ge(mod_copied, 1)
            signed_gates(grow[:], gsgn[:], gmag[:], 0)

            with dve.Fori(0, NG) as g:
                norm_steps = [0]

                def norm_link(ins):
                    norm_steps[0] += 1
                    ins.then_inc(qk_norm_step, 1)
                    dve.wait_ge(qk_norm_step, g * NORM_STEPS + norm_steps[0])

                for t in range(NT):
                    dve.wait_ge(v_split, g * NT + (t + 1))
                    nc.vector.tensor_copy(k_f[:, t, :], ps[:, t % 4, 0:HD]).then_inc(keys_copied, 1)
                    nc.vector.tensor_tensor(v_lo[:, t, :], ps[:, t % 4, HD:2 * HD], v_hi[:, t, :],
                                            ALU.subtract).then_inc(kv_copied, 1)
                dve.wait_ge(key_sums, g * NT + NT)
                norm_link(nc.vector.tensor_scalar(rs_in[:, 0:NT], rk_in[:], 1.0 / HD, EPS_Q, ALU.mult, ALU.add))
                inverse_root(NT, norm_link)

                def q_low(t):
                    dve.wait_ge(qT_hi_done, g * NT + (t + 1))
                    nc.vector.scalar_tensor_tensor(
                        qT_lo[:, :, t * P:(t + 1) * P], ps[:, 4 + t % 2, :].rearrange("p (h t) -> p h t", h=HPG),
                        qks[:, 0:1], qT_hi[:, :, t * P:(t + 1) * P], ALU.mult, ALU.subtract).then_inc(qT_lo_done, 1)

                for t in range(NT):
                    dve.wait_ge(squares, g * NT + (t + 1))
                    nc.vector.reduce_sum(rs_in[:, HPG * t:HPG * t + HPG], sq[:].rearrange("p (h d) -> p h d", d=HD),
                                         AX.X).then_inc(square_sums, 1)
                    if t >= 1:
                        q_low(t - 1)
                    if t >= NT - 2:
                        b = t - (NT - 2)
                        dve.wait_ge(kT_hi_done, g * 2 + (b + 1))
                        s = slice(b * 512, (b + 1) * 512)
                        nc.vector.scalar_tensor_tensor(kT_lo[:, s], ps[:, 2 + b, :], qks[:, 1:2], kT_hi[:, s],
                                                       ALU.mult, ALU.subtract).then_inc(kT_lo_done, 1)
                q_low(NT - 1)
                dve.wait_ge(square_sums, g * NT + NT)
                w = HPG * NT
                norm_link(nc.vector.tensor_scalar(rs_in[:, 0:w], rs_in[:, 0:w], 1.0 / HD, EPS_Q,
                                                  ALU.mult, ALU.add))
                inverse_root(w, norm_link)
                norm_link(nc.vector.tensor_scalar(rqs[:].rearrange("p t h -> p (t h)"), rs_y[:, 0:w], HD ** -0.5,
                                                  None, ALU.mult))
                for n in range(STEPS + WOLAG - 3):
                    if n == STEPS + 4:
                        dve.wait_ge(y_added, g * 4 + 2)
                        idle_step()
                        row_stats(lambda t: x[:, t, :], range(4), norm_link, before=idle_step)
                    if n < STEPS:
                        m, c, h, qi = step_of(n)
                        w = blocks(n) * P
                        pair = 2 * (n % 2)
                        i = n % 2
                        dve.wait_ge(scored, g * STEPS + (n + 1))
                        if c == 0:
                            nc.vector.reduce_max(mx[:, i:i + 1], ps[:, pair, 0:w], AX.X).then_inc(row_max, 1)
                        else:
                            nc.vector.reduce_max(mx[:, i:i + 1], ps[:, pair:pair + 2, 0:w // 2],
                                                 AX.XY).then_inc(row_max, 1)
                        dve.wait_ge(row_max, g * STEPS + (n + 1))
                        if n >= 2:
                            dve.wait_ge(exp_done, g * STEPS + (n - 1))
                        nc.vector.tensor_scalar(negb[:, i:i + 1], mx[:, i:i + 1], rqs[:, 4 * c + qi, h:h + 1], -1.0,
                                                ALU.mult, ALU.mult).then_inc(bias_ready, 1)
                    m = head_at(n, RLAG - 2)
                    if m is not None:
                        dve.wait_ge(exp_done, g * STEPS + (4 * m + 4))
                        if m >= 2:
                            dve.wait_ge(r_spread, g * 2 * HPG + (m - 1))
                        nc.vector.reciprocal(rinv[:, m % 2, :], rsum[:, m % 2, :]).then_inc(row_inv, 1)
                    m = head_at(n, OLAG)
                    if m is not None:
                        dve.wait_ge(pv_done, g * 2 * HPG * NP + NP * (m + 1))
                        dve.wait_ge(r_copied, g * 2 * HPG + (m + 1))
                        if m >= 1:
                            dve.wait_ge(oT_lo_done, g * 2 * HPG + m)
                        nc.vector.tensor_tensor(o_f[:], ps[:, 6 + m % 2, :], r_sb[:, m % 2, :],
                                                ALU.mult).then_inc(o_normed, 1)
                    for what, place in BANK_AT.get(n, []):
                        if what[0] == "p":
                            _, q, u, j0, nb = what
                            m, c, h, qi = step_of(n - TLAG)
                            unit = unit_base(m) + u
                            dve.wait_ge(pT_hi_done, g * TGS + (q + 1))
                            dst = (slice(None), unit % NUNITS, slice(0, nb), slice(qi * P, (qi + 1) * P))
                            nc.vector.tensor_tensor(pT_lo[dst],
                                                    ps[:, 4 + place % 2, 0:nb * P].rearrange("p (j t) -> p j t",
                                                                                             j=nb),
                                                    pT_hi[dst], ALU.subtract).then_inc(pT_lo_done, 1)
                        elif what[0] == "y":
                            y = what[1]
                            dve.wait_ge(wo_done, g * 4 + (y + 1))
                            nc.vector.tensor_tensor(ytmp[:, 2 * (y % 2):2 * (y % 2) + 2, :],
                                                    ps[:, 4 + place % 2, :].rearrange("p (r d) -> p r d", r=2),
                                                    gates[:, 0:1, :].to_broadcast([P, 2, D]),
                                                    ALU.mult).then_inc(y_scaled, 1)
                            dve.wait_ge(y_scaled, g * 4 + (y + 1))
                            nc.vector.tensor_tensor(x[:, 2 * y:2 * y + 2, :], x[:, 2 * y:2 * y + 2, :],
                                                    ytmp[:, 2 * (y % 2):2 * (y % 2) + 2, :],
                                                    ALU.add).then_inc(y_added, 1)
                dve.wait_ge(y_added, g * 4 + 4)
                assert norm_steps[0] == NORM_STEPS

            def pick(source, width, k):
                for t in range(NT):
                    ins = nc.vector.max(top[:, t, :], source[:, t, 0:width])
                link(ins)
                for t in range(NT):
                    ins = nc.vector.max_index(topi[:, t, :], top[:, t, :], source[:, t, 0:width])
                link(ins)
                link(nc.vector.tensor_copy(topf[:], topi[:]))
                place = iota[:, 0:width].unsqueeze(1).to_broadcast([P, NT, width])
                for i in range(k):
                    index = topf[:, :, i:i + 1].to_broadcast([P, NT, width])
                    got = sel if i == 0 else eq
                    link(nc.vector.tensor_tensor(got[:, :, 0:width], place, index, ALU.is_equal))
                    if i:
                        link(nc.vector.tensor_tensor(sel[:, :, 0:width], sel[:, :, 0:width], eq[:, :, 0:width],
                                                     ALU.add))

            def store_combine(f, width):
                dve.wait_ge(wc_transposed, f + 1)
                nc.vector.tensor_copy(wT[0:width, :], ps[0:width, 1:3, :].rearrange("p b t -> p (b t)")
                                      ).then_inc(wT_ready, 1)

            def ffn(f, width):
                base, total, cused = FF[f]["base"], FF[f]["total"], FF[f]["cused"]

                def low_half(pos, hf, back):
                    dve.wait_ge(hid_hi_done, pos * 2 + (2 * (base - back) + hf + 1))
                    nc.vector.tensor_tensor(hid_lo[:, hf, :], fc[:, hf, :], hid_hi[:, hf, :],
                                            ALU.subtract).then_inc(hid_lo_done, 1)

                def gate_half(pos, hf):
                    k1 = 2 * base + hf + 1
                    dve.wait_ge(tanh_done, pos * 2 + k1)
                    nc.vector.scalar_tensor_tensor(fa[:, hf, :], th[:, hf, :], 1.0, ps[:, 4 + 2 * hf, :],
                                                   ALU.add, ALU.mult).then_inc(silu_done, 1)
                    dve.wait_ge(silu_done, pos * 2 + k1)
                    nc.vector.tensor_tensor(fb[:, hf, :], fa[:, hf, :], ps[:, 5 + 2 * hf, :],
                                            ALU.mult).then_inc(gated, 1)

                def tile(pos, turn, low, gated_before=False):
                    buf = low % NB
                    for hf in range(2):
                        k1 = 2 * base + hf + 1
                        if not gated_before:
                            gate_half(pos, hf)
                        dve.wait_ge(gated, pos * 2 + k1)
                        if 2 * (base + low) + hf - 1 > 0:
                            dve.wait_ge(hid_lo_done, pos * 2 + (k1 - 2))
                        if f == 0 and isinstance(pos, int) and pos == 0:
                            nc.vector.tensor_scalar(fc[:, hf, :], fb[:, hf, :], 0.5, None,
                                                    ALU.mult).then_inc(weighted, 1)
                        else:
                            dve.wait_ge(wbc_in[buf], turn * 16 + 16 * (cused[buf] + 1))
                            nc.vector.tensor_tensor(fc[:, hf, :], fb[:, hf, :],
                                                    wbc[:, buf, hf * 512:hf * 512 + 512],
                                                    ALU.mult).then_inc(weighted, 1)
                        if hf == 1:
                            low_half(pos, 0, 0)
                        elif low > 0:
                            low_half(pos, 1, 1)

                gate_half(0, 0)
                store_combine(f, width)
                gate_half(0, 1)
                dve.wait_ge(banks_marked, 2 * f + 2)
                nc.vector.tensor_copy(ps[:, 1:3, :], x[:, 2:6, :].rearrange("p (b r) d -> p b (r d)", b=2)
                                      ).then_inc(x_in_sum, 1)
                tile(0, 0, 0, gated_before=True)
                walk(dve, f, tile, start=1)
                low_half(total - 1, 1, 0)

            dve.wait_ge(y_added, 4 * NG)
            normalise(lambda t: x[:, t, :], xn_of[1], range(4))
            row_stats(lambda t: x[:, t, :], range(4, NT), link)
            normalise(lambda t: x[:, t, :], xn_of[1], range(4, NT))
            split_input(1)
            dve.wait_ge(logits_exp, 1)
            link(nc.vector.tensor_copy(key[:], ps[:, 0, :].rearrange("p (t e) -> p t e", t=NT)))
            for t in range(NT):
                ins = nc.vector.max(top[:, t, :], key[:, t, :])
            link(ins)
            for t in range(NT):
                ins = nc.vector.max_index(topi[:, t, :], top[:, t, :], key[:, t, :])
            link(ins)
            last = top[:, :, TOPK0 - 1:TOPK0].to_broadcast([P, NT, E0])
            nc.vector.tensor_copy(topf[:], topi[:]).then_inc(vec_step, 1)
            steps[0] += 1
            nc.vector.tensor_tensor(eq[:], key[:], last, ALU.is_gt)
            nc.vector.tensor_tensor(wc[:], key[:], last, ALU.is_ge)
            dve.wait_ge(vec_step, steps[0])
            link(nc.vector.tensor_tensor(sel[:], iota[:].unsqueeze(1).to_broadcast([P, NT, E0]),
                                         topf[:, :, TOPK0 - 1:TOPK0].to_broadcast([P, NT, E0]), ALU.is_le))
            link(nc.vector.tensor_tensor(sel[:], sel[:], eq[:], ALU.max))
            nc.vector.tensor_tensor(sel_b[:], sel[:], wc[:], ALU.mult).then_inc(sel_ready, 1)
            dve.wait_ge(sel_ready, 1)
            link(nc.vector.tensor_scalar(sig[:], sig[:], 1.0, None, ALU.add))
            link(nc.vector.reciprocal(sig[:], sig[:]))
            link(nc.vector.tensor_tensor(ws[:], sel_b[:], sig[:], ALU.mult))
            link(nc.vector.reduce_sum(rsm[:, 0, :], ws[:], AX.X))
            link(nc.vector.reciprocal(rsm[:, 1, :], rsm[:, 0, :]))
            link(nc.vector.tensor_scalar(rsm[:, 2, :], rsm[:, 1, :], 0.5, None, ALU.mult))
            link(nc.vector.tensor_tensor(ws[:], ws[:], rsm[:, 2, :].unsqueeze(2).to_broadcast([P, NT, E0]),
                                         ALU.mult))
            dve.wait_ge(mod_done, 3)
            nc.vector.tensor_copy(modc[:, 1, :], ps[:, 1, 0:8])
            nc.vector.tensor_scalar(opc[:, 1, :], ps[:, 1, 0:8], 1.0, None, ALU.add)
            link(nc.vector.tensor_copy(key[:].rearrange("p t e -> p (t e)"), ps[:, 2, :]))
            dve.wait_ge(counted, 1)
            nc.vector.scalar_tensor_tensor(wc[:], ps[:, 3, :].rearrange("p (t e) -> p t e", t=NT), float(CAP),
                                           ws[:], ALU.is_lt, ALU.mult).then_inc(wc_ready, 1)
            ffn(0, E0)

            def gate_rows(t):
                return t[:].rearrange("p t e -> p (t e)").rearrange("p (r d) -> p r d", r=2)

            dve.wait_ge(ssm_loaded, 80)
            signed_gates(gate_rows(key), gate_rows(eq), gate_rows(ws), 1)
            nc.vector.tensor_scalar(opd[:], svec[:, 1:1 + KC], 1.0, None, ALU.add).then_inc(gates1_ready, 1)
            nc.vector.tensor_tensor(lnwb[:], lnwb[:], gates[:, 2:3, :].to_broadcast([P, 2, D]),
                                    ALU.mult).then_inc(gates1_ready, 1)
            sums = ps[:, 0:4, :].rearrange("p b (r d) -> p (b r) d", r=2)
            row_stats(lambda t: sums[:, t, :], range(NT), link,
                      lambda t: dve.wait_ge(down_done, 2 * FF[1]["base"] - 1 + t // 4))
            normalise(lambda t: sums[:, t, :], xn_of[2], range(NT))
            for hf in range(2):
                nc.vector.tensor_copy(x[:, 4 * hf:4 * hf + 4, :], sums[:, 4 * hf:4 * hf + 4, :]).then_inc(x_kept, 1)
            dve.wait_ge(gates1_ready, 2)
            dve.wait_ge(a_step, 2)
            for hf in range(2):
                dve.wait_ge(u_done, hf + 1)
                nc.vector.tensor_tensor_scan(hs[:, hf * 512:hf * 512 + 512], a_disc[:].to_broadcast([P, 512]),
                                             ps[:, hf, :], 0.0 if hf == 0 else hs[:, 511:512], ALU.mult,
                                             ALU.add).then_inc(scanned, 1)
                dve.wait_ge(scanned, hf + 1)
            for hf in range(2):
                for mc in range(KC):
                    b = 2 * hf + mc
                    dve.wait_ge(hc_done, b + 1)
                    s = slice(hf * 512, hf * 512 + 512)
                    nc.vector.scalar_tensor_tensor(zT[:, mc, s], hT_b[:, mc, s], opd[:, mc:mc + 1], ps[:, 4 + b, :],
                                                   ALU.mult, ALU.add).then_inc(z_ready, 1)
            row_stats(lambda t: sums[:, t, :], range(NT), link, lambda t: dve.wait_ge(z_transposed, 2 * (t // 2) + 2))
            for t in range(NT):
                ins = nc.vector.scalar_tensor_tensor(xn_b[:, t, :], sums[:, t, :], mv[:, t, 0:1], lnwb[:, 0, :],
                                                     ALU.subtract, ALU.mult)
            link(ins)
            dve.wait_ge(x_shifted, 1)
            for t in range(NT):
                ins = nc.vector.scalar_tensor_tensor(x[:, t, :], xn_b[:, t, :], rs_y[:, t:t + 1], x_b[:, t, :],
                                                     ALU.mult, ALU.add)
            link(ins)

            row_stats(lambda t: x[:, t, :], range(NT), link)
            normalise(lambda t: x[:, t, :], xn_of[3], range(NT))
            split_input(3)
            dve.wait_ge(logits_done, 2)
            lg = ps[:, 0, 0:NT * E1].rearrange("p (t e) -> p t e", t=NT)
            link(nc.vector.reduce_max(rsm[:, 0, :], lg, AX.X))
            nc.vector.tensor_tensor(sig[:, :, 0:E1], lg, rsm[:, 0, :].unsqueeze(2).to_broadcast([P, NT, E1]),
                                    ALU.subtract).then_inc(shifted, 1)
            dve.wait_ge(logits_exp, 2)
            link(nc.vector.reduce_sum(rsm[:, 1, :], key[:, :, 0:E1], AX.X))
            link(nc.vector.reciprocal(rsm[:, 1, :], rsm[:, 1, :]))
            link(nc.vector.tensor_tensor(key[:, :, 0:E1], key[:, :, 0:E1],
                                         rsm[:, 1, :].unsqueeze(2).to_broadcast([P, NT, E1]), ALU.mult))
            pick(key, E1, TOPK1)
            link(nc.vector.tensor_tensor(ws[:, :, 0:E1], sel[:, :, 0:E1], key[:, :, 0:E1], ALU.mult))
            link(nc.vector.reduce_sum(rsm[:, 2, :], ws[:, :, 0:E1], AX.X))
            link(nc.vector.reciprocal(rsm[:, 2, :], rsm[:, 2, :]))
            link(nc.vector.tensor_scalar(rsm[:, 3, :], rsm[:, 2, :], 0.5, None, ALU.mult))
            nc.vector.tensor_tensor(wc[:, :, 0:E1], ws[:, :, 0:E1],
                                    rsm[:, 3, :].unsqueeze(2).to_broadcast([P, NT, E1]),
                                    ALU.mult).then_inc(wc_ready, 1)
            ffn(1, E1)
            dve.wait_ge(down_done, 2 * (FF[1]["base"] + IT1) - 1)
            nc.vector.tensor_copy(x[:, 0:4, :].rearrange("p (b r) d -> p b (r d)", b=2),
                                  ps[:, 0:2, :]).then_inc(x_out, 1)

        @block.tensor
        def _(pe):
            def three(out, w_hi_, w_lo_, m_hi, m_lo, start, stop):
                nc.tensor.matmul(out, w_hi_, m_hi, start=start, stop=False, skip_group_check=True)
                nc.tensor.matmul(out, w_hi_, m_lo, start=False, stop=False, skip_group_check=True)
                return nc.tensor.matmul(out, w_lo_, m_hi, start=False, stop=stop, skip_group_check=True)

            def transpose_input(n):
                xn = xn_of[n]
                for hf in range(2):
                    pe.wait_ge(ln_normed, NT * n + 4 * hf + 4)
                    for kc in range(KC):
                        for t in range(4):
                            ins = nc.tensor.transpose(ps[:, 4 + 2 * hf + kc, t * P:(t + 1) * P],
                                                      xn[:, 4 * hf + t, kc * P:(kc + 1) * P], ident[:])
                        ins.then_inc(ln_transposed, 1)

            def mod_columns(w, layer, bank, col, kinds):
                for i, kind in enumerate(kinds):
                    for mc in range(KC):
                        j = col + KC * i + mc
                        for kc in range(KC):
                            ins = nc.tensor.matmul(ps[:, bank, j:j + 1],
                                                   w[kc][:, kind * D + mc * P:kind * D + (mc + 1) * P],
                                                   csil[:, 2 * layer + kc:2 * layer + kc + 1],
                                                   start=(kc == 0), stop=(kc == KC - 1), skip_group_check=True)
                return ins

            def gate_rows(w, layer, bank):
                for i, kind in enumerate((2, 5)):
                    for kc in range(KC):
                        ins = nc.tensor.matmul(ps[:, bank, i * D:(i + 1) * D], csb[:, 2 * layer + kc, :],
                                               w[kc][:, kind * D:(kind + 1) * D],
                                               start=(kc == 0), stop=(kc == KC - 1), skip_group_check=True)
                return ins

            wmod0 = [wmod[:, kc, :] for kc in range(KC)]
            pe.wait_ge(c_ready, 1)
            pe.wait_ge(first_mod_loaded, 16)
            mod_columns(wmod0, 0, 0, 0, (0, 1)).then_inc(mod_done, 1)
            pe.wait_ge(consts_ready, 1)
            transpose_input(0)
            pe.wait_ge(rest_mod_loaded, 16)
            mod_columns(wmod0, 0, 2, 0, (3, 4))
            gate_rows(wmod0, 0, 1).then_inc(mod_done, 1)
            pe.wait_ge(h_lo, 4)
            pe.wait_ge(mod_copied, 1)

            with pe.Fori(0, NG) as g:
                def transpose_q(t):
                    pe.wait_ge(q_copied, g * NT + (t + 1))
                    if t >= 2:
                        pe.wait_ge(qT_lo_done, g * NT + (t - 1))
                    for h in range(HPG):
                        ins = nc.tensor.transpose(ps[:, 4 + t % 2, h * P:(h + 1) * P],
                                                  q_f[:, t % 2, h * HD:(h + 1) * HD], ident[:])
                    ins.then_inc(q_transposed, 1)

                def project(out, t, cols):
                    tok = slice(t * P, (t + 1) * P)
                    for kc in range(KC):
                        ins = three(out, hT_hi[:, kc, tok], hT_lo[:, kc, tok], wqkv_hi[:, kc, cols],
                                    wqkv_lo[:, kc, cols], kc == 0, kc == KC - 1)
                    return ins

                pe.wait_ge(wqkv_ready, g + 1)
                for t in range(NT):
                    if t >= 4:
                        pe.wait_ge(kv_copied, g * NT + (t - 3))
                    project(ps[:, t % 4, 0:2 * HD], t, slice(HPG * HD, QKV)).then_inc(kv_projected, 1)
                for t in range(NT):
                    if t < 2:
                        pe.wait_ge(kv_copied, g * NT + (t + 5))
                    else:
                        pe.wait_ge(q_copied, g * NT + (t - 1))
                    project(ps[:, t % 2, :], t, slice(0, HPG * HD)).then_inc(projected, 1)
                    if t >= 1:
                        transpose_q(t - 1)
                    if t >= NT - 2:
                        b = t - (NT - 2)
                        pe.wait_ge(kv_copied, g * NT + NT)
                        pe.wait_ge(k_normed, g * 2 + (b + 1))
                        for i in range(4):
                            ins = nc.tensor.transpose(ps[:, 2 + b, i * P:(i + 1) * P], k_f[:, 4 * b + i, :],
                                                      ident[:])
                        ins.then_inc(k_transposed, 1)
                transpose_q(NT - 1)
                pe.wait_ge(q_copied, g * NT + NT)
                pe.wait_ge(qT_lo_done, g * NT + NT)
                pe.wait_ge(kT_lo_done, g * 2 + 2)

                for n in range(STEPS + WOLAG - 3):
                    if n < STEPS:
                        m, c, h, qi = step_of(n)
                        w = blocks(n) * P
                        pair = 2 * (n % 2)
                        pieces = [(pair, 0, w)] if c == 0 else [(pair, 0, w // 2), (pair + 1, w // 2, w // 2)]
                        q = slice((4 * c + qi) * P, (4 * c + qi + 1) * P)
                        if n >= 2:
                            pe.wait_ge(exp_done, g * STEPS + (n - 1))
                        for bank, k0, kw in pieces:
                            three(ps[:, bank, 0:kw], qT_hi[:, h, q], qT_lo[:, h, q], kT_hi[:, k0:k0 + kw],
                                  kT_lo[:, k0:k0 + kw], True, False)
                        bank, k0, kw = pieces[-1]
                        nc.tensor.matmul(ps[:, bank, kw - P:kw], ident_b[:], mask_b[:], start=False, stop=True,
                                         skip_group_check=True).then_inc(scored, 1)
                    def bank_free(place):
                        if place >= 2:
                            kind, index = BANK_ORDER[place - 2][:2]
                            if kind == "p":
                                pe.wait_ge(pT_lo_done, g * TGS + (index + 1))
                            elif kind == "r":
                                pe.wait_ge(r_copied, g * 2 * HPG + (index + 1))
                            else:
                                pe.wait_ge(y_scaled, g * 4 + (index + 1))

                    for what, place in BANK_AT.get(n, []):
                        if what[0] == "p":
                            _, q, u, j0, nb = what
                            k = n - TLAG
                            bank_free(place)
                            pe.wait_ge(exp_done, g * STEPS + (k + 1))
                            for j in range(nb):
                                ins = nc.tensor.transpose(ps[:, 4 + place % 2, j * P:(j + 1) * P],
                                                          prob[:, k % 3, (j0 + j) * P:(j0 + j + 1) * P], ident[:])
                            ins.then_inc(p_transposed, 1)
                    for r in range(NP):
                        m = head_at(n, PVLAG + r)
                        if m is None:
                            continue
                        c = m // HPG
                        if r == 0:
                            pe.wait_ge(pT_lo_done, g * TGS + TG_BEFORE[4 * m + 4])
                            if m >= 2:
                                pe.wait_ge(o_normed, g * 2 * HPG + (m - 1))
                        for j in PIECES[c][r]:
                            q0 = max(0, j - 4 * c) * P
                            u = (unit_base(m) + j // 4) % NUNITS
                            ins = three(ps[:, 6 + m % 2, q0:512], v_hi[:, j, :], v_lo[:, j, :],
                                        pT_hi[:, u, j % 4, q0:512], pT_lo[:, u, j % 4, q0:512], j == 0,
                                        j == 4 * c + 3)
                        ins.then_inc(pv_done, 1)
                    for what, place in BANK_AT.get(n, []):
                        if what[0] == "r":
                            m = what[1]
                            bank_free(place)
                            pe.wait_ge(row_inv, g * 2 * HPG + (m + 1))
                            for qi in range(4):
                                ins = nc.tensor.transpose(ps[:, 4 + place % 2, qi * P:(qi + 1) * P],
                                                          rinv[:, m % 2, qi:qi + 1].to_broadcast([P, P]), ident[:])
                            ins.then_inc(r_spread, 1)
                    quarters = [(what[1], place) for what, place in BANK_AT.get(n, []) if what[0] == "y"]
                    for h in range(HPG):
                        for y, place in quarters:
                            if h == 0:
                                bank_free(place)
                                pe.wait_ge(wo_ready, g + 1)
                            pe.wait_ge(oT_lo_done, g * 2 * HPG + (HPG * (y // 2) + h + 1))
                            for t in range(2):
                                tok = slice((2 * (y % 2) + t) * P, (2 * (y % 2) + t + 1) * P)
                                ins = three(ps[:, 4 + place % 2, t * D:(t + 1) * D], oT_hi[:, h, tok],
                                            oT_lo[:, h, tok], wo_hi[:, h, :], wo_lo[:, h, :],
                                            h == 0 and t == 0, h == HPG - 1)
                            if h == HPG - 1:
                                ins.then_inc(wo_done, 1)

            def router(gate, width, h_before):
                for t in range(NT):
                    if t % 4 == 0:
                        pe.wait_ge(h_full, h_before + t // 2 + 2)
                    for kc in range(KC):
                        ins = nc.tensor.matmul(ps[:, 0, t * width:(t + 1) * width], hT_b[:, kc, t * P:(t + 1) * P],
                                               gate[:, kc, :], start=(kc == 0), stop=(kc == KC - 1),
                                               skip_group_check=True)
                ins.then_inc(logits_done, 1)

            def mark_banks(banks):
                for b in banks:
                    ins = nc.tensor.matmul(ps[:, b, :], ident_b[:], sel_b[:].rearrange("p t e -> p (t e)"),
                                           start=True, stop=True, skip_group_check=True)
                ins.then_inc(banks_marked, 1)

            def transpose_combine(f, width):
                pe.wait_ge(wc_ready, f + 1)
                mark_banks((0, 3))
                for t in range(NT):
                    ins = nc.tensor.transpose(ps[0:width, 1 + t // 4, (t % 4) * P:(t % 4 + 1) * P],
                                              wc[:, t, 0:width], ident[:])
                ins.then_inc(wc_transposed, 1)
                pe.wait_ge(wT_ready, f + 1)
                mark_banks((1, 2))

            def ffn(f, combine):
                base, total = FF[f]["base"], FF[f]["total"]

                def up(pos, low, hf):
                    buf = low % NB
                    if 2 * (base + low) + hf - 1 > 0:
                        pe.wait_ge(gated, pos * 2 + (2 * base + hf - 1))
                    tok = slice(hf * 512, hf * 512 + 512)
                    for v in range(2):
                        for kc in range(KC):
                            s = slice((2 * kc + v) * P, (2 * kc + v + 1) * P)
                            ins = three(ps[:, 4 + 2 * hf + v, :], w_hi[:, buf, s], w_lo[:, buf, s],
                                        hT_hi[:, kc, tok], hT_lo[:, kc, tok], kc == 0, kc == KC - 1)
                    ins.then_inc(up_done, 1)

                def down(pos, buf, hf, back):
                    pe.wait_ge(hid_lo_done, pos * 2 + (2 * (base - back) + hf + 1))
                    for t in range(4):
                        tile = 4 * hf + t
                        tok = slice(t * P, (t + 1) * P)
                        ins = three(ps[:, tile // 2, (tile % 2) * D:(tile % 2 + 1) * D], hid_hi[:, hf, tok],
                                    hid_lo[:, hf, tok], w_hi[:, buf, 4 * P:], w_lo[:, buf, 4 * P:], False, False)
                    ins.then_inc(down_done, 1)

                def tile(pos, turn, low):
                    pe.wait_ge(w_ready, pos + (base + 1))
                    for hf in range(2):
                        if low > 1:
                            up(pos, low, hf)
                        down(pos, (low - 1) % NB, hf, 1)

                pe.wait_ge(h_lo, 4 * f + 8)
                pe.wait_ge(w_ready, base + 1)
                up(0, 0, 0)
                up(0, 0, 1)
                combine()
                pe.wait_ge(w_ready, base + 2)
                up(1, 1, 0)
                up(1, 1, 1)
                pe.wait_ge(x_in_sum, 3 * (f + 1))
                walk(pe, f, tile, start=1)
                for hf in range(2):
                    down(total - 1, (total - 1) % NB, hf, 0)

            transpose_input(1)
            pe.wait_ge(gate_loaded, 16)
            router(wgate, E0, 4)

            def combine0():
                pe.wait_ge(sel_ready, 1)
                for t in range(NT):
                    for s in range(t + 1):
                        ins = nc.tensor.matmul(ps[:, 3, t * E0:(t + 1) * E0], (before_b if s == t else ones_b)[:],
                                               sel_b[:, s, :], start=(s == 0), stop=(s == t),
                                               skip_group_check=True)
                ins.then_inc(counted, 1)
                pe.wait_ge(mod1_loaded, 32)
                mod_columns(wmod1, 1, 1, 0, (0, 1))
                mod_columns(wmod1, 1, 1, 4, (3, 4))
                gate_rows(wmod1, 1, 2).then_inc(mod_done, 1)
                transpose_combine(0, E0)

            ffn(0, combine0)

            transpose_input(2)
            pe.wait_ge(ssm_loaded, 80)
            pe.wait_ge(x_kept, 1)
            for hf in range(2):
                pe.wait_ge(h_full, 10 + 2 * hf)
                for kc in range(KC):
                    ins = nc.tensor.matmul(ps[:, hf, :], bT[:, kc, :], hT_b[:, kc, hf * 512:hf * 512 + 512],
                                           start=(kc == 0), stop=(kc == KC - 1))
                ins.then_inc(u_done, 1)
            for hf in range(2):
                pe.wait_ge(scanned, hf + 1)
                for mc in range(KC):
                    nc.tensor.matmul(ps[:, 4 + 2 * hf + mc, :], cT[:, mc * P:(mc + 1) * P],
                                     hs[:, hf * 512:hf * 512 + 512], start=True, stop=True).then_inc(hc_done, 1)
            pe.wait_ge(x_kept, 2)
            for t in range(NT):
                if t % 4 == 0:
                    pe.wait_ge(z_ready, 2 * (t // 4) + 2)
                for mc in range(KC):
                    ins = nc.tensor.transpose(ps[:, t // 2, (t % 2) * D + mc * P:(t % 2) * D + (mc + 1) * P],
                                              zT[:, mc, t * P:(t + 1) * P], ident[:])
                ins.then_inc(z_transposed, 1)

            transpose_input(3)
            pe.wait_ge(ssm_loaded, 80)
            router(wgate1, E1, 12)
            ffn(1, lambda: transpose_combine(1, E1))


def kernel(L0_attn_x, L0_attn_Wq, L0_attn_Wk, L0_attn_Wv, L0_attn_Wo, L0_attn_q_scale, L0_attn_k_scale,
           L0_ffn_w_gate, L0_ffn_w_shared_up, L0_ffn_w_shared_down, L0_ffn_w_up, L0_ffn_w_down, L0_c, L0_wmod,
           L1_attn_log_A_diag, L1_attn_B_mat, L1_attn_C_mat, L1_attn_D_vec, L1_attn_ln_w, L1_attn_ln_b,
           L1_ffn_gate_weight, L1_ffn_gate_up_proj, L1_ffn_down_proj, L1_c, L1_wmod):
    import numpy as np
    import concourse.bacc as bacc
    from concourse.bass_utils import run_bass_kernel_spmd

    def a(v):
        return np.asarray(v)

    def k_on_partitions(w):
        return np.ascontiguousarray(w.reshape(KC, P, -1).transpose(1, 0, 2))

    w_attn, w_out = [], []
    for g in range(NG):
        rows = slice(g * HPG * HD, (g + 1) * HPG * HD)
        kv = slice(g * HD, (g + 1) * HD)
        cols = np.concatenate([a(L0_attn_Wq)[rows].T, a(L0_attn_Wk)[kv].T, a(L0_attn_Wv)[kv].T], axis=1)
        w_attn.append(k_on_partitions(cols))
        w_out.append(a(L0_attn_Wo)[:, rows].T.reshape(HPG, HD, D).transpose(1, 0, 2))

    def hidden_tile(gate, value, down):
        gv = np.stack([gate.reshape(KC, P, P), value.reshape(KC, P, P)], axis=1)
        return np.concatenate([gv.transpose(2, 0, 1, 3).reshape(P, 4 * P), down], axis=1)

    up = a(L0_ffn_w_shared_up)
    pad = np.zeros((D, P - HS), up.dtype)
    ffn0 = [hidden_tile(np.concatenate([up[:, HS:], pad], axis=1), np.concatenate([up[:, :HS], pad], axis=1),
                        np.concatenate([a(L0_ffn_w_shared_down), np.zeros((P - HS, D), up.dtype)], axis=0))]
    for i in range(IT0):
        e = a(L0_ffn_w_up)[EPT0 * i:EPT0 * (i + 1)].transpose(1, 0, 2)
        ffn0.append(hidden_tile(e[:, :, :H0].reshape(D, P), e[:, :, H0:].reshape(D, P),
                                a(L0_ffn_w_down)[EPT0 * i:EPT0 * (i + 1)].reshape(P, D)))
    ffn1 = []
    for e in range(E1):
        for q in range(H1 // P):
            rows = slice(q * P, (q + 1) * P)
            gate_up = a(L1_ffn_gate_up_proj)[e]
            ffn1.append(hidden_tile(gate_up[:H1][rows].T, gate_up[H1:][rows].T, a(L1_ffn_down_proj)[e][:, rows].T))

    n = np.arange(P)
    const = np.concatenate([np.eye(P), np.where(n[None, :] > n[:, None], MASKED, 0.0), n[:, None] < n[None, :],
                            np.broadcast_to(np.arange(E0), (P, E0))], axis=1).astype(np.float32)
    ins = {
        "x": a(L0_attn_x).reshape(T, D),
        "w_attn": np.stack(w_attn), "w_out": np.stack(w_out),
        "qk_scale": np.stack([a(L0_attn_q_scale), a(L0_attn_k_scale)], axis=1),
        "gate0": k_on_partitions(a(L0_ffn_w_gate)), "ffn0": np.stack(ffn0),
        "c": np.concatenate([a(L0_c).reshape(KC, P).T, a(L1_c).reshape(KC, P).T], axis=1),
        "wmod": np.stack([k_on_partitions(a(L0_wmod)), k_on_partitions(a(L1_wmod))], axis=1),
        "const": const,
        "ssm_vec": np.concatenate([a(L1_attn_log_A_diag)[:, None], a(L1_attn_D_vec).reshape(KC, P).T], axis=1),
        "bmat": k_on_partitions(a(L1_attn_B_mat).T), "cmat": a(L1_attn_C_mat).T,
        "lnwb": np.stack([a(L1_attn_ln_w), a(L1_attn_ln_b)]),
        "gate1": k_on_partitions(a(L1_ffn_gate_weight).T), "ffn1": np.stack(ffn1),
    }
    ins = {k: np.ascontiguousarray(v) for k, v in ins.items()}
    nc = bacc.Bacc("TRN2", target_bir_lowering=False, num_devices=1)
    aps = [nc.dram_tensor("in_" + k, v.shape, F32, kind="ExternalInput").ap() for k, v in ins.items()]
    out = nc.dram_tensor("out", (T, D), F32, kind="ExternalOutput").ap()
    wt0 = nc.dram_tensor("combine0", (E0, T), F32, kind="Internal").ap()
    wt1 = nc.dram_tensor("combine1", (E1, 4, T), F32, kind="Internal").ap()
    program(nc, *aps, out, wt0, wt1)
    r = run_bass_kernel_spmd(nc, [{"in_" + k: v for k, v in ins.items()}], core_ids=[0])
    return r.results[0]["out"].reshape(1, T, D)
```
